# Optimizing a Trainium2 kernel written in Bass

```python
import numpy as np
import jax
import jax.numpy as jnp

def _softmax(x, axis=-1):
    return jax.nn.softmax(x, axis=axis)

def _gelu(x):
    return jax.nn.gelu(x, approximate=True)

def _silu(x):
    return jax.nn.silu(x)

def _sigmoid(x):
    return jax.nn.sigmoid(x)

def _layernorm(x, axis=-1, eps=1e-05):
    m = jnp.mean(x, axis=axis, keepdims=True)
    v = jnp.var(x, axis=axis, keepdims=True)
    return (x - m) / jnp.sqrt(v + eps)

def _scatter_add(tgt, idx, src, axis=0):
    return tgt.at[idx].add(src)

def _segment_sum(src, seg, n):
    return jax.ops.segment_sum(src, seg, n)
kernel_name = 'mk_prb_d1_jaxref_r4_7ad9c8'

def setup_inputs(seed: int=0):
    np.random.seed(seed)
    _w = jnp.asarray

    def _L0_attn_setup():
        import jax, jax.numpy as jnp
        import numpy as np
        D_MODEL = 256
        N_HEADS = 16
        HEAD_DIM = D_MODEL // N_HEADS
        WINDOW = 128
        LOCAL_BLOCK = 64
        LATENT_TOKENS = 64
        LATENT_D = 64
        LATENT_HEADS = 4
        LATENT_HD = LATENT_D // LATENT_HEADS
        NEG = -1000000000.0

        def _local_attention(q, k, v):
            B, H, S, hd = q.shape
            bs = min(S, max(WINDOW, LOCAL_BLOCK))
            nb = S // bs
            w = WINDOW
            L = bs + w - 1
            k_pad = jnp.pad(k, ((0, 0), (0, 0), (w - 1, 0), (0, 0)))
            v_pad = jnp.pad(v, ((0, 0), (0, 0), (w - 1, 0), (0, 0)))
            starts = jnp.arange(nb) * bs
            idx = starts[:, None] + jnp.arange(L)[None, :]
            kb = k_pad[:, :, idx]
            vb = v_pad[:, :, idx]
            qb = q.reshape(B, H, nb, bs, hd)
            q_pos = starts[:, None] + jnp.arange(bs)[None, :]
            k_gpos = starts[:, None] + jnp.arange(L)[None, :] - (w - 1)
            dist = q_pos[:, :, None] - k_gpos[:, None, :]
            allowed = (dist > 0) & (dist <= w) & (k_gpos[:, None, :] >= 0)
            scale = 1.0 / np.sqrt(hd)
            scores = jnp.einsum('bhnqd,bhnkd->bhnqk', qb, kb) * scale
            scores = jnp.where(allowed, scores, NEG)
            attn = jax.nn.softmax(scores, axis=-1)
            attn = jnp.where(allowed.any(-1)[None, None, :, :, None], attn, 0.0)
            out = jnp.einsum('bhnqk,bhnkd->bhnqd', attn, vb)
            return out.reshape(B, H, S, hd)
        key = jax.random.key(seed)
        ks = jax.random.split(key, 14)
        B, S = (2, 1024)
        s = 0.02
        f32 = jnp.float32
        return {'x': jax.random.normal(ks[0], (B, S, D_MODEL), f32), 'qkv_w': jax.random.normal(ks[1], (D_MODEL, 3 * D_MODEL), f32) * s, 'qkv_b': jnp.zeros((3 * D_MODEL,), f32), 'rq_w': jax.random.normal(ks[2], (D_MODEL, LATENT_D), f32) * s, 'rq_b': jnp.zeros((LATENT_D,), f32), 'rkv_w': jax.random.normal(ks[3], (D_MODEL, 2 * LATENT_D), f32) * s, 'rkv_b': jnp.zeros((2 * LATENT_D,), f32), 'rout_w': jax.random.normal(ks[4], (LATENT_D, D_MODEL), f32) * s, 'rout_b': jnp.zeros((D_MODEL,), f32), 'out_w': jax.random.normal(ks[5], (D_MODEL, D_MODEL), f32) * s, 'out_b': jnp.zeros((D_MODEL,), f32), 'gl_w': jax.random.normal(ks[6], (HEAD_DIM, 1), f32) * s, 'gr_w': jax.random.normal(ks[7], (HEAD_DIM, 1), f32) * s}
    _L0_attn_in = _L0_attn_setup()

    def _L0_ffn_setup():
        import jax, jax.numpy as jnp
        import numpy as np
        B, S, H = (2, 512, 256)
        E, F, K = (64, 128, 8)
        G, TG = (8, 4)
        SCALE = 2.5
        F_SH = 128

        def _gate(x, gate_w, gate_bias):
            scores = jax.nn.sigmoid(x @ gate_w.T)
            sc = scores + gate_bias[None, :]
            T = x.shape[0]
            group_scores = jax.lax.top_k(sc.reshape(T, G, E // G), 2)[0].sum(-1)
            _, gidx = jax.lax.top_k(group_scores, TG)
            gmask = jnp.zeros((T, G), sc.dtype).at[jnp.arange(T)[:, None], gidx].set(1.0)
            smask = jnp.repeat(gmask, E // G, axis=1)
            masked = jnp.where(smask > 0, sc, -jnp.inf)
            _, tidx = jax.lax.top_k(masked, K)
            tw = jnp.take_along_axis(scores, tidx, axis=1)
            tw = tw / (tw.sum(-1, keepdims=True) + 1e-20)
            return (tidx, tw * SCALE)
        key = jax.random.key(seed)
        ks = jax.random.split(key, 9)

        def w(k, shape, fan_in):
            return jax.random.normal(k, shape, jnp.float32) / np.float32(np.sqrt(fan_in))
        return {'hidden_states': jax.random.normal(ks[0], (B, S, H), jnp.float32), 'gate_w': w(ks[1], (E, H), H), 'gate_bias': jax.random.normal(ks[2], (E,), jnp.float32) * 0.01, 'We_gate': w(ks[3], (E, H, F), H), 'We_up': w(ks[4], (E, H, F), H), 'We_down': w(ks[5], (E, F, H), F), 'Ws_gate': w(ks[6], (H, F_SH), H), 'Ws_up': w(ks[7], (H, F_SH), H), 'Ws_down': w(ks[8], (F_SH, H), F_SH)}
    _L0_ffn_in = _L0_ffn_setup()
    _d = {'L0_attn_x': _L0_attn_in['x'], 'L0_attn_qkv_w': _L0_attn_in['qkv_w'], 'L0_attn_qkv_b': _L0_attn_in['qkv_b'], 'L0_attn_rq_w': _L0_attn_in['rq_w'], 'L0_attn_rq_b': _L0_attn_in['rq_b'], 'L0_attn_rkv_w': _L0_attn_in['rkv_w'], 'L0_attn_rkv_b': _L0_attn_in['rkv_b'], 'L0_attn_rout_w': _L0_attn_in['rout_w'], 'L0_attn_rout_b': _L0_attn_in['rout_b'], 'L0_attn_out_w': _L0_attn_in['out_w'], 'L0_attn_out_b': _L0_attn_in['out_b'], 'L0_attn_gl_w': _L0_attn_in['gl_w'], 'L0_attn_gr_w': _L0_attn_in['gr_w'], 'L0_ffn_gate_w': _L0_ffn_in['gate_w'], 'L0_ffn_gate_bias': _L0_ffn_in['gate_bias'], 'L0_ffn_We_gate': _L0_ffn_in['We_gate'], 'L0_ffn_We_up': _L0_ffn_in['We_up'], 'L0_ffn_We_down': _L0_ffn_in['We_down'], 'L0_ffn_Ws_gate': _L0_ffn_in['Ws_gate'], 'L0_ffn_Ws_up': _L0_ffn_in['Ws_up'], 'L0_ffn_Ws_down': _L0_ffn_in['Ws_down']}
    _x0 = _d['L0_attn_x']
    _d['L0_attn_x'] = jax.random.normal(jax.random.fold_in(jax.random.key(seed), 1), (4, 1024, 256), dtype=_x0.dtype)
    del _x0
    return _d

def reference(L0_attn_x, L0_attn_qkv_w, L0_attn_qkv_b, L0_attn_rq_w, L0_attn_rq_b, L0_attn_rkv_w, L0_attn_rkv_b, L0_attn_rout_w, L0_attn_rout_b, L0_attn_out_w, L0_attn_out_b, L0_attn_gl_w, L0_attn_gr_w, L0_ffn_gate_w, L0_ffn_gate_bias, L0_ffn_We_gate, L0_ffn_We_up, L0_ffn_We_down, L0_ffn_Ws_gate, L0_ffn_Ws_up, L0_ffn_Ws_down):

    def _L0_attn_ref(x, qkv_w, qkv_b, rq_w, rq_b, rkv_w, rkv_b, rout_w, rout_b, out_w, out_b, gl_w, gr_w):
        import jax, jax.numpy as jnp
        import numpy as np
        D_MODEL = 256
        N_HEADS = 16
        HEAD_DIM = D_MODEL // N_HEADS
        WINDOW = 128
        LOCAL_BLOCK = 64
        LATENT_TOKENS = 64
        LATENT_D = 64
        LATENT_HEADS = 4
        LATENT_HD = LATENT_D // LATENT_HEADS
        NEG = -1000000000.0

        def _local_attention(q, k, v):
            B, H, S, hd = q.shape
            bs = min(S, max(WINDOW, LOCAL_BLOCK))
            nb = S // bs
            w = WINDOW
            L = bs + w - 1
            k_pad = jnp.pad(k, ((0, 0), (0, 0), (w - 1, 0), (0, 0)))
            v_pad = jnp.pad(v, ((0, 0), (0, 0), (w - 1, 0), (0, 0)))
            starts = jnp.arange(nb) * bs
            idx = starts[:, None] + jnp.arange(L)[None, :]
            kb = k_pad[:, :, idx]
            vb = v_pad[:, :, idx]
            qb = q.reshape(B, H, nb, bs, hd)
            q_pos = starts[:, None] + jnp.arange(bs)[None, :]
            k_gpos = starts[:, None] + jnp.arange(L)[None, :] - (w - 1)
            dist = q_pos[:, :, None] - k_gpos[:, None, :]
            allowed = (dist > 0) & (dist <= w) & (k_gpos[:, None, :] >= 0)
            scale = 1.0 / np.sqrt(hd)
            scores = jnp.einsum('bhnqd,bhnkd->bhnqk', qb, kb) * scale
            scores = jnp.where(allowed, scores, NEG)
            attn = jax.nn.softmax(scores, axis=-1)
            attn = jnp.where(allowed.any(-1)[None, None, :, :, None], attn, 0.0)
            out = jnp.einsum('bhnqk,bhnkd->bhnqd', attn, vb)
            return out.reshape(B, H, S, hd)
        B, S, D = x.shape
        qkv = x @ qkv_w + qkv_b
        q, k, v = jnp.split(qkv, 3, axis=-1)

        def heads(t):
            return t.reshape(B, S, N_HEADS, HEAD_DIM).transpose(0, 2, 1, 3)
        local = _local_attention(heads(q), heads(k), heads(v))
        chunk = -(-S // min(LATENT_TOKENS, S))
        nlat = S // chunk
        pooled = x.reshape(B, nlat, chunk, D).mean(axis=2)
        chunk_ids = jnp.arange(S) // chunk
        rq = (x @ rq_w + rq_b).reshape(B, S, LATENT_HEADS, LATENT_HD).transpose(0, 2, 1, 3)
        rkv = pooled @ rkv_w + rkv_b
        rk, rv = jnp.split(rkv, 2, axis=-1)
        rk = rk.reshape(B, nlat, LATENT_HEADS, LATENT_HD).transpose(0, 2, 1, 3)
        rv = rv.reshape(B, nlat, LATENT_HEADS, LATENT_HD).transpose(0, 2, 1, 3)
        lscale = 1.0 / np.sqrt(LATENT_HD)
        lscores = jnp.einsum('bhsd,bhld->bhsl', rq, rk) * lscale
        lat_allowed = jnp.arange(nlat)[None, :] < chunk_ids[:, None]
        lscores = jnp.where(lat_allowed[None, None], lscores, NEG)
        lattn = jax.nn.softmax(lscores, axis=-1)
        lattn = jnp.where(lat_allowed.any(-1)[None, None, :, None], lattn, 0.0)
        lat_out = jnp.einsum('bhsl,bhld->bhsd', lattn, rv)
        lat_out = lat_out.transpose(0, 2, 1, 3).reshape(B, S, LATENT_D)
        remote = lat_out @ rout_w + rout_b
        remote_h = remote.reshape(B, S, N_HEADS, HEAD_DIM).transpose(0, 2, 1, 3)
        gate = jax.nn.sigmoid(local @ gl_w + remote_h @ gr_w)
        mixed = gate * local + (1.0 - gate) * remote_h
        mixed = mixed.transpose(0, 2, 1, 3).reshape(B, S, D)
        return mixed @ out_w + out_b

    def _L0_ffn_ref(hidden_states, gate_w, gate_bias, We_gate, We_up, We_down, Ws_gate, Ws_up, Ws_down):
        import jax, jax.numpy as jnp
        import numpy as np
        B, S, H = (2, 512, 256)
        E, F, K = (64, 128, 8)
        G, TG = (8, 4)
        SCALE = 2.5
        F_SH = 128

        def _gate(x, gate_w, gate_bias):
            scores = jax.nn.sigmoid(x @ gate_w.T)
            sc = scores + gate_bias[None, :]
            T = x.shape[0]
            group_scores = jax.lax.top_k(sc.reshape(T, G, E // G), 2)[0].sum(-1)
            _, gidx = jax.lax.top_k(group_scores, TG)
            gmask = jnp.zeros((T, G), sc.dtype).at[jnp.arange(T)[:, None], gidx].set(1.0)
            smask = jnp.repeat(gmask, E // G, axis=1)
            masked = jnp.where(smask > 0, sc, -jnp.inf)
            _, tidx = jax.lax.top_k(masked, K)
            tw = jnp.take_along_axis(scores, tidx, axis=1)
            tw = tw / (tw.sum(-1, keepdims=True) + 1e-20)
            return (tidx, tw * SCALE)
        b, s, h = hidden_states.shape
        x = hidden_states.reshape(-1, h).astype(jnp.float32)
        tidx, tw = _gate(x, gate_w, gate_bias)
        T = x.shape[0]
        w_dense = jnp.zeros((T, E), tw.dtype).at[jnp.arange(T)[:, None], tidx].add(tw)

        def body(acc, ws):
            wg, wu, wdn, cw = ws
            hmid = jax.nn.silu(x @ wg) * (x @ wu)
            return (acc + cw[:, None] * (hmid @ wdn), None)
        y, _ = jax.lax.scan(body, jnp.zeros_like(x), (We_gate, We_up, We_down, w_dense.T))
        y = y.reshape(b, s, h)
        shared = jax.nn.silu(hidden_states @ Ws_gate) * (hidden_states @ Ws_up) @ Ws_down
        return y + shared
    x = L0_attn_x
    xn = _layernorm(x, axis=-1)
    x = x + _L0_attn_ref(xn, L0_attn_qkv_w, L0_attn_qkv_b, L0_attn_rq_w, L0_attn_rq_b, L0_attn_rkv_w, L0_attn_rkv_b, L0_attn_rout_w, L0_attn_rout_b, L0_attn_out_w, L0_attn_out_b, L0_attn_gl_w, L0_attn_gr_w) + _L0_ffn_ref(xn, L0_ffn_gate_w, L0_ffn_gate_bias, L0_ffn_We_gate, L0_ffn_We_up, L0_ffn_We_down, L0_ffn_Ws_gate, L0_ffn_Ws_up, L0_ffn_Ws_down)
    return x

_drawn_inputs = setup_inputs


def setup_inputs(seed=0):
    import zlib

    import numpy as np

    out = dict(_drawn_inputs(seed))
    spreads = {'L0_attn_qkv_b': (0.0, 0.665),
     'L0_attn_rq_b': (0.0, 0.8),
     'L0_attn_rkv_b': (0.0, 0.8),
     'L0_attn_rout_b': (0.0, 0.679),
     'L0_attn_out_b': (0.0, 0.1)}
    factors = {'L0_attn_qkv_w': 8.0,
     'L0_attn_rq_w': 8.0,
     'L0_attn_rkv_w': 8.0,
     'L0_attn_rout_w': 8.0,
     'L0_attn_out_w': 2.966,
     'L0_attn_gl_w': 8.0,
     'L0_attn_gr_w': 8.0}
    for name, (base, spread) in spreads.items():
        noise = np.random.default_rng([zlib.crc32(name.encode()), seed]).standard_normal(out[name].shape)
        drawn = base * np.exp(spread * noise) if base else spread * noise
        out[name] = jnp.asarray(drawn.astype(out[name].dtype))
    for name, factor in factors.items():
        out[name] = (out[name] * factor).astype(out[name].dtype)
    return out
```

```python
from contextlib import ExitStack

import concourse.bass as bass
import concourse.mybir as mybir
from concourse.alu_op_type import AluOpType as ALU

ACT = mybir.ActivationFunctionType
AX_X = mybir.AxisListType.X
F32 = mybir.dt.float32
I32 = mybir.dt.int32
U32 = mybir.dt.uint32

P = 128
B, S, D = 4, 1024, 256
T = B * S
NB = T // P
BPS = S // P
DC = D // P
H, HD = 16, 16
HPC = P // HD
NPAIR = H // 2
LD, LH = 64, 4
LHD = LD // LH
NLAT = 64
CH = S // NLAT
LPB = P // CH
E, F, K = 64, 128, 8
G, TG = 8, 4
EPG = E // G
SCALE = 2.5
TILES = (T * K + E * (P - 1)) // P // 4 * 4 + 4
SLOTS = TILES * P
QT = -(-TILES // P)
RING = 14
WE = 3 * D
MANY = 9
ZROWS = 8
FILL = 3e38
EPS = 1e-5
NEG = -1e30
FLOOR = -1e20
TINY = 1e-30


def build(nc, A, out):
    with ExitStack() as ctx:
        def sb(name, shape, dt=F32):
            return ctx.enter_context(nc.sbuf_tensor(name, shape, dt))

        def ps(name, shape):
            return ctx.enter_context(nc.psum_tensor(name, shape, F32))

        def sem(name):
            return ctx.enter_context(nc.semaphore(name))

        x_all = sb("x_all", [P, NB, D])
        xT_all = sb("xT_all", [P, NB, DC, P])
        wqkv = sb("wqkv", [P, DC, 3 * D])
        wrq = sb("wrq", [P, DC, LD])
        wrkv = sb("wrkv", [P, DC, 2 * LD])
        wout = sb("wout", [P, DC, D])
        wrout = sb("wrout", [LD, D])
        wsg = sb("wsg", [P, DC, F])
        wsu = sb("wsu", [P, DC, F])
        wsd = sb("wsd", [F, D])
        gate_rows = sb("gate_rows", [E, D])
        gateT = sb("gateT", [P, DC, E])
        bqk = sb("bqk", [P, 2 * DC])
        bv = sb("bv", [P, D])
        brq = sb("brq", [LD, 1])
        brk = sb("brk", [LD, 1])
        brv = sb("brv", [P, LD])
        brout = sb("brout", [P, D])
        bout = sb("bout", [P, D])
        gl = sb("gl", [P, HD])
        gr = sb("gr", [P, HD])
        ident = sb("ident", [P, P])
        head_parity = sb("head_parity", [P, 2])
        rq_head = sb("rq_head", [LD, LH])
        mask_prev = sb("mask_prev", [P, BPS, P])
        mask = sb("mask", [P, 2, P])
        lat_wide = sb("lat_wide", [P, NLAT - LPB + NLAT])
        lat_mask = sb("lat_mask", [P, NLAT])
        eps = sb("eps", [P, 1])
        stats = sb("stats", [P, NB, 6])
        mean = sb("mean", [P, NB])
        mdif = sb("mdif", [P, NB])
        var = sb("var", [P, NB])
        std = sb("std", [P, NB])
        rstd = sb("rstd", [P, NB])
        xn_st = sb("xn_st", [P, 4, D])
        xTa = sb("xTa", [P, 2, DC, P])
        shared_mem = sb("shared_mem", [P, RING * WE])
        table = lambda n: shared_mem[:, n * NB * E:(n + 1) * NB * E].rearrange("p (t e) -> p t e", t=NB)
        scores_t, sc_t, ra_t, rb_t, sel_t = (table(n) for n in range(5))
        ring_gu = shared_mem[:, 0:RING * 2 * D].rearrange("p (r c n) -> p r c n", r=RING, c=DC)
        ring_d = shared_mem[:, RING * 2 * D:RING * WE].rearrange("p (r n) -> p r n", r=RING)
        rows_in = shared_mem[:, 0:2 * K * D].rearrange("p (j k d) -> p j k d", j=2, k=K)
        gbias = sb("gbias", [P, E])
        lower = sb("lower", [P, G, G])
        before = sb("before", [P, P])
        ones = sb("ones", [P, P])
        small = sb("small", [P, 4, NB * G])
        top8 = sb("top8", [P, NB, K])
        slot8 = sb("slot8", [P, NB, K])
        slot_idx = sb("slot_idx", [P, NB, K], U32)
        w8 = sb("w8", [P, NB, K])
        wsum = sb("wsum", [P, NB])
        wj = sb("wj", [P, 2, E])
        count_i = sb("count_i", [P, E], I32)
        per_e = sb("per_e", [P, 5, E])
        tile_no_i = sb("tile_no_i", [P, QT], I32)
        tile_no = sb("tile_no", [P, QT])
        tile_cmp = sb("tile_cmp", [P, QT, E])
        tile_e = sb("tile_e", [P, QT])
        tile_ei = sb("tile_ei", [P, QT], I32)
        expert_row = sb("expert_row", [1, QT * P], I32)
        ends_row = sb("ends_row", [1, E], I32)
        x_out_st = sb("x_out_st", [P, 2, D])
        idx_st = sb("idx_st", [P, 2, K], U32)
        ex = scores_t
        xTs = sb("xTs", [P, 2, DC, P])
        qz = sb("qz", [P, 2, DC, 2, P])
        kT = sb("kT", [P, 2, DC, P])
        vv = sb("vv", [P, 2, H, HD + 1])
        rqz = sb("rqz", [LD, LH, P])
        pooledT = sb("pooledT", [P, DC, 2, NLAT])
        rkT = sb("rkT", [LD, NLAT])
        rv = sb("rv", [P, LH, LHD + 1])
        sm = sb("sm", [P, 4, 2, 2 * P])
        nmax = sb("nmax", [P, 4, 2])
        pr = sb("pr", [P, 4, 2, 2 * P])
        prT = sb("prT", [P, 2, 2, 2, P])
        lsm = sb("lsm", [P, LH, NLAT])
        lmax = sb("lmax", [P, LH])
        lneg = sb("lneg", [P, LH, NLAT])
        lpr = sb("lpr", [P, LH, NLAT])
        lprT = sb("lprT", [P, 2, P])
        lden = sb("lden", [P, LH])
        lrec = sb("lrec", [P, LH])
        lat = sb("lat", [P, P])
        latT = sb("latT", [LD, P])
        remote = sb("remote", [P, H, HD])
        den = sb("den", [P, H])
        met = sb("met", [1, 4])
        rec = sb("rec", [P, H])
        local = sb("local", [P, H, HD])
        zl = sb("zl", [P, H, HD])
        zr = sb("zr", [P, H, HD])
        zs = sb("zs", [P, H, HD])
        z = sb("z", [P, H])
        ez = sb("ez", [P, H])
        ez1 = sb("ez1", [P, H])
        gate = sb("gate", [P, H])
        dif = sb("dif", [P, H, HD])
        gdif = sb("gdif", [P, H, HD])
        mixed = sb("mixed", [P, H, HD])
        zeros = pr[:].rearrange("p a b t -> p (a b t)")
        rc_t = sm[:].rearrange("p a b (t e) -> p (a b t) e", e=E)
        tiles_mem = pr[:].rearrange("p a b t -> p (a b t)")
        xs = tiles_mem[:, 0:4 * D].rearrange("p (j d) -> p j d", j=4)
        ys = tiles_mem[:, 4 * D:8 * D].rearrange("p (j d) -> p j d", j=4)
        tiles_mem = sm[:].rearrange("p a b t -> p (a b t)")
        xsT = tiles_mem[:, 0:2 * D].rearrange("p (j c t) -> p j c t", j=2, c=DC)
        sg, hh, hhT = (tiles_mem[:, (2 + n) * D:(3 + n) * D].rearrange("p (j f) -> p j f", j=2) for n in range(3))
        mixedT = sb("mixedT", [P, DC, P])
        eg = sb("eg", [F, P])
        eg1 = sb("eg1", [F, P])
        sig = sb("sig", [F, P])
        gs = sb("gs", [F, P])
        hsT = sb("hsT", [F, 2, P])

        psQ = ps("psQ", [P, 512])
        psV = ps("psV", [P, 512])
        psS = ps("psS", [P, 2, 512])
        psT = ps("psT", [P, 2, 512])
        psM = ps("psM", [P, 512])
        psO = ps("psO", [P, 512])

        NX = 4
        x_in = [sem(f"x_in{n}") for n in range(NX)]
        w_in = sem("w_in")
        consts = sem("consts")
        pool_order = sem("pool_order")
        gw_turned = sem("gw_turned")
        gw_ready = sem("gw_ready")
        stats_done = sem("stats_done")
        mv_done = sem("mv_done")
        std_done = sem("std_done")
        rstd_done = sem("rstd_done")
        xn_staged = sem("xn_staged")
        xn_turned = sem("xn_turned")
        xTa_ready = sem("xTa_ready")
        logits = sem("logits")
        ex_ready = sem("ex_ready")
        xT_kept = sem("xT_kept")
        xn_out = [sem(f"xn_out{j}") for j in range(4)]
        x_biased = sem("x_biased")
        xT_staged = sem("xT_staged")
        masks_staged = sem("masks_staged")
        pooled = sem("pooled")
        qk_ready = sem("qk_ready")
        v_ready = sem("v_ready")
        sh_ready = sem("sh_ready")
        q_kept = sem("q_kept")
        k_kept = sem("k_kept")
        v_kept = sem("v_kept")
        rq_kept = sem("rq_kept")
        eg_ready = sem("eg_ready")
        sh_steps = sem("sh_steps")
        hs_ready = sem("hs_ready")
        s_ready = sem("s_ready")
        masked = sem("masked")
        probs = sem("probs")
        probs_turned = sem("probs_turned")
        prT_ready = sem("prT_ready")
        pv_pair = sem("pv_pair")
        lat_kv = sem("lat_kv")
        rk_kept = sem("rk_kept")
        lat_s = sem("lat_s")
        lat_steps = sem("lat_steps")
        lat_neg = sem("lat_neg")
        lat_p = sem("lat_p")
        lat_turned = sem("lat_turned")
        lprT_ready = sem("lprT_ready")
        lat_o = sem("lat_o")
        lat_kept = sem("lat_kept")
        lat_oT = sem("lat_oT")
        latT_ready = sem("latT_ready")
        remote_ready = sem("remote_ready")
        remote_kept = sem("remote_kept")
        mix_steps = sem("mix_steps")
        z_ready = sem("z_ready")
        ez_ready = sem("ez_ready")
        local_kept = sem("local_kept")
        mixed_ready = sem("mixed_ready")
        mixed_turned = sem("mixed_turned")
        mixedT_ready = sem("mixedT_ready")
        out_ready = sem("out_ready")
        acc_done = sem("acc_done")
        stored = sem("stored")
        blocks_staged = sem("blocks_staged")
        cleared = sem("cleared")
        zeros_ready = sem("zeros_ready")
        route_steps = sem("route_steps")
        sel_ready = sem("sel_ready")
        ranks_ready = sem("ranks_ready")
        slots_ready = sem("slots_ready")
        tiles_ready = sem("tiles_ready")
        experts_known = sem("experts_known")
        routed = sem("routed")
        scatter_in = [sem(f"scatter_in{j}") for j in range(2)]
        scattered = [sem(f"scattered{j}") for j in range(2)]
        weights_in = [sem(f"weights_in{j}") for j in range(2)]
        experts_ready = sem("experts_ready")
        tiles_done = sem("tiles_done")
        xs_in = [sem(f"xs_in{j}") for j in range(4)]
        xs_turned = sem("xs_turned")
        xsT_ready = sem("xsT_ready")
        gu_ready = sem("gu_ready")
        silu_ready = sem("silu_ready")
        h_ready = sem("h_ready")
        h_turned = sem("h_turned")
        hT_ready = sem("hT_ready")
        y_ready = sem("y_ready")
        y_kept = sem("y_kept")
        y_out = [sem(f"y_out{j}") for j in range(4)]
        idx_in = [sem(f"idx_in{j}") for j in range(2)]
        rows_ready = [sem(f"rows_ready{j}") for j in range(2)]
        combine_steps = sem("combine_steps")
        combined = sem("combined")
        slot_rows = nc.dram_tensor("slot_rows", (SLOTS, D), F32, kind="Internal").ap()
        slot_outs = nc.dram_tensor("slot_outs", (SLOTS, D), F32, kind="Internal").ap()
        xn_tiles = nc.dram_tensor("xn_tiles", (NB, P, D), F32, kind="Internal").ap()
        slot_tiles = slot_rows.rearrange("(t p) d -> t p d", p=P)
        out_tiles = slot_outs.rearrange("(t p) d -> t p d", p=P)

        xt = A["L0_attn_x"].rearrange("b (t p) d -> p (b t) d", p=P)
        yt = out.rearrange("b (t p) d -> p (b t) d", p=P)
        rows = lambda w: w.rearrange("(c p) n -> p c n", p=P)
        col = lambda b, n: b.rearrange("(c p) -> p c", p=n)
        W_ALL = 16 * 19
        block = ctx.enter_context(nc.Block())

        @block.sync
        def _(sp):
            for n in range(NX):
                t = slice(n * NB // NX, (n + 1) * NB // NX)
                sp.dma_start(x_all[:, t, :], xt[:, t, :]).then_inc(x_in[n], 16)
            spread = lambda v: v.partition_broadcast(P)
            with nc.allow_non_contiguous_dma("biases, one value a partition"):
                for dst, src in (
                    (gate_rows[:], A["L0_ffn_gate_w"]),
                    (wqkv[:], rows(A["L0_attn_qkv_w"])),
                    (wrq[:], rows(A["L0_attn_rq_w"])),
                    (wrkv[:], rows(A["L0_attn_rkv_w"])),
                    (wout[:], rows(A["L0_attn_out_w"])),
                    (wrout[:], A["L0_attn_rout_w"]),
                    (wsg[:], rows(A["L0_ffn_Ws_gate"])),
                    (wsu[:], rows(A["L0_ffn_Ws_up"])),
                    (wsd[:], A["L0_ffn_Ws_down"]),
                    (bqk[:], col(A["L0_attn_qkv_b"][0:2 * D], P)),
                    (bv[:], spread(A["L0_attn_qkv_b"][2 * D:3 * D])),
                    (brq[:], col(A["L0_attn_rq_b"], LD)),
                    (brk[:], col(A["L0_attn_rkv_b"][0:LD], LD)),
                    (brv[:], spread(A["L0_attn_rkv_b"][LD:2 * LD])),
                    (brout[:], spread(A["L0_attn_rout_b"])),
                    (bout[:], spread(A["L0_attn_out_b"])),
                    (gl[:], spread(A["L0_attn_gl_w"].rearrange("d a -> (d a)"))),
                    (gr[:], spread(A["L0_attn_gr_w"].rearrange("d a -> (d a)"))),
                    (gbias[:], spread(A["L0_ffn_gate_bias"])),
                ):
                    sp.dma_start(dst, src).then_inc(w_in, 16)
            def store_xn(j, i):
                sp.wait_ge(xn_staged, i + 1)
                sp.dma_start(xn_tiles[i], xn_st[:, j, :]).then_inc(xn_out[j], 16)

            with sp.Fori(0, NB // 4) as g:
                for j in range(4):
                    store_xn(j, g * 4 + j)
            sp.wait_ge(zeros_ready, 1)
            clear = slot_rows.rearrange("(n p r) d -> n p (r d)", p=P, r=ZROWS)
            with sp.Fori(0, SLOTS // (P * ZROWS)) as n:
                sp.dma_start(clear[n], zeros).then_inc(cleared, 16)
            sp.wait_ge(tiles_ready, 1)
            with nc.allow_non_contiguous_dma("a column to a row"):
                for q in range(QT):
                    sp.dma_start(expert_row[0:1, q * P:(q + 1) * P], tile_ei[:, q:q + 1]).then_inc(experts_known, 16)

            def stage_scatter(j, i, first):
                if not first:
                    sp.wait_ge(scattered[j], 16 * K * i)
                sp.dma_start(x_out_st[:, j, :], xn_tiles[2 * i + j]).then_inc(scatter_in[j], 16)
                sp.dma_start(idx_st[:, j, :], slot_idx[:, 2 * i + j, :]).then_inc(scatter_in[j], 16)

            sp.wait_ge(slots_ready, 1)
            for j in range(4):
                sp.wait_ge(xn_out[j], 16 * (NB // 4))
            for j in range(2):
                stage_scatter(j, 0, True)
            with sp.Fori(1, NB // 2) as g:
                for j in range(2):
                    stage_scatter(j, g, False)
            for j in range(2):
                sp.wait_ge(scattered[j], 16 * K * NB // 2)

            sp.wait_ge(probs_turned, NB * NPAIR)
            sp.wait_ge(masked, 2 * NB * NPAIR)
            def load_tile(j, g, first):
                s = g * 4 + j
                if not first:
                    sp.wait_ge(xs_turned, s - 3)
                sp.dma_start(xs[:, j, :], slot_tiles[s]).then_inc(xs_in[j], 16)

            def store_tile(j, g):
                s = g * 4 + j
                sp.wait_ge(y_kept, s + 1)
                sp.dma_start(out_tiles[s], ys[:, j, :]).then_inc(y_out[j], 16)

            for j in range(4):
                load_tile(j, 0, True)
            with sp.Fori(1, TILES // 4) as g:
                for j in range(4):
                    load_tile(j, g, False)
                    store_tile(j, g - 1)
            for j in range(4):
                store_tile(j, TILES // 4 - 1)
            for j in range(4):
                sp.wait_ge(y_out[j], 16 * (TILES // 4))

            def stage_gather(j, i, first):
                if not first:
                    sp.wait_ge(rows_ready[j], 16 * K * i)
                sp.dma_start(idx_st[:, j, :], slot_idx[:, 2 * i + j, :]).then_inc(idx_in[j], 16)

            def store_block(i):
                sp.wait_ge(combined, i + 1)
                sp.dma_start(yt[:, i, :], x_all[:, i, :]).then_inc(stored, 16)

            for j in range(2):
                stage_gather(j, 0, True)
            with sp.Fori(1, NB // 2) as g:
                for j in range(2):
                    stage_gather(j, g, False)
                    store_block(2 * g + j - 2)
            for j in range(2):
                store_block(NB - 2 + j)
            sp.wait_ge(stored, 16 * NB)

        @block.gpsimd
        def _(pool):
            steps = 0

            def after(ins):
                nonlocal steps
                steps += 1
                ins.then_inc(pool_order, 1)
                pool.wait_ge(pool_order, steps)

            def fill(v, value, tests):
                for pattern, base, mult, op in tests:
                    after(nc.gpsimd.affine_select(out=v, in_=v, compare_op=op, fill=value, base=base,
                                                  pattern=pattern, channel_multiplier=mult))

            nc.gpsimd.memset(zeros, 0.0).then_inc(zeros_ready, 1)
            after(nc.gpsimd.memset(ident[:], 0.0))
            after(nc.gpsimd.memset(ones[:], 1.0))
            after(nc.gpsimd.memset(before[:], 1.0))
            fill(before[:], 0.0, [([[1, P]], -1, -1, ALU.is_ge)])
            after(nc.gpsimd.memset(lower[:], 1.0))
            fill(lower[:], 0.0, [([[1, G], [-1, G]], -1, 0, ALU.is_ge)])
            after(nc.gpsimd.iota(tile_no_i[:], pattern=[[P, QT]], base=0, channel_multiplier=1))
            after(nc.gpsimd.tensor_copy(tile_no[:], tile_no_i[:]))
            fill(ident[:], 1.0, [([[-1, P]], 0, 1, ALU.not_equal)])
            after(nc.gpsimd.memset(eps[:], EPS))
            after(nc.gpsimd.memset(head_parity[:], 0.0))
            for par in range(2):
                for n in range(HPC // 2):
                    lo = (2 * n + par) * HD
                    v = head_parity[:, par:par + 1]
                    t = gate[:, 0:1]
                    after(nc.gpsimd.memset(t, HD ** -0.5))
                    fill(t, 0.0, [([[0, 1]], -lo, 1, ALU.is_ge), ([[0, 1]], lo + HD - 1, -1, ALU.is_ge)])
                    after(nc.gpsimd.tensor_tensor(v, v, t, ALU.add))
            after(nc.gpsimd.memset(rq_head[:], LHD ** -0.5))
            fill(rq_head[:], 0.0, [([[-LHD, LH]], 0, 1, ALU.is_ge), ([[LHD, LH]], LHD - 1, -1, ALU.is_ge)])
            after(nc.gpsimd.memset(mask_prev[:], 0.0))
            fill(mask_prev[:], NEG, [([[0, BPS], [1, P]], 0, -1, ALU.is_ge), ([[0, BPS], [1, P]], -1, 0, ALU.is_ge),
                                      ([[1, BPS], [0, P]], -1, 0, ALU.is_ge)])
            after(nc.gpsimd.memset(mask[:], 0.0))
            fill(mask[:, 1, :], NEG, [([[-1, P]], -1, 1, ALU.is_ge)])
            after(nc.gpsimd.memset(lat_wide[:], 0.0))
            fill(lat_wide[:], NEG, [([[-CH, 2 * NLAT - LPB]], CH * (NLAT - LPB) - CH, 1, ALU.is_ge)])
            after(nc.gpsimd.memset(vv[:], 1.0))
            after(nc.gpsimd.memset(vv[:, 1, :, 0:HD], 0.0))
            after(nc.gpsimd.memset(kT[:, 1, :, :], 0.0))
            after(nc.gpsimd.memset(rv[:], 0.0))
            for par in range(2):
                after(nc.gpsimd.memset(rv[par * NLAT:(par + 1) * NLAT, par::2, LHD:LHD + 1], 1.0))
            after(nc.gpsimd.memset(lat[:], 0.0))
            nc.gpsimd.memset(pooledT[:], 0.0).then_inc(consts, 1)
            pool.wait_ge(w_in, W_ALL)
            with pool.Fori(0, NB // 2) as g:
                for j in range(2):
                    i = g * 2 + j
                    pool.wait_ge(xn_staged, i + 1)
                    pool.wait_ge(consts, 1)
                    nc.gpsimd.tensor_tensor(x_all[:, i, :], x_all[:, i, :], bout[:], ALU.add).then_inc(x_biased, 1)
                    pool.wait_ge(xTa_ready, i + 1)
                    pool.wait_ge(consts, 1)
                    nc.gpsimd.tensor_copy(xT_all[:, i, :, :], xTa[:, j, :, :]).then_inc(xT_kept, 1)

            def scatter(j, g):
                pool.wait_ge(scatter_in[j], 32 * (g + 1))
                pool.sem_inc(blocks_staged, 1)
                for k in range(K):
                    pool.indirect_dma_start(slot_rows, bass.IndirectOffsetOnAxis(ap=idx_st[:, j, k:k + 1], axis=0),
                                            x_out_st[:, j, :], None).then_inc(scattered[j], 16)

            pool.wait_ge(cleared, 16 * (SLOTS // (P * ZROWS)))
            with pool.Fori(0, NB // 2) as g:
                for j in range(2):
                    scatter(j, g)

            def load_expert(j, e, first):
                if not first:
                    end = pool.value_load(ends_row[0:1, bass.ds(e - RING, 1)], min_val=1, max_val=TILES + 1)
                    pool.wait_ge(tiles_done, end)
                r = e % RING
                pool.dma_start(ring_gu[:, r, :, 0:F], rows(A["L0_ffn_We_gate"][e])).then_inc(weights_in[j], 16)
                pool.dma_start(ring_gu[:, r, :, F:2 * F], rows(A["L0_ffn_We_up"][e])).then_inc(weights_in[j], 16)
                pool.dma_start(ring_d[:, r, :], A["L0_ffn_We_down"][e]).then_inc(weights_in[j], 16)

            def announce(j, g):
                pool.wait_ge(weights_in[j], 48 * (g + 1))
                pool.sem_inc(experts_ready, 1)

            pool.wait_ge(routed, 1)
            load_expert(0, 0, True)
            load_expert(1, 1, True)
            with pool.Fori(1, RING // 2) as g:
                for j in range(2):
                    announce(j, g - 1)
                    load_expert(j, 2 * g + j, True)
            with pool.Fori(RING // 2, E // 2) as g:
                for j in range(2):
                    announce(j, g - 1)
                    load_expert(j, 2 * g + j, False)
            for j in range(2):
                announce(j, E // 2 - 1)

            def gather(j, g, first):
                pool.wait_ge(idx_in[j], 16 * (g + 1))
                if not first:
                    pool.wait_ge(combined, 2 * g + j - 1)
                pool.sem_inc(blocks_staged, 1)
                for k in range(K):
                    pool.indirect_dma_start(rows_in[:, j, k, :], None, slot_outs,
                                            bass.IndirectOffsetOnAxis(ap=idx_st[:, j, k:k + 1], axis=0)
                                            ).then_inc(rows_ready[j], 16)

            for j in range(4):
                pool.wait_ge(y_out[j], 16 * (TILES // 4))
            for j in range(2):
                gather(j, 0, True)
            with pool.Fori(1, NB // 2) as g:
                for j in range(2):
                    gather(j, g, False)

        @block.tensor
        def _(pe):
            mm = nc.tensor.matmul

            pe.wait_ge(w_in, W_ALL)
            pe.wait_ge(consts, 1)
            for c in range(DC):
                last = nc.tensor.transpose(psM[:, c * E:(c + 1) * E], gate_rows[:, c * P:(c + 1) * P], ident[0:E, 0:E])
            last.then_inc(gw_turned, 1)

            def turn_x(j, i, first):
                pe.wait_ge(xn_staged, i + 1)
                if not first:
                    pe.wait_ge(xTa_ready, i - 1)
                for c in range(DC):
                    last = nc.tensor.transpose(psT[:, j % 2, c * P:(c + 1) * P], xn_st[:, j, c * P:(c + 1) * P], ident[:])
                last.then_inc(xn_turned, 1)

            def route(j, i, first):
                pe.wait_ge(xTa_ready, i + 1)
                if not first:
                    pe.wait_ge(ex_ready, i - 1)
                for c in range(DC):
                    last = mm(psS[:, j % 2, 0:E], xTa[:, j % 2, c, :], gateT[:, c, :], start=(c == 0), stop=(c == DC - 1))
                last.then_inc(logits, 1)

            pe.wait_ge(gw_ready, 1)
            for j in range(4):
                turn_x(j, j, j < 2)
                route(j, j, j < 2)
            with pe.Fori(1, NB // 4) as g:
                for j in range(4):
                    turn_x(j, g * 4 + j, False)
                    route(j, g * 4 + j, False)

            pe.wait_ge(sel_ready, 1)
            sel_flat = sel_t.rearrange("p t e -> p (t e)")
            for n in range(4):
                mm((psS[:, n, :] if n < 2 else psT[:, n - 2, :]), before[:], sel_flat[:, n * 512:(n + 1) * 512], start=True, stop=True)
            for n, bank in enumerate((psQ, psV, psM, psO)):
                last = mm(bank[:], ones[:], sel_flat[:, n * 512:(n + 1) * 512], start=True, stop=True)
            last.then_inc(ranks_ready, 1)
            pe.wait_ge(routed, 1)

            def project(j, i, first):
                pe.wait_ge(xT_staged, i + 1)
                if not first:
                    pe.wait_ge(hs_ready, i)
                for m in range(2 * DC):
                    for c in range(DC):
                        last = mm(psQ[:, m * P:(m + 1) * P], wqkv[:, c, m * P:(m + 1) * P], xTs[:, j, c, :],
                                  start=(c == 0), stop=(c == DC - 1))
                last.then_inc(qk_ready, 1)
                if not first:
                    pe.wait_ge(rq_kept, i)
                for c in range(DC):
                    mm(psV[:, 0:D], xTs[:, j, c, :], wqkv[:, c, 2 * D:3 * D], start=(c == 0), stop=(c == DC - 1))
                for c in range(DC):
                    last = mm(psV[0:LD, D:D + P], wrq[:, c, :], xTs[:, j, c, :], start=(c == 0), stop=(c == DC - 1))
                last.then_inc(v_ready, 1)

            def shared(j, i):
                pe.wait_ge(q_kept, i + 1)
                pe.wait_ge(k_kept, i + 1)
                for n, w in enumerate((wsg, wsu)):
                    for c in range(DC):
                        last = mm(psQ[:, n * P:(n + 1) * P], w[:, c, :], xTs[:, j, c, :], start=(c == 0), stop=(c == DC - 1))
                last.then_inc(sh_ready, 1)

            def turn_mixed(i):
                pe.wait_ge(mixed_ready, i + 1)
                for c in range(DC):
                    last = nc.tensor.transpose(psM[:, c * P:(c + 1) * P],
                                               mixed[:].rearrange("p h d -> p (h d)")[:, c * P:(c + 1) * P], ident[:])
                last.then_inc(mixed_turned, 1)

            def out_project(j, i):
                pe.wait_ge(mixedT_ready, i + 1)
                pe.wait_ge(hs_ready, i + 1)
                for c in range(DC):
                    mm(psM[:, D:2 * D], mixedT[:, c, :], wout[:, c, :], start=(c == 0), stop=False)
                mm(psM[:, D:2 * D], hsT[:, j, :], wsd[:], start=False, stop=True).then_inc(out_ready, 1)

            def scores(j, i, p, first):
                n = i * NPAIR + p
                if p == 0:
                    pe.wait_ge(q_kept, i + 1)
                    pe.wait_ge(k_kept, i + 1)
                if p >= 2 or not first:
                    pe.wait_ge(masked, 2 * (n - 1))
                c, r = p // (NPAIR // DC), (p % (NPAIR // DC)) * 2 * HD
                for par in range(2):
                    for half in range(2):
                        last = mm(psS[:, p % 2, (2 * par + half) * P:(2 * par + half + 1) * P],
                                  qz[r:r + 2 * HD, j, c, par, :], kT[r:r + 2 * HD, (j + 1 + half) % 2, c, :],
                                  start=True, stop=True)
                last.then_inc(s_ready, 1)

            def turn_probs(i, p, first):
                n = i * NPAIR + p
                pe.wait_ge(probs, 2 * n + 2)
                if p >= 2 or not first:
                    pe.wait_ge(prT_ready, n - 1)
                for par in range(2):
                    for half in range(2):
                        last = nc.tensor.transpose(psT[:, p % 2, (2 * par + half) * P:(2 * par + half + 1) * P],
                                                   pr[:, p % 4, par, half * P:(half + 1) * P], ident[:])
                last.then_inc(probs_turned, 1)

            def values(j, i, p, first):
                n = i * NPAIR + p
                pe.wait_ge(prT_ready, n + 1)
                if p == 0:
                    pe.wait_ge(v_kept, i + 1)
                    if not first:
                        pe.wait_ge(local_kept, i)
                for par in range(2):
                    h = 2 * p + par
                    for half in range(2):
                        last = mm(psO[:, h * (HD + 1):(h + 1) * (HD + 1)], prT[:, p % 2, par, half, :],
                                  vv[:, (j + 1 + half) % 2, h, :], start=(half == 0), stop=(half == 1))
                last.then_inc(pv_pair, 1)

            def latent_kv(i, first):
                pe.wait_ge(pooled, i + 1)
                if not first:
                    pe.wait_ge(acc_done, i)
                for c in range(DC):
                    mm(psM[0:LD, 0:NLAT], wrkv[:, c, 0:LD], pooledT[:, c, 0, :], start=(c == 0), stop=(c == DC - 1))
                for c in range(DC):
                    last = mm(psM[:, NLAT:NLAT + LD], pooledT[:, c, :, :].rearrange("p a n -> p (a n)"), wrkv[:, c, LD:2 * LD],
                              start=(c == 0), stop=(c == DC - 1))
                last.then_inc(lat_kv, 1)

            def latent_scores(i):
                pe.wait_ge(rk_kept, 3 * i + 3)
                pe.wait_ge(rq_kept, i + 1)
                for h in range(LH):
                    last = mm(psM[:, h * NLAT:(h + 1) * NLAT], rqz[:, h, :], rkT[:], start=True, stop=True)
                last.then_inc(lat_s, 1)

            def latent_turn(i):
                pe.wait_ge(lat_p, i + 1)
                flat = lpr[:].rearrange("p h n -> p (h n)")
                for n in range(2):
                    last = nc.tensor.transpose(psM[:, n * P:(n + 1) * P], flat[:, n * P:(n + 1) * P], ident[:])
                last.then_inc(lat_turned, 1)

            def latent_values(i):
                pe.wait_ge(lprT_ready, i + 1)
                for n in range(LH // 2):
                    last = mm(psM[:, 2 * n * (LHD + 1):2 * (n + 1) * (LHD + 1)], lprT[:, n, :],
                              rv[:, 2 * n:2 * n + 2, :].rearrange("p h d -> p (h d)"), start=True, stop=True)
                last.then_inc(lat_o, 1)

            def latent_out_turn(i):
                pe.wait_ge(lat_kept, i + 1)
                nc.tensor.transpose(psM[:, 0:P], lat[:], ident[:]).then_inc(lat_oT, 1)

            def latent_project(i):
                pe.wait_ge(latT_ready, i + 1)
                mm(psM[:, D:2 * D], latT[:], wrout[:], start=True, stop=True).then_inc(remote_ready, 1)

            def body(j, i, first, second):
                project(j, i, first)
                if not first:
                    turn_mixed(i - 1)
                shared(j, i)
                if not first:
                    out_project(1 - j, i - 1)
                for s in range(NPAIR + 3):
                    if s < NPAIR:
                        scores(j, i, s, first)
                    if 2 <= s < NPAIR + 2:
                        turn_probs(i, s - 2, first)
                    if 3 <= s:
                        values(j, i, s - 3, first)
                    if s == 0:
                        latent_kv(i, first)
                    if s == 2:
                        latent_scores(i)
                    if s == 5:
                        latent_turn(i)
                    if s == 7:
                        latent_values(i)
                    if s == 9:
                        latent_out_turn(i)
                    if s == 10:
                        latent_project(i)

            pe.wait_ge(xT_kept, NB)
            for j in range(2):
                body(j, j, j == 0, j == 1)
            with pe.Fori(1, NB // 2) as g:
                for j in range(2):
                    body(j, g * 2 + j, False, False)
            turn_mixed(NB - 1)
            out_project((NB - 1) % 2, NB - 1)

            def turn_tile(j, s, turn, first):
                pe.wait_ge(xs_in[j], 16 * (turn + 1))
                if not first:
                    pe.wait_ge(xsT_ready, s - 1)
                for c in range(DC):
                    last = nc.tensor.transpose(psT[:, j % 2, c * P:(c + 1) * P], xs[:, j, c * P:(c + 1) * P], ident[:])
                last.then_inc(xs_turned, 1)

            def expert_of(s):
                return pe.value_load(expert_row[0:1, bass.ds(s, 1)], min_val=0, max_val=E - 1)

            def gate_up(j, s, first):
                e = expert_of(s)
                pe.wait_ge(experts_ready, e + 1)
                pe.wait_ge(xsT_ready, s + 1)
                if not first:
                    pe.wait_ge(h_ready, s - 1)
                for c in range(DC):
                    last = mm(psS[:, j % 2, 0:2 * F], xsT[:, j % 2, c, :], ring_gu[:, e % RING, c, :], start=(c == 0), stop=(c == DC - 1))
                last.then_inc(gu_ready, 1)

            def turn_h(j, s, first):
                pe.wait_ge(h_ready, s + 1)
                if not first:
                    pe.wait_ge(hT_ready, s - 1)
                nc.tensor.transpose((psQ, psV)[j % 2][:, 0:P], hh[:, j % 2, :], ident[:]).then_inc(h_turned, 1)

            def down(j, s, first):
                e = expert_of(s)
                pe.wait_ge(hT_ready, s + 1)
                if not first:
                    pe.wait_ge(y_kept, s - 1)
                mm((psM, psO)[j % 2][:, 0:D], hhT[:, j % 2, :], ring_d[:, e % RING, :], start=True, stop=True).then_inc(tiles_done, 1)

            def step(j, g, nth, final):
                s = g * 4 + j
                if not final:
                    turn_tile((j + 1) % 4, s + 1, g + (j + 1) // 4, nth == 0)
                if nth > 0:
                    turn_h((j - 1) % 4, s - 1, nth <= 2)
                gate_up(j, s, nth < 2)
                if nth > 0:
                    down((j - 1) % 4, s - 1, nth <= 2)

            pe.wait_ge(experts_known, 16 * QT)
            pe.wait_ge(acc_done, NB)
            pe.sem_inc(tiles_done, 1)
            turn_tile(0, 0, 0, True)
            for j in range(4):
                step(j, 0, j, False)
            with pe.Fori(1, TILES // 4 - 1) as g:
                for j in range(4):
                    step(j, g, MANY, False)
            for j in range(4):
                step(j, TILES // 4 - 1, MANY, j == 3)
            turn_h(3, TILES - 1, False)
            down(3, TILES - 1, False)

        @block.scalar
        def _(act):
            act.wait_ge(gw_turned, 1)
            nc.scalar.copy(gateT[:].rearrange("p c e -> p (c e)"), psM[:, 0:DC * E]).then_inc(gw_ready, 1)
            act.wait_ge(mv_done, 7)
            nc.scalar.activation(std[:], var[:], ACT.Sqrt, bias=eps[:]).then_inc(std_done, 1)

            def keep_xT(j, i, first):
                act.wait_ge(xn_turned, i + 1)
                if not first:
                    act.wait_ge(xT_kept, i - 1)
                    act.wait_ge(logits, i - 1)
                nc.scalar.copy(xTa[:, j, :, :].rearrange("p c t -> p (c t)"), psT[:, j, 0:D]).then_inc(xTa_ready, 1)
                act.wait_ge(logits, i + 1)
                nc.scalar.activation(ex[:, i, :], psS[:, j, 0:E], ACT.Exp, scale=-1.0).then_inc(ex_ready, 1)

            for j in range(2):
                keep_xT(j, j, True)
            with act.Fori(1, NB // 2) as g:
                for j in range(2):
                    keep_xT(j, g * 2 + j, False)

            def keep_k(j, i, first):
                act.wait_ge(qk_ready, i + 1)
                if not first:
                    act.wait_ge(s_ready, NPAIR * i)
                act.wait_ge(consts, 1)
                for c in range(DC):
                    last = nc.scalar.activation(kT[:, j, c, :], psQ[:, (DC + c) * P:(DC + c + 1) * P], ACT.Identity,
                                                bias=bqk[:, DC + c:DC + c + 1])
                last.then_inc(k_kept, 1)

            def gate_exp(i):
                act.wait_ge(z_ready, i + 1)
                nc.scalar.activation(ez[:], z[:], ACT.Exp, scale=-1.0).then_inc(ez_ready, 1)

            def keep_mixedT(i, first):
                act.wait_ge(mixed_turned, i + 1)
                if not first:
                    act.wait_ge(out_ready, i)
                nc.scalar.copy(mixedT[:].rearrange("p c t -> p (c t)"), psM[:, 0:D]).then_inc(mixedT_ready, 1)

            def shared_exp(i, first):
                act.wait_ge(sh_ready, i + 1)
                if not first:
                    act.wait_ge(hs_ready, i)
                nc.scalar.activation(eg[:], psQ[:, 0:P], ACT.Exp, scale=-1.0).then_inc(eg_ready, 1)

            act.wait_ge(cleared, 16 * (SLOTS // (P * ZROWS)))
            act.wait_ge(routed, 1)

            def exps(i, p, first):
                n = i * NPAIR + p
                if p >= 4 or not first:
                    act.wait_ge(probs_turned, n - 3)
                for par in range(2):
                    act.wait_ge(masked, 2 * n + par + 1)
                    nc.scalar.activation(pr[:, p % 4, par, :], sm[:, p % 4, par, :], ACT.Exp,
                                         bias=nmax[:, p % 4, par:par + 1], scale=-1.0).then_inc(probs, 1)

            def keep_prT(i, p, first):
                n = i * NPAIR + p
                act.wait_ge(probs_turned, n + 1)
                if p >= 2 or not first:
                    act.wait_ge(pv_pair, n - 1)
                nc.scalar.copy(prT[:, p % 2].rearrange("p a b t -> p (a b t)"), psT[:, p % 2, :]).then_inc(prT_ready, 1)

            def body(j, i, first):
                keep_k(j, i, first)
                if not first:
                    gate_exp(i - 1)
                    keep_mixedT(i - 1, isinstance(i, int) and i == 1)
                shared_exp(i, first)
                for s in range(NPAIR + 2):
                    if s < NPAIR:
                        exps(i, s, first)
                    if 2 <= s:
                        keep_prT(i, s - 2, first)
                    if s == 4:
                        act.wait_ge(lat_neg, i + 1)
                        if not first:
                            act.wait_ge(lat_turned, i)
                        nc.scalar.activation(lpr[:], lneg[:], ACT.Exp, scale=-1.0).then_inc(lat_p, 1)
                    if s == 6:
                        act.wait_ge(lat_turned, i + 1)
                        nc.scalar.copy(lprT[:].rearrange("p a t -> p (a t)"), psM[:, 0:2 * P]).then_inc(lprT_ready, 1)
                act.wait_ge(lat_oT, i + 1)
                nc.scalar.copy(latT[:], psM[0:LD, 0:P]).then_inc(latT_ready, 1)

            for j in range(2):
                body(j, j, j == 0)
            with act.Fori(1, NB // 2) as g:
                for j in range(2):
                    body(j, g * 2 + j, False)
            gate_exp(NB - 1)
            keep_mixedT(NB - 1, False)

            def keep_tile(j, s, first):
                act.wait_ge(xs_turned, s + 1)
                if not first:
                    act.wait_ge(gu_ready, s - 1)
                nc.scalar.copy(xsT[:, j % 2].rearrange("p c t -> p (c t)"), psT[:, j % 2, 0:D]).then_inc(xsT_ready, 1)

            def silu(j, s, first):
                act.wait_ge(gu_ready, s + 1)
                if not first:
                    act.wait_ge(h_ready, s - 1)
                nc.scalar.activation(sg[:, j % 2, :], psS[:, j % 2, 0:F], ACT.Silu).then_inc(silu_ready, 1)

            def step(j, s, nth, final):
                if not final:
                    keep_tile((j + 1) % 4, s + 1, nth == 0)
                silu(j, s, nth < 2)

            keep_tile(0, 0, True)
            for j in range(4):
                step(j, j, j, False)
            with act.Fori(1, TILES // 4 - 1) as g:
                for j in range(4):
                    step(j, g * 4 + j, MANY, False)
            for j in range(4):
                step(j, TILES - 4 + j, MANY, j == 3)

        @block.vector
        def _(dve):
            v = nc.vector
            per = NB // NX
            for n in range(NX):
                dve.wait_ge(x_in[n], 16)
                with dve.Fori(n * per, (n + 1) * per) as i:
                    v.bn_stats(stats[:, i, :], x_all[:, i, :]).then_inc(stats_done, 1)
            dve.wait_ge(stats_done, NB)
            v.tensor_tensor(mean[:], stats[:, :, 1], stats[:, :, 4], ALU.add).then_inc(mv_done, 1)
            v.tensor_tensor(mdif[:], stats[:, :, 1], stats[:, :, 4], ALU.subtract).then_inc(mv_done, 1)
            v.tensor_tensor(var[:], stats[:, :, 2], stats[:, :, 5], ALU.add).then_inc(mv_done, 1)
            dve.wait_ge(mv_done, 3)
            v.tensor_scalar(mean[:], mean[:], 0.5, None, ALU.mult).then_inc(mv_done, 1)
            v.tensor_tensor(mdif[:], mdif[:], mdif[:], ALU.mult).then_inc(mv_done, 1)
            v.tensor_scalar(var[:], var[:], 1.0 / D, None, ALU.mult).then_inc(mv_done, 1)
            dve.wait_ge(mv_done, 6)
            v.scalar_tensor_tensor(var[:], mdif[:], 0.25, var[:], ALU.mult, ALU.add).then_inc(mv_done, 1)
            dve.wait_ge(std_done, 1)
            v.reciprocal(rstd[:], std[:]).then_inc(rstd_done, 1)
            dve.wait_ge(rstd_done, 1)

            def normalise(j, n, first):
                i = n * 4 + j
                if not first:
                    dve.wait_ge(xn_turned, i - 3)
                    dve.wait_ge(xn_out[j], 16 * n)
                v.tensor_scalar(xn_st[:, j, :], x_all[:, i, :], mean[:, bass.ds(i, 1)], rstd[:, bass.ds(i, 1)],
                                ALU.subtract, ALU.mult).then_inc(xn_staged, 1)

            for j in range(4):
                normalise(j, 0, True)
            with dve.Fori(1, NB // 4) as g:
                for j in range(4):
                    normalise(j, g, False)
            dve.wait_ge(xT_kept, NB)
            dve.wait_ge(x_biased, NB)
            dve.wait_ge(consts, 1)
            dve.wait_ge(w_in, W_ALL)

            def bcast(ap, n, at):
                return ap.unsqueeze(at).broadcast_to([*ap.shape[:at], n, *ap.shape[at:]])

            n_route = 0

            def then(ins):
                nonlocal n_route
                n_route += 1
                ins.then_inc(route_steps, 1)
                dve.wait_ge(route_steps, n_route)

            dve.wait_ge(ex_ready, NB)
            tt, ts = v.tensor_tensor, v.tensor_scalar
            sml = lambda n: small[:, n, :]
            then(ts(sc_t, ex, 1.0, None, ALU.add))
            then(v.reciprocal(scores_t, sc_t))
            then(tt(sc_t, scores_t, bcast(gbias[:], NB, 1), ALU.add))
            high = sc_t.rearrange("p t (g e) -> p (t g) e", g=G)
            low = None
            n_in, bufs = EPG, [ra_t, rb_t, rc_t]
            level = 0
            while n_in > 1:
                n_in //= 2
                size = NB * G * n_in
                flat = bufs[level].rearrange("p t e -> p (t e)")
                part = lambda m: flat[:, m * size:(m + 1) * size].rearrange("p (g e) -> p g e", e=n_in)
                a, b = high[:, :, 0:n_in], high[:, :, n_in:2 * n_in]
                new_high, new_low = part(0), part(1)
                then(tt(new_high, a, b, ALU.max))
                then(tt(new_low, a, b, ALU.min))
                if low is not None:
                    then(tt(part(2), low[:, :, 0:n_in], low[:, :, n_in:2 * n_in], ALU.max))
                    then(tt(part(3), new_low, part(2), ALU.max))
                    new_low = part(3)
                high, low = new_high, new_low
                level += 1
            group = sml(0).rearrange("p (t g) -> p t g", g=G)
            then(tt(sml(0), high.rearrange("p g e -> p (g e)"), low.rearrange("p g e -> p (g e)"), ALU.add))
            other, own = bcast(group, G, 2), bcast(group, G, 3)
            gt, ge = (x.rearrange("p t (g h) -> p t g h", g=G) for x in (ra_t, rb_t))
            then(tt(gt, other, own, ALU.is_gt))
            then(tt(ge, other, own, ALU.is_ge))
            then(tt(rb_t, rb_t, bcast(lower[:].rearrange("p g h -> p (g h)"), NB, 1), ALU.mult))
            then(tt(ra_t, ra_t, rb_t, ALU.max))
            then(v.tensor_reduce(sml(1), ra_t.rearrange("p t (g h) -> p (t g) h", g=G), AX_X, ALU.add))
            then(ts(sml(2), sml(1), TG - 0.5, None, ALU.is_lt))
            then(ts(sml(3), sml(2), FILL, FILL, ALU.mult, ALU.subtract))
            by_group = lambda x: x.rearrange("p t (g e) -> p (t g) e", g=G)
            then(tt(by_group(ra_t), by_group(sc_t), bcast(sml(2), EPG, 2), ALU.mult))
            then(tt(by_group(ra_t), by_group(ra_t), bcast(sml(3), EPG, 2), ALU.add))
            for t in range(NB):
                last = v.max(top8[:, t, :], ra_t[:, t, :])
            then(last)
            for t in range(NB):
                last = v.match_replace(rb_t[:, t, :], top8[:, t, :], ra_t[:, t, :], -1.1 * FILL)
            then(last)
            tt(sel_t, ra_t, rb_t, ALU.not_equal).then_inc(sel_ready, 1)
            dve.wait_ge(sel_ready, 1)
            then(tt(sc_t, scores_t, sel_t, ALU.mult))
            then(v.tensor_reduce(wsum[:], sc_t, AX_X, ALU.add))
            then(ts(wsum[:], wsum[:], 1e-20, None, ALU.add))
            then(v.reciprocal(wsum[:], wsum[:]))
            then(ts(wsum[:], wsum[:], SCALE, None, ALU.mult))
            weight_t = scores_t
            then(tt(weight_t, sc_t, bcast(wsum[:], E, 2), ALU.mult))
            dve.wait_ge(ranks_ready, 1)
            flat = lambda x, n: x.rearrange("p t e -> p (t e)")[:, n * 512:(n + 1) * 512]
            for n, bank in enumerate((psS[:, 0, :], psS[:, 1, :], psT[:, 0, :], psT[:, 1, :])):
                v.tensor_copy(flat(sc_t, n), bank)
            for n, bank in enumerate((psQ, psV, psM, psO)):
                last = v.tensor_copy(flat(ra_t, n), bank[:])
            then(last)
            then(tt(sc_t, sc_t, ra_t, ALU.subtract))
            src, dst, d = ra_t, rb_t, 1
            while d < NB:
                v.tensor_copy(dst[:, 0:d, :], src[:, 0:d, :])
                then(tt(dst[:, d:, :], src[:, d:, :], src[:, 0:NB - d, :], ALU.add))
                src, dst, d = dst, (rc_t if dst is rb_t else rb_t), 2 * d
            upto = src
            n_e, base, e_a, e_b, e_c = (per_e[:, n, :] for n in range(5))
            then(ts(e_a, upto[:, NB - 1, :], float(P - 1), None, ALU.add))
            then(v.tensor_copy(count_i[:], e_a))
            then(ts(count_i[:], count_i[:], 7, None, ALU.arith_shift_right))
            then(v.tensor_copy(n_e, count_i[:]))
            then(v.tensor_copy(e_a, n_e))
            src, dst, d = e_a, e_b, 1
            while d < E:
                v.tensor_copy(dst[:, 0:d], src[:, 0:d])
                then(tt(dst[:, d:], src[:, d:], src[:, 0:E - d], ALU.add))
                src, dst, d = dst, (e_c if dst is e_b else e_b), 2 * d
            ends = src
            then(tt(base, ends, n_e, ALU.subtract))
            then(ts(base, base, float(P), 1.0, ALU.mult, ALU.add))
            then(ts(ends_row[:], ends[0:1, :], 1.0, None, ALU.add))
            then(tt(tile_cmp[:], bcast(ends, QT, 1), bcast(tile_no[:], E, 2), ALU.is_le))
            then(v.tensor_reduce(tile_e[:], tile_cmp[:], AX_X, ALU.add))
            ts(tile_ei[:], tile_e[:], float(E - 1), None, ALU.min).then_inc(tiles_ready, 1)
            then(tt(sc_t, sc_t, upto, ALU.add))
            then(tt(sc_t, sc_t, bcast(base, NB, 1), ALU.add))
            then(tt(sc_t, sc_t, sel_t, ALU.mult))
            for t in range(NB):
                last = v.max(slot8[:, t, :], sc_t[:, t, :])
            then(last)
            ts(slot_idx[:], slot8[:], 1.0, None, ALU.subtract).then_inc(slots_ready, 1)
            for t in range(NB):
                for k in range(K):
                    last = v.scalar_tensor_tensor(rb_t[:, (t % 4) * K + k, :], sc_t[:, t, :], slot8[:, t, k:k + 1], weight_t[:, t, :],
                                                  ALU.is_equal, ALU.mult, accum_out=w8[:, t, k:k + 1])
                if t % 4 == 3 and t < NB - 1:
                    then(last)
            last.then_inc(routed, 1)

            def stage(j, i, blk, first):
                if not first:
                    dve.wait_ge(lat_kv, i)
                if not isinstance(i, int) or i >= 2:
                    dve.wait_ge(sh_ready, i - 1)
                v.tensor_copy(xTs[:, j, :, :], xT_all[:, i, :, :]).then_inc(xT_staged, 1)
                dve.wait_ge(xT_staged, i + 1)
                v.tensor_copy(mask[:, 0, :], mask_prev[:, blk, :]).then_inc(masks_staged, 1)
                v.tensor_copy(lat_mask[:], lat_wide[:, bass.ds((BPS - 1 - blk) * LPB, NLAT)]).then_inc(masks_staged, 1)
                src = xTs[:, j, :, :].rearrange("p c (n t) -> p c n t", t=CH)
                v.tensor_reduce(pooledT[:, :, 0, bass.ds(blk * LPB, LPB)], src, AX_X, ALU.add).then_inc(masks_staged, 1)
                dve.wait_ge(masks_staged, 3 * i + 3)
                v.tensor_copy(pooledT[:, :, 1, :], pooledT[:, :, 0, :]).then_inc(pooled, 1)

            def mix(i):
                n = 0

                def step(ins):
                    nonlocal n
                    n += 1
                    ins.then_inc(mix_steps, 1)
                    return i * 9 + n

                o = psO[:, 0:H * (HD + 1)].rearrange("p (h d) -> p h d", h=H)
                dve.wait_ge(pv_pair, NPAIR * (i + 1))
                at = step(v.tensor_scalar(den[:], o[:, :, HD], TINY, None, ALU.max))
                dve.wait_ge(mix_steps, at)
                at = step(v.reciprocal(rec[:], den[:]))
                dve.wait_ge(mix_steps, at)
                v.tensor_tensor(local[:], o[:, :, 0:HD], bcast(rec[:], HD, 2), ALU.mult).then_inc(local_kept, 1)
                dve.wait_ge(local_kept, i + 1)
                dve.wait_ge(remote_kept, i + 1)
                step(v.tensor_tensor(zl[:], local[:], bcast(gl[:], H, 1), ALU.mult))
                at = step(v.tensor_tensor(zr[:], remote[:], bcast(gr[:], H, 1), ALU.mult))
                dve.wait_ge(mix_steps, at)
                at = step(v.tensor_tensor(zs[:], zl[:], zr[:], ALU.add))
                dve.wait_ge(mix_steps, at)
                v.tensor_reduce(z[:], zs[:], AX_X, ALU.add).then_inc(z_ready, 1)
                step(v.tensor_tensor(dif[:], local[:], remote[:], ALU.subtract))
                dve.wait_ge(ez_ready, i + 1)
                at = step(v.tensor_scalar(ez1[:], ez[:], 1.0, None, ALU.add))
                dve.wait_ge(mix_steps, at)
                at = step(v.reciprocal(gate[:], ez1[:]))
                dve.wait_ge(mix_steps, at)
                at = step(v.tensor_tensor(gdif[:], dif[:], bcast(gate[:], HD, 2), ALU.mult))
                dve.wait_ge(mix_steps, at)
                v.tensor_tensor(mixed[:], gdif[:], remote[:], ALU.add).then_inc(mixed_ready, 1)

            def keep_q(j, i):
                dve.wait_ge(k_kept, i + 1)
                for c in range(DC):
                    last = v.scalar_tensor_tensor(qz[:, j, c, :, :], bcast(psQ[:, c * P:(c + 1) * P], 2, 1), bqk[:, c:c + 1],
                                                  bcast(head_parity[:], P, 2), ALU.add, ALU.mult)
                last.then_inc(q_kept, 1)

            def keep_v(j, i):
                dve.wait_ge(v_ready, i + 1)
                v.tensor_tensor(vv[:, j, :, 0:HD], psV[:, 0:D].rearrange("p (h d) -> p h d", h=H),
                                bv[:].rearrange("p (h d) -> p h d", h=H), ALU.add).then_inc(v_kept, 1)
                v.scalar_tensor_tensor(rqz[:], bcast(psV[0:LD, D:D + P], LH, 1), brq[:], bcast(rq_head[:], P, 2),
                                       ALU.add, ALU.mult).then_inc(rq_kept, 1)

            def keep_shared(j, i):
                dve.wait_ge(eg_ready, i + 1)
                v.tensor_scalar(eg1[:], eg[:], 1.0, None, ALU.add).then_inc(sh_steps, 1)
                dve.wait_ge(sh_steps, 3 * i + 1)
                v.reciprocal(sig[:], eg1[:]).then_inc(sh_steps, 1)
                dve.wait_ge(sh_steps, 3 * i + 2)
                v.tensor_tensor(gs[:], psQ[:, 0:P], sig[:], ALU.mult).then_inc(sh_steps, 1)
                dve.wait_ge(sh_steps, 3 * i + 3)
                v.tensor_tensor(hsT[:, j, :], psQ[:, P:2 * P], gs[:], ALU.mult).then_inc(hs_ready, 1)

            def accumulate(i):
                dve.wait_ge(out_ready, i + 1)
                v.tensor_tensor(x_all[:, i, :], psM[:, D:2 * D], x_all[:, i, :], ALU.add).then_inc(acc_done, 1)

            def mask_pair(i, p, first):
                n = i * NPAIR + p
                dve.wait_ge(s_ready, n + 1)
                if p >= 4 or not first:
                    dve.wait_ge(probs, 2 * (n - 3))
                v.memset(met[:, p % 4:p % 4 + 1], 0.0)
                for par in range(2):
                    v.tensor_tensor_reduce(sm[:, p % 4, par, :], psS[:, p % 2, par * 2 * P:(par + 1) * 2 * P],
                                           mask[:].rearrange("p a t -> p (a t)"), -1.0, -FLOOR, ALU.add, ALU.min,
                                           nmax[:, p % 4, par:par + 1]).then_inc(masked, 1)

            def body(j, i, blk, first):
                stage(j, i, blk, first)
                if not first:
                    mix(i - 1)
                keep_q(j, i)
                keep_v(j, i)
                keep_shared(j, i)
                if not first:
                    accumulate(i - 1)
                dve.wait_ge(masks_staged, 3 * i + 2)
                for p in range(NPAIR):
                    mask_pair(i, p, first)
                    if p == 1:
                        dve.wait_ge(lat_kv, i + 1)
                        v.tensor_scalar(rkT[:], psM[0:LD, 0:NLAT], 1.0 / CH, brk[:], ALU.mult, ALU.add).then_inc(rk_kept, 1)
                        for par in range(2):
                            r = slice(par * NLAT, (par + 1) * NLAT)
                            v.scalar_tensor_tensor(rv[r, par::2, 0:LHD],
                                                   psM[r, NLAT:NLAT + LD].rearrange("p (h d) -> p h d", h=LH)[:, par::2, :], 1.0 / CH,
                                                   brv[r, :].rearrange("p (h d) -> p h d", h=LH)[:, par::2, :],
                                                   ALU.mult, ALU.add).then_inc(rk_kept, 1)
                    if p == 3:
                        dve.wait_ge(lat_s, i + 1)
                        v.tensor_tensor(lsm[:], psM[:, 0:LH * NLAT].rearrange("p (h n) -> p h n", h=LH), bcast(lat_mask[:], LH, 1),
                                        ALU.add).then_inc(lat_steps, 1)
                        dve.wait_ge(lat_steps, 4 * i + 1)
                        v.tensor_reduce(lmax[:], lsm[:], AX_X, ALU.max).then_inc(lat_steps, 1)
                        dve.wait_ge(lat_steps, 4 * i + 2)
                        v.scalar_tensor_tensor(lneg[:], bcast(lmax[:], NLAT, 2), FLOOR, lsm[:], ALU.max, ALU.subtract).then_inc(lat_neg, 1)
                dve.wait_ge(lat_o, i + 1)
                lo = psM[:, 0:LH * (LHD + 1)].rearrange("p (h d) -> p h d", h=LH)
                v.tensor_scalar(lden[:], lo[:, :, LHD], TINY, None, ALU.max).then_inc(lat_steps, 1)
                dve.wait_ge(lat_steps, 4 * i + 3)
                v.reciprocal(lrec[:], lden[:]).then_inc(lat_steps, 1)
                dve.wait_ge(lat_steps, 4 * i + 4)
                v.tensor_tensor(lat[:, 0:LD].rearrange("p (h d) -> p h d", h=LH), lo[:, :, 0:LHD], bcast(lrec[:], LHD, 2),
                                ALU.mult).then_inc(lat_kept, 1)
                dve.wait_ge(remote_ready, i + 1)
                v.tensor_tensor(remote[:].rearrange("p h d -> p (h d)"), psM[:, D:2 * D], brout[:], ALU.add).then_inc(remote_kept, 1)

            for j in range(2):
                body(j, j, j, j == 0)
            with dve.Fori(1, NB // 2) as g:
                for j in range(2):
                    body(j, g * 2 + j, (g % (BPS // 2)) * 2 + j, False)
            mix(NB - 1)
            accumulate(NB - 1)

            def make_h(j, s, first):
                dve.wait_ge(silu_ready, s + 1)
                if not first:
                    dve.wait_ge(h_turned, s - 1)
                v.tensor_tensor(hh[:, j % 2, :], psS[:, j % 2, F:2 * F], sg[:, j % 2, :], ALU.mult).then_inc(h_ready, 1)

            def keep_hT(j, s, first):
                dve.wait_ge(h_turned, s + 1)
                if not first:
                    dve.wait_ge(tiles_done, s)
                v.tensor_copy(hhT[:, j % 2, :], (psQ, psV)[j % 2][:, 0:P]).then_inc(hT_ready, 1)

            def keep_y(j, s, turn, first):
                dve.wait_ge(tiles_done, s + 2)
                if not first:
                    dve.wait_ge(y_out[j], 16 * turn)
                v.tensor_copy(ys[:, j, :], (psM, psO)[j % 2][:, 0:D]).then_inc(y_kept, 1)

            def step(j, g, nth):
                s = g * 4 + j
                if nth > 0:
                    keep_hT((j - 1) % 4, s - 1, nth <= 2)
                make_h(j, s, nth < 2)
                if nth > 0:
                    keep_y((j - 1) % 4, s - 1, g - (0 if j else 1), nth <= 4)

            for j in range(4):
                step(j, 0, j)
            for j in range(4):
                step(j, 1, 4 + j)
            with dve.Fori(2, TILES // 4) as g:
                for j in range(4):
                    step(j, g, MANY)
            keep_hT(3, TILES - 1, False)
            keep_y(3, TILES - 1, TILES // 4 - 1, False)

            def combine(j, g):
                i = 2 * g + j
                dve.wait_ge(rows_ready[j], 16 * K * (g + 1))
                for k in range(K):
                    ins = v.scalar_tensor_tensor(x_all[:, i, :], rows_in[:, j, k, :], w8[:, i, k:k + 1], x_all[:, i, :],
                                                 ALU.mult, ALU.add)
                    if k < K - 1:
                        ins.then_inc(combine_steps, 1)
                        dve.wait_ge(combine_steps, (K - 1) * i + k + 1)
                    else:
                        ins.then_inc(combined, 1)

            with dve.Fori(0, NB // 2) as g:
                for j in range(2):
                    combine(j, g)


_INS = ['L0_attn_x', 'L0_attn_qkv_w', 'L0_attn_qkv_b', 'L0_attn_rq_w', 'L0_attn_rq_b', 'L0_attn_rkv_w', 'L0_attn_rkv_b',
        'L0_attn_rout_w', 'L0_attn_rout_b', 'L0_attn_out_w', 'L0_attn_out_b', 'L0_attn_gl_w', 'L0_attn_gr_w',
        'L0_ffn_gate_w', 'L0_ffn_gate_bias', 'L0_ffn_We_gate', 'L0_ffn_We_up', 'L0_ffn_We_down',
        'L0_ffn_Ws_gate', 'L0_ffn_Ws_up', 'L0_ffn_Ws_down']


def kernel(**inputs):
    import numpy as np
    import concourse.bacc as bacc
    from concourse.bass_utils import run_bass_kernel_spmd

    nc = bacc.Bacc("TRN2", target_bir_lowering=False, num_devices=1)
    arrays, aps = {}, {}
    for name in _INS:
        arrays[f"in_{name}"] = np.ascontiguousarray(inputs[name])
        aps[name] = nc.dram_tensor(f"in_{name}", arrays[f"in_{name}"].shape, F32, kind="ExternalInput").ap()
    out = nc.dram_tensor("out", (B, S, D), F32, kind="ExternalOutput").ap()
    build(nc, aps, out)
    r = run_bass_kernel_spmd(nc, [arrays], core_ids=[0])
    return r.results[0]["out"]
```

```python
from contextlib import ExitStack

import concourse.bass as bass
import concourse.mybir as mybir
from concourse.alu_op_type import AluOpType as ALU

ACT = mybir.ActivationFunctionType
AX_X = mybir.AxisListType.X
F32 = mybir.dt.float32
I32 = mybir.dt.int32
U32 = mybir.dt.uint32

P = 128
B, S, D = 4, 1024, 256
T = B * S
NB = T // P
BPS = S // P
DC = D // P
H, HD = 16, 16
HPC = P // HD
NPAIR = H // 2
LD, LH = 64, 4
LHD = LD // LH
NLAT = 64
CH = S // NLAT
LPB = P // CH
E, F, K = 64, 128, 8
G, TG = 8, 4
EPG = E // G
SCALE = 2.5
TILES = (T * K + E * (P - 1)) // P // 4 * 4 + 4
SLOTS = TILES * P
PAIRS = TILES // 2
XS, YS = 4, 2
HALF = NB // 2
QT = -(-TILES // P)
RING = 14
WE = 3 * D
MANY = 9
ZROWS = 8
FILL = 3e38
EPS = 1e-5
NEG = -1e30
FLOOR = -1e20
TINY = 1e-30


def build(nc, A, out):
    with ExitStack() as ctx:
        def sb(name, shape, dt=F32):
            return ctx.enter_context(nc.sbuf_tensor(name, shape, dt))

        def ps(name, shape):
            return ctx.enter_context(nc.psum_tensor(name, shape, F32))

        def sem(name):
            return ctx.enter_context(nc.semaphore(name))

        x_all = sb("x_all", [P, NB, D])
        xT_all = sb("xT_all", [P, NB, DC, P])
        wqkv = sb("wqkv", [P, DC, 3 * D])
        wrq = sb("wrq", [P, DC, LD])
        wrkv = sb("wrkv", [P, DC, 2 * LD])
        wout = sb("wout", [P, DC, D])
        wrout = sb("wrout", [LD, D])
        wsg = sb("wsg", [P, DC, F])
        wsu = sb("wsu", [P, DC, F])
        wsd = sb("wsd", [F, D])
        gate_rows = sb("gate_rows", [E, D])
        gateT = sb("gateT", [P, DC, E])
        bqk = sb("bqk", [P, 2 * DC])
        bv = sb("bv", [P, D])
        brq = sb("brq", [LD, 1])
        brk = sb("brk", [LD, 1])
        brv = sb("brv", [P, LD])
        brout = sb("brout", [P, D])
        bout = sb("bout", [P, D])
        gl = sb("gl", [P, HD])
        gr = sb("gr", [P, HD])
        ident = sb("ident", [P, P])
        head_parity = sb("head_parity", [P, 2])
        rq_head = sb("rq_head", [LD, LH])
        mask_prev = sb("mask_prev", [P, P])
        no_past = sb("no_past", [P, BPS])
        mask = sb("mask", [P, 2, P])
        lat_wide = sb("lat_wide", [P, NLAT - LPB + NLAT])
        lat_mask = sb("lat_mask", [P, NLAT])
        eps = sb("eps", [P, 1])
        stats = sb("stats", [P, NB, 6])
        mean = sb("mean", [P, NB])
        mdif = sb("mdif", [P, NB])
        var = sb("var", [P, NB])
        std = sb("std", [P, NB])
        rstd = sb("rstd", [P, NB])
        xn_st = sb("xn_st", [P, 4, D])
        xTa = sb("xTa", [P, 2, DC, P])
        shared_mem = sb("shared_mem", [P, RING * WE])
        table = lambda n: shared_mem[:, n * NB * E:(n + 1) * NB * E].rearrange("p (t e) -> p t e", t=NB)
        scores_t, sc_t, ra_t, rb_t, sel_t = (table(n) for n in range(5))
        ring_gu = shared_mem[:, 0:RING * 2 * D].rearrange("p (r c n) -> p r c n", r=RING, c=DC)
        ring_d = shared_mem[:, RING * 2 * D:RING * WE].rearrange("p (r n) -> p r n", r=RING)
        rows_in = shared_mem[:, 0:2 * K * D].rearrange("p (j k d) -> p j k d", j=2, k=K)
        gbias = sb("gbias", [P, E])
        lower = sb("lower", [P, G, G])
        before = sb("before", [P, P])
        ones = sb("ones", [P, P])
        small = sb("small", [P, 4, NB * G])
        top8 = sb("top8", [P, NB, K])
        slot8 = sb("slot8", [P, NB, K])
        slot_idx = sb("slot_idx", [P, NB, K], U32)
        w8 = sb("w8", [P, NB, K])
        wsum = sb("wsum", [P, NB])
        wj = sb("wj", [P, 2, E])
        count_i = sb("count_i", [P, E], I32)
        per_e = sb("per_e", [P, 5, E])
        tile_no_i = sb("tile_no_i", [P, QT], I32)
        tile_no = sb("tile_no", [P, QT])
        tile_cmp = sb("tile_cmp", [P, QT, E])
        tile_e = sb("tile_e", [P, QT])
        tile_ei = sb("tile_ei", [P, QT], I32)
        expert_row = sb("expert_row", [1, QT * P], I32)
        pair_row = sb("pair_row", [1, QT * P // 2], I32)
        ends_row = sb("ends_row", [1, E], I32)
        x_out_st = sb("x_out_st", [P, 2, D])
        idx_st = sb("idx_st", [P, 2, K], U32)
        ex = scores_t
        xTs = sb("xTs", [P, 2, DC, P])
        qz = sb("qz", [P, 2, DC, 2, P])
        kT = sb("kT", [P, 2, DC, P])
        vv = sb("vv", [P, 2, H, HD + 1])
        rqz = sb("rqz", [LD, LH, P])
        pooledT = sb("pooledT", [P, DC, 2, NLAT])
        rkT = sb("rkT", [LD, NLAT])
        rv = sb("rv", [P, LH, LHD + 1])
        sm = sb("sm", [P, 4, 2, 2 * P])
        nmax = sb("nmax", [P, 4, 2])
        pr = sb("pr", [P, 4, 2, 2 * P])
        prT = sb("prT", [P, 2, 2, 2, P])
        lsm = sb("lsm", [P, LH, NLAT])
        lmax = sb("lmax", [P, LH])
        lneg = sb("lneg", [P, LH, NLAT])
        lpr = sb("lpr", [P, LH, NLAT])
        lprT = sb("lprT", [P, 2, P])
        lden = sb("lden", [P, LH])
        lrec = sb("lrec", [P, LH])
        lat = sb("lat", [P, P])
        latT = sb("latT", [LD, P])
        remote = sb("remote", [P, H, HD])
        den = sb("den", [P, H])
        met = sb("met", [1, 4])
        rec = sb("rec", [P, H])
        local = sb("local", [P, H, HD])
        zl = sb("zl", [P, H, HD])
        zr = sb("zr", [P, H, HD])
        zs = sb("zs", [P, H, HD])
        z = sb("z", [P, H])
        ez = sb("ez", [P, H])
        ez1 = sb("ez1", [P, H])
        gate = sb("gate", [P, H])
        dif = sb("dif", [P, H, HD])
        gdif = sb("gdif", [P, H, HD])
        mixed = sb("mixed", [P, H, HD])
        zeros = pr[:].rearrange("p a b t -> p (a b t)")
        rc_t = sm[:].rearrange("p a b (t e) -> p (a b t) e", e=E)
        pr_mem, sm_mem = (x[:].rearrange("p a b t -> p (a b t)") for x in (pr, sm))
        xs = pr_mem[:, 0:XS * 2 * D].rearrange("p (j a d) -> p j a d", j=XS, a=2)
        ys = sm_mem[:, 0:YS * 2 * D].rearrange("p (j a d) -> p j a d", j=YS, a=2)
        xsT = sm_mem[:, YS * 2 * D:(YS + 2) * 2 * D].rearrange("p (j a c t) -> p j a c t", j=2, a=2, c=DC)
        sg, hh = (prT[:].rearrange("p a b c t -> p (a b c t)")[:, n * 4 * F:(n + 1) * 4 * F].rearrange("p (j a f) -> p j a f", j=2, a=2)
                  for n in range(2))
        hhT = sb("hhT", [P, 2, 2, P])
        mixedT = sb("mixedT", [P, DC, P])
        eg = sb("eg", [F, P])
        eg1 = sb("eg1", [F, P])
        sig = sb("sig", [F, P])
        gs = sb("gs", [F, P])
        hsT = sb("hsT", [F, 2, P])

        psQ = ps("psQ", [P, 512])
        psV = ps("psV", [P, 512])
        psS = ps("psS", [P, 2, 512])
        psT = ps("psT", [P, 2, 512])
        psM = ps("psM", [P, 512])
        psO = ps("psO", [P, 512])

        NX = 4
        x_in = [sem(f"x_in{n}") for n in range(NX)]
        w_in = sem("w_in")
        consts = sem("consts")
        pool_order = sem("pool_order")
        gw_turned = sem("gw_turned")
        gw_ready = sem("gw_ready")
        stats_done = sem("stats_done")
        mv_done = sem("mv_done")
        std_done = sem("std_done")
        rstd_done = sem("rstd_done")
        xn_staged = sem("xn_staged")
        xn_turned = sem("xn_turned")
        xTa_ready = sem("xTa_ready")
        logits = sem("logits")
        ex_ready = sem("ex_ready")
        xT_kept = sem("xT_kept")
        xn_out = [sem(f"xn_out{j}") for j in range(4)]
        x_biased = sem("x_biased")
        xT_staged = sem("xT_staged")
        masks_staged = sem("masks_staged")
        pooled = sem("pooled")
        qk_ready = sem("qk_ready")
        v_ready = sem("v_ready")
        sh_ready = sem("sh_ready")
        q_kept = sem("q_kept")
        k_kept = sem("k_kept")
        v_kept = sem("v_kept")
        rq_kept = sem("rq_kept")
        eg_ready = sem("eg_ready")
        sh_steps = sem("sh_steps")
        hs_ready = sem("hs_ready")
        s_ready = sem("s_ready")
        masked = sem("masked")
        probs = sem("probs")
        probs_turned = sem("probs_turned")
        prT_ready = sem("prT_ready")
        pv_pair = sem("pv_pair")
        lat_kv = sem("lat_kv")
        rk_kept = sem("rk_kept")
        lat_s = sem("lat_s")
        lat_steps = sem("lat_steps")
        lat_neg = sem("lat_neg")
        lat_p = sem("lat_p")
        lat_turned = sem("lat_turned")
        lprT_ready = sem("lprT_ready")
        lat_o = sem("lat_o")
        lat_kept = sem("lat_kept")
        lat_oT = sem("lat_oT")
        latT_ready = sem("latT_ready")
        remote_ready = sem("remote_ready")
        remote_kept = sem("remote_kept")
        mix_steps = sem("mix_steps")
        z_ready = sem("z_ready")
        ez_ready = sem("ez_ready")
        local_kept = sem("local_kept")
        mixed_ready = sem("mixed_ready")
        mixed_turned = sem("mixed_turned")
        mixedT_ready = sem("mixedT_ready")
        out_ready = sem("out_ready")
        acc_done = sem("acc_done")
        stored = sem("stored")
        blocks_staged = sem("blocks_staged")
        cleared = sem("cleared")
        zeros_ready = sem("zeros_ready")
        route_steps = sem("route_steps")
        sel_ready = sem("sel_ready")
        ranks_ready = sem("ranks_ready")
        slots_ready = sem("slots_ready")
        tiles_ready = sem("tiles_ready")
        experts_known = sem("experts_known")
        words_ready = sem("words_ready")
        routed = sem("routed")
        scatter_in = [sem(f"scatter_in{j}") for j in range(2)]
        scattered = [sem(f"scattered{j}") for j in range(2)]
        weights_in = [sem(f"weights_in{j}") for j in range(2)]
        experts_ready = sem("experts_ready")
        pairs_done = sem("pairs_done")
        xs_in = [sem(f"xs_in{j}") for j in range(XS)]
        xs_turned = sem("xs_turned")
        xsT_ready = sem("xsT_ready")
        gu_ready = sem("gu_ready")
        silu_ready = sem("silu_ready")
        h_ready = sem("h_ready")
        h_turned = sem("h_turned")
        hT_ready = sem("hT_ready")
        y_ready = sem("y_ready")
        y_kept = sem("y_kept")
        y_out = [sem(f"y_out{j}") for j in range(YS)]
        idx_in = [sem(f"idx_in{j}") for j in range(2)]
        rows_ready = [sem(f"rows_ready{j}") for j in range(2)]
        combine_steps = sem("combine_steps")
        combined = sem("combined")
        slot_rows = nc.dram_tensor("slot_rows", (SLOTS, D), F32, kind="Internal").ap()
        slot_outs = nc.dram_tensor("slot_outs", (SLOTS, D), F32, kind="Internal").ap()
        xn_tiles = nc.dram_tensor("xn_tiles", (NB, P, D), F32, kind="Internal").ap()
        slot_pairs = slot_rows.rearrange("(u a p) d -> u p a d", a=2, p=P)
        out_pairs = slot_outs.rearrange("(u a p) d -> u p a d", a=2, p=P)

        xt = A["L0_attn_x"].rearrange("b (t p) d -> p (b t) d", p=P)
        yt = out.rearrange("b (t p) d -> p (b t) d", p=P)
        rows = lambda w: w.rearrange("(c p) n -> p c n", p=P)
        col = lambda b, n: b.rearrange("(c p) -> p c", p=n)
        W_ALL = 16 * 19
        block = ctx.enter_context(nc.Block())

        @block.sync
        def _(sp):
            for n in range(NX):
                t = slice(n * NB // NX, (n + 1) * NB // NX)
                sp.dma_start(x_all[:, t, :], xt[:, t, :]).then_inc(x_in[n], 16)
            spread = lambda v: v.partition_broadcast(P)
            with nc.allow_non_contiguous_dma("biases, one value a partition"):
                for dst, src in (
                    (gate_rows[:], A["L0_ffn_gate_w"]),
                    (wqkv[:], rows(A["L0_attn_qkv_w"])),
                    (wrq[:], rows(A["L0_attn_rq_w"])),
                    (wrkv[:], rows(A["L0_attn_rkv_w"])),
                    (wout[:], rows(A["L0_attn_out_w"])),
                    (wrout[:], A["L0_attn_rout_w"]),
                    (wsg[:], rows(A["L0_ffn_Ws_gate"])),
                    (wsu[:], rows(A["L0_ffn_Ws_up"])),
                    (wsd[:], A["L0_ffn_Ws_down"]),
                    (bqk[:], col(A["L0_attn_qkv_b"][0:2 * D], P)),
                    (bv[:], spread(A["L0_attn_qkv_b"][2 * D:3 * D])),
                    (brq[:], col(A["L0_attn_rq_b"], LD)),
                    (brk[:], col(A["L0_attn_rkv_b"][0:LD], LD)),
                    (brv[:], spread(A["L0_attn_rkv_b"][LD:2 * LD])),
                    (brout[:], spread(A["L0_attn_rout_b"])),
                    (bout[:], spread(A["L0_attn_out_b"])),
                    (gl[:], spread(A["L0_attn_gl_w"].rearrange("d a -> (d a)"))),
                    (gr[:], spread(A["L0_attn_gr_w"].rearrange("d a -> (d a)"))),
                    (gbias[:], spread(A["L0_ffn_gate_bias"])),
                ):
                    sp.dma_start(dst, src).then_inc(w_in, 16)
            def store_xn(j, i):
                sp.wait_ge(xn_staged, i + 1)
                sp.dma_start(xn_tiles[i], xn_st[:, j, :]).then_inc(xn_out[j], 16)

            with sp.Fori(0, NB // 4) as g:
                for j in range(4):
                    store_xn(j, g * 4 + j)
            sp.wait_ge(zeros_ready, 1)
            clear = slot_rows.rearrange("(n p r) d -> n p (r d)", p=P, r=ZROWS)
            with sp.Fori(0, SLOTS // (P * ZROWS)) as n:
                sp.dma_start(clear[n], zeros).then_inc(cleared, 16)
            sp.wait_ge(tiles_ready, 1)
            with nc.allow_non_contiguous_dma("a column to a row"):
                for q in range(QT):
                    sp.dma_start(expert_row[0:1, q * P:(q + 1) * P], tile_ei[:, q:q + 1]).then_inc(experts_known, 16)

            def stage_scatter(j, i, first):
                if not first:
                    sp.wait_ge(scattered[j], 16 * K * i)
                sp.dma_start(x_out_st[:, j, :], xn_tiles[2 * i + j]).then_inc(scatter_in[j], 16)
                sp.dma_start(idx_st[:, j, :], slot_idx[:, 2 * i + j, :]).then_inc(scatter_in[j], 16)

            sp.wait_ge(slots_ready, 1)
            for j in range(4):
                sp.wait_ge(xn_out[j], 16 * (NB // 4))
            for j in range(2):
                stage_scatter(j, 0, True)
            with sp.Fori(1, NB // 2) as g:
                for j in range(2):
                    stage_scatter(j, g, False)
            for j in range(2):
                sp.wait_ge(scattered[j], 16 * K * NB // 2)

            sp.wait_ge(probs_turned, HALF * NPAIR)
            sp.wait_ge(masked, 2 * HALF * NPAIR)
            sp.wait_ge(probs, 2 * HALF * NPAIR)

            def load_pair(j, g, first):
                u = g * XS + j
                if not first:
                    sp.wait_ge(xs_turned, u - XS + 1)
                sp.dma_start(xs[:, j, :, :], slot_pairs[u]).then_inc(xs_in[j], 16)

            def store_pair(j, u):
                sp.wait_ge(y_kept, u + 1)
                sp.dma_start(out_pairs[u], ys[:, j % YS, :, :]).then_inc(y_out[j % YS], 16)

            for j in range(XS):
                load_pair(j, 0, True)
            with sp.Fori(1, PAIRS // XS) as g:
                for j in range(XS):
                    load_pair(j, g, False)
                    store_pair(j, (g - 1) * XS + j)
            for j in range(XS):
                store_pair(j, PAIRS - XS + j)
            for j in range(YS):
                sp.wait_ge(y_out[j], 16 * (PAIRS // YS))

            def stage_gather(j, i, first):
                if not first:
                    sp.wait_ge(rows_ready[j], 16 * K * i)
                sp.dma_start(idx_st[:, j, :], slot_idx[:, 2 * i + j, :]).then_inc(idx_in[j], 16)

            def store_block(i):
                sp.wait_ge(combined, i + 1)
                sp.wait_ge(acc_done, i + 1)
                sp.dma_start(yt[:, i, :], x_all[:, i, :]).then_inc(stored, 16)

            for j in range(2):
                stage_gather(j, 0, True)
            with sp.Fori(1, NB // 2) as g:
                for j in range(2):
                    stage_gather(j, g, False)
                    store_block(2 * g + j - 2)
            for j in range(2):
                store_block(NB - 2 + j)
            sp.wait_ge(stored, 16 * NB)

        @block.gpsimd
        def _(pool):
            steps = 0

            def after(ins):
                nonlocal steps
                steps += 1
                ins.then_inc(pool_order, 1)
                pool.wait_ge(pool_order, steps)

            def fill(v, value, tests):
                for pattern, base, mult, op in tests:
                    after(nc.gpsimd.affine_select(out=v, in_=v, compare_op=op, fill=value, base=base,
                                                  pattern=pattern, channel_multiplier=mult))

            nc.gpsimd.memset(zeros, 0.0).then_inc(zeros_ready, 1)
            after(nc.gpsimd.memset(ident[:], 0.0))
            after(nc.gpsimd.memset(ones[:], 1.0))
            after(nc.gpsimd.memset(before[:], 1.0))
            fill(before[:], 0.0, [([[1, P]], -1, -1, ALU.is_ge)])
            after(nc.gpsimd.memset(lower[:], 1.0))
            fill(lower[:], 0.0, [([[1, G], [-1, G]], -1, 0, ALU.is_ge)])
            after(nc.gpsimd.iota(tile_no_i[:], pattern=[[P, QT]], base=0, channel_multiplier=1))
            after(nc.gpsimd.tensor_copy(tile_no[:], tile_no_i[:]))
            fill(ident[:], 1.0, [([[-1, P]], 0, 1, ALU.not_equal)])
            after(nc.gpsimd.memset(eps[:], EPS))
            after(nc.gpsimd.memset(head_parity[:], 0.0))
            for par in range(2):
                for n in range(HPC // 2):
                    lo = (2 * n + par) * HD
                    v = head_parity[:, par:par + 1]
                    t = gate[:, 0:1]
                    after(nc.gpsimd.memset(t, HD ** -0.5))
                    fill(t, 0.0, [([[0, 1]], -lo, 1, ALU.is_ge), ([[0, 1]], lo + HD - 1, -1, ALU.is_ge)])
                    after(nc.gpsimd.tensor_tensor(v, v, t, ALU.add))
            after(nc.gpsimd.memset(rq_head[:], LHD ** -0.5))
            fill(rq_head[:], 0.0, [([[-LHD, LH]], 0, 1, ALU.is_ge), ([[LHD, LH]], LHD - 1, -1, ALU.is_ge)])
            after(nc.gpsimd.memset(mask_prev[:], 0.0))
            fill(mask_prev[:], NEG, [([[1, P]], 0, -1, ALU.is_ge), ([[1, P]], -1, 0, ALU.is_ge)])
            after(nc.gpsimd.memset(no_past[:], 0.0))
            after(nc.gpsimd.memset(no_past[:, 0:1], NEG))
            after(nc.gpsimd.memset(mask[:], 0.0))
            fill(mask[:, 1, :], NEG, [([[-1, P]], -1, 1, ALU.is_ge)])
            after(nc.gpsimd.memset(lat_wide[:], 0.0))
            fill(lat_wide[:], NEG, [([[-CH, 2 * NLAT - LPB]], CH * (NLAT - LPB) - CH, 1, ALU.is_ge)])
            after(nc.gpsimd.memset(vv[:], 1.0))
            after(nc.gpsimd.memset(vv[:, 1, :, 0:HD], 0.0))
            after(nc.gpsimd.memset(kT[:, 1, :, :], 0.0))
            after(nc.gpsimd.memset(rv[:], 0.0))
            for par in range(2):
                after(nc.gpsimd.memset(rv[par * NLAT:(par + 1) * NLAT, par::2, LHD:LHD + 1], 1.0))
            after(nc.gpsimd.memset(lat[:], 0.0))
            nc.gpsimd.memset(pooledT[:], 0.0).then_inc(consts, 1)
            pool.wait_ge(w_in, W_ALL)
            with pool.Fori(0, NB // 2) as g:
                for j in range(2):
                    i = g * 2 + j
                    pool.wait_ge(xn_staged, i + 1)
                    pool.wait_ge(consts, 1)
                    nc.gpsimd.tensor_tensor(x_all[:, i, :], x_all[:, i, :], bout[:], ALU.add).then_inc(x_biased, 1)
                    pool.wait_ge(xTa_ready, i + 1)
                    pool.wait_ge(consts, 1)
                    nc.gpsimd.tensor_copy(xT_all[:, i, :, :], xTa[:, j, :, :]).then_inc(xT_kept, 1)

            def scatter(j, g):
                pool.wait_ge(scatter_in[j], 32 * (g + 1))
                pool.sem_inc(blocks_staged, 1)
                for k in range(K):
                    pool.indirect_dma_start(slot_rows, bass.IndirectOffsetOnAxis(ap=idx_st[:, j, k:k + 1], axis=0),
                                            x_out_st[:, j, :], None).then_inc(scattered[j], 16)

            pool.wait_ge(cleared, 16 * (SLOTS // (P * ZROWS)))
            with pool.Fori(0, NB // 2) as g:
                for j in range(2):
                    scatter(j, g)

            def load_expert(j, e, first):
                if not first:
                    end = pool.value_load(ends_row[0:1, bass.ds(e - RING, 1)], min_val=1, max_val=PAIRS + 1)
                    pool.wait_ge(pairs_done, end)
                r = e % RING
                pool.dma_start(ring_gu[:, r, :, 0:F], rows(A["L0_ffn_We_gate"][e])).then_inc(weights_in[j], 16)
                pool.dma_start(ring_gu[:, r, :, F:2 * F], rows(A["L0_ffn_We_up"][e])).then_inc(weights_in[j], 16)
                pool.dma_start(ring_d[:, r, :], A["L0_ffn_We_down"][e]).then_inc(weights_in[j], 16)

            def announce(j, g):
                pool.wait_ge(weights_in[j], 48 * (g + 1))
                pool.sem_inc(experts_ready, 1)

            pool.wait_ge(routed, 1)
            load_expert(0, 0, True)
            load_expert(1, 1, True)
            with pool.Fori(1, RING // 2) as g:
                for j in range(2):
                    announce(j, g - 1)
                    load_expert(j, 2 * g + j, True)
            with pool.Fori(RING // 2, E // 2) as g:
                for j in range(2):
                    announce(j, g - 1)
                    load_expert(j, 2 * g + j, False)
            for j in range(2):
                announce(j, E // 2 - 1)

            def gather(j, g, first):
                pool.wait_ge(idx_in[j], 16 * (g + 1))
                if not first:
                    pool.wait_ge(combined, 2 * g + j - 1)
                pool.sem_inc(blocks_staged, 1)
                for k in range(K):
                    pool.indirect_dma_start(rows_in[:, j, k, :], None, slot_outs,
                                            bass.IndirectOffsetOnAxis(ap=idx_st[:, j, k:k + 1], axis=0)
                                            ).then_inc(rows_ready[j], 16)

            for j in range(YS):
                pool.wait_ge(y_out[j], 16 * (PAIRS // YS))
            for j in range(2):
                gather(j, 0, True)
            with pool.Fori(1, NB // 2) as g:
                for j in range(2):
                    gather(j, g, False)

        @block.tensor
        def _(pe):
            mm = nc.tensor.matmul

            pe.wait_ge(w_in, W_ALL)
            pe.wait_ge(consts, 1)
            for c in range(DC):
                last = nc.tensor.transpose(psM[:, c * E:(c + 1) * E], gate_rows[:, c * P:(c + 1) * P], ident[0:E, 0:E])
            last.then_inc(gw_turned, 1)

            def turn_x(j, i, first):
                pe.wait_ge(xn_staged, i + 1)
                if not first:
                    pe.wait_ge(xTa_ready, i - 1)
                for c in range(DC):
                    last = nc.tensor.transpose(psT[:, j % 2, c * P:(c + 1) * P], xn_st[:, j, c * P:(c + 1) * P], ident[:])
                last.then_inc(xn_turned, 1)

            def route(j, i, first):
                pe.wait_ge(xTa_ready, i + 1)
                if not first:
                    pe.wait_ge(ex_ready, i - 1)
                for c in range(DC):
                    last = mm(psS[:, j % 2, 0:E], xTa[:, j % 2, c, :], gateT[:, c, :], start=(c == 0), stop=(c == DC - 1))
                last.then_inc(logits, 1)

            pe.wait_ge(gw_ready, 1)
            for j in range(4):
                turn_x(j, j, j < 2)
                route(j, j, j < 2)
            with pe.Fori(1, NB // 4) as g:
                for j in range(4):
                    turn_x(j, g * 4 + j, False)
                    route(j, g * 4 + j, False)

            pe.wait_ge(sel_ready, 1)
            sel_flat = sel_t.rearrange("p t e -> p (t e)")
            for n in range(4):
                mm((psS[:, n, :] if n < 2 else psT[:, n - 2, :]), before[:], sel_flat[:, n * 512:(n + 1) * 512], start=True, stop=True)
            for n, bank in enumerate((psQ, psV, psM, psO)):
                last = mm(bank[:], ones[:], sel_flat[:, n * 512:(n + 1) * 512], start=True, stop=True)
            last.then_inc(ranks_ready, 1)
            pe.wait_ge(routed, 1)

            def project(j, i, first):
                pe.wait_ge(xT_staged, i + 1)
                if not first:
                    pe.wait_ge(hs_ready, i)
                for m in range(2 * DC):
                    for c in range(DC):
                        last = mm(psQ[:, m * P:(m + 1) * P], wqkv[:, c, m * P:(m + 1) * P], xTs[:, j, c, :],
                                  start=(c == 0), stop=(c == DC - 1))
                last.then_inc(qk_ready, 1)
                if not first:
                    pe.wait_ge(rq_kept, i)
                for c in range(DC):
                    mm(psV[:, 0:D], xTs[:, j, c, :], wqkv[:, c, 2 * D:3 * D], start=(c == 0), stop=(c == DC - 1))
                for c in range(DC):
                    last = mm(psV[0:LD, D:D + P], wrq[:, c, :], xTs[:, j, c, :], start=(c == 0), stop=(c == DC - 1))
                last.then_inc(v_ready, 1)

            def shared(j, i):
                pe.wait_ge(q_kept, i + 1)
                pe.wait_ge(k_kept, i + 1)
                for n, w in enumerate((wsg, wsu)):
                    for c in range(DC):
                        last = mm(psQ[:, n * P:(n + 1) * P], w[:, c, :], xTs[:, j, c, :], start=(c == 0), stop=(c == DC - 1))
                last.then_inc(sh_ready, 1)

            def turn_mixed(i):
                pe.wait_ge(mixed_ready, i + 1)
                for c in range(DC):
                    last = nc.tensor.transpose(psM[:, c * P:(c + 1) * P],
                                               mixed[:].rearrange("p h d -> p (h d)")[:, c * P:(c + 1) * P], ident[:])
                last.then_inc(mixed_turned, 1)

            def out_project(j, i):
                pe.wait_ge(mixedT_ready, i + 1)
                pe.wait_ge(hs_ready, i + 1)
                for c in range(DC):
                    mm(psM[:, D:2 * D], mixedT[:, c, :], wout[:, c, :], start=(c == 0), stop=False)
                mm(psM[:, D:2 * D], hsT[:, j, :], wsd[:], start=False, stop=True).then_inc(out_ready, 1)

            def scores(j, i, p, first):
                n = i * NPAIR + p
                if p == 0:
                    pe.wait_ge(q_kept, i + 1)
                    pe.wait_ge(k_kept, i + 1)
                if p >= 2 or not first:
                    pe.wait_ge(masked, 2 * (n - 1))
                c, r = p // (NPAIR // DC), (p % (NPAIR // DC)) * 2 * HD
                for par in range(2):
                    for half in range(2):
                        last = mm(psS[:, p % 2, (2 * par + half) * P:(2 * par + half + 1) * P],
                                  qz[r:r + 2 * HD, j, c, par, :], kT[r:r + 2 * HD, (j + 1 + half) % 2, c, :],
                                  start=True, stop=True)
                last.then_inc(s_ready, 1)

            def turn_probs(i, p, first):
                n = i * NPAIR + p
                pe.wait_ge(probs, 2 * n + 2)
                if p >= 2 or not first:
                    pe.wait_ge(prT_ready, n - 1)
                for par in range(2):
                    for half in range(2):
                        last = nc.tensor.transpose(psT[:, p % 2, (2 * par + half) * P:(2 * par + half + 1) * P],
                                                   pr[:, p % 4, par, half * P:(half + 1) * P], ident[:])
                last.then_inc(probs_turned, 1)

            def values(j, i, p, first):
                n = i * NPAIR + p
                pe.wait_ge(prT_ready, n + 1)
                if p == 0:
                    pe.wait_ge(v_kept, i + 1)
                    if not first:
                        pe.wait_ge(local_kept, i)
                for par in range(2):
                    h = 2 * p + par
                    for half in range(2):
                        last = mm(psO[:, h * (HD + 1):(h + 1) * (HD + 1)], prT[:, p % 2, par, half, :],
                                  vv[:, (j + 1 + half) % 2, h, :], start=(half == 0), stop=(half == 1))
                last.then_inc(pv_pair, 1)

            def latent_kv(i, first):
                pe.wait_ge(pooled, i + 1)
                if not first:
                    pe.wait_ge(acc_done, i)
                for c in range(DC):
                    mm(psM[0:LD, 0:NLAT], wrkv[:, c, 0:LD], pooledT[:, c, 0, :], start=(c == 0), stop=(c == DC - 1))
                for c in range(DC):
                    last = mm(psM[:, NLAT:NLAT + LD], pooledT[:, c, :, :].rearrange("p a n -> p (a n)"), wrkv[:, c, LD:2 * LD],
                              start=(c == 0), stop=(c == DC - 1))
                last.then_inc(lat_kv, 1)

            def latent_scores(i):
                pe.wait_ge(rk_kept, 3 * i + 3)
                pe.wait_ge(rq_kept, i + 1)
                for h in range(LH):
                    last = mm(psM[:, h * NLAT:(h + 1) * NLAT], rqz[:, h, :], rkT[:], start=True, stop=True)
                last.then_inc(lat_s, 1)

            def latent_turn(i):
                pe.wait_ge(lat_p, i + 1)
                flat = lpr[:].rearrange("p h n -> p (h n)")
                for n in range(2):
                    last = nc.tensor.transpose(psM[:, n * P:(n + 1) * P], flat[:, n * P:(n + 1) * P], ident[:])
                last.then_inc(lat_turned, 1)

            def latent_values(i):
                pe.wait_ge(lprT_ready, i + 1)
                for n in range(LH // 2):
                    last = mm(psM[:, 2 * n * (LHD + 1):2 * (n + 1) * (LHD + 1)], lprT[:, n, :],
                              rv[:, 2 * n:2 * n + 2, :].rearrange("p h d -> p (h d)"), start=True, stop=True)
                last.then_inc(lat_o, 1)

            def latent_out_turn(i):
                pe.wait_ge(lat_kept, i + 1)
                nc.tensor.transpose(psM[:, 0:P], lat[:], ident[:]).then_inc(lat_oT, 1)

            def latent_project(i):
                pe.wait_ge(latT_ready, i + 1)
                mm(psM[:, D:2 * D], latT[:], wrout[:], start=True, stop=True).then_inc(remote_ready, 1)

            def body(j, i, first, tail):
                project(j, i, first)
                if tail:
                    turn_mixed(i - 1)
                shared(j, i)
                if tail:
                    out_project(1 - j, i - 1)
                for s in range(NPAIR + 3):
                    if s < NPAIR:
                        scores(j, i, s, first)
                    if 2 <= s < NPAIR + 2:
                        turn_probs(i, s - 2, first)
                    if 3 <= s:
                        values(j, i, s - 3, first)
                    if s == 0:
                        latent_kv(i, first)
                    if s == 2:
                        latent_scores(i)
                    if s == 5:
                        latent_turn(i)
                    if s == 7:
                        latent_values(i)
                    if s == 9:
                        latent_out_turn(i)
                    if s == 10:
                        latent_project(i)

            def attention(start):
                for j in range(2):
                    body(j, start + j, start + j == 0, j > 0)
                with pe.Fori(start // 2 + 1, (start + HALF) // 2) as g:
                    for j in range(2):
                        body(j, g * 2 + j, False, True)
                turn_mixed(start + HALF - 1)
                out_project(1, start + HALF - 1)

            def turn_tiles(j, u, turn, first):
                pe.wait_ge(xs_in[j], 16 * (turn + 1))
                if not first:
                    pe.wait_ge(xsT_ready, u - 1)
                for a in range(2):
                    for c in range(DC):
                        last = nc.tensor.transpose(psT[:, j % 2, (a * DC + c) * P:(a * DC + c + 1) * P],
                                                   xs[:, j, a, c * P:(c + 1) * P], ident[:])
                last.then_inc(xs_turned, 1)

            def experts_of(u):
                word = pe.value_load(pair_row[0:1, bass.ds(u, 1)], min_val=0, max_val=E * E - 1)
                return word % E, word // E

            def gate_up(j, u, experts, first):
                if not first:
                    pe.wait_ge(h_ready, u - 1)
                pe.wait_ge(xsT_ready, u + 1)
                pe.wait_ge(experts_ready, experts[1] + 1)
                for a, e in enumerate(experts):
                    for c in range(DC):
                        last = mm(psS[:, j % 2, a * 2 * F:(a + 1) * 2 * F], xsT[:, j % 2, a, c, :], ring_gu[:, e % RING, c, :],
                                  start=(c == 0), stop=(c == DC - 1))
                last.then_inc(gu_ready, 1)

            def turn_h(j, u, first):
                pe.wait_ge(h_ready, u + 1)
                if not first:
                    pe.wait_ge(hT_ready, u - 1)
                for a in range(2):
                    last = nc.tensor.transpose((psQ, psV)[j % 2][:, a * P:(a + 1) * P], hh[:, j % 2, a, :], ident[:])
                last.then_inc(h_turned, 1)

            def down(j, u, experts, first):
                pe.wait_ge(hT_ready, u + 1)
                if not first:
                    pe.wait_ge(y_kept, u - 1)
                for a, e in enumerate(experts):
                    last = mm((psM, psO)[j % 2][:, a * D:(a + 1) * D], hhT[:, j % 2, a, :], ring_d[:, e % RING, :],
                              start=True, stop=True)
                last.then_inc(pairs_done, 1)

            def round_of(g, nth, final):
                u = g * XS
                before = experts_of(u - 1) if nth > 0 else None
                now = experts_of(u)
                for j in range(XS):
                    gate_up(j, u + j, now, nth + j < 2)
                    after = experts_of(u + j + 1) if j < XS - 1 else None
                    if not (final and j == XS - 1):
                        turn_tiles((j + 1) % XS, u + j + 1, g + (j + 1) // XS, nth + j == 0)
                    if nth + j > 0:
                        down((j - 1) % XS, u + j - 1, before, nth + j <= 2)
                    turn_h(j, u + j, nth + j < 2)
                    before, now = now, after
                return before

            def experts():
                turn_tiles(0, 0, 0, True)
                round_of(0, 0, False)
                with pe.Fori(1, PAIRS // XS - 1) as g:
                    round_of(g, MANY, False)
                last = round_of(PAIRS // XS - 1, MANY, True)
                down(XS - 1, PAIRS - 1, last, False)

            pe.wait_ge(xT_kept, NB)
            attention(0)
            pe.wait_ge(words_ready, 1)
            pe.wait_ge(acc_done, HALF)
            pe.sem_inc(pairs_done, 1)
            experts()
            pe.wait_ge(y_kept, PAIRS)
            attention(HALF)

        @block.scalar
        def _(act):
            act.wait_ge(gw_turned, 1)
            nc.scalar.copy(gateT[:].rearrange("p c e -> p (c e)"), psM[:, 0:DC * E]).then_inc(gw_ready, 1)
            act.wait_ge(mv_done, 7)
            nc.scalar.activation(std[:], var[:], ACT.Sqrt, bias=eps[:]).then_inc(std_done, 1)

            def keep_xT(j, i, first):
                act.wait_ge(xn_turned, i + 1)
                if not first:
                    act.wait_ge(xT_kept, i - 1)
                    act.wait_ge(logits, i - 1)
                nc.scalar.copy(xTa[:, j, :, :].rearrange("p c t -> p (c t)"), psT[:, j, 0:D]).then_inc(xTa_ready, 1)
                act.wait_ge(logits, i + 1)
                nc.scalar.activation(ex[:, i, :], psS[:, j, 0:E], ACT.Exp, scale=-1.0).then_inc(ex_ready, 1)

            for j in range(2):
                keep_xT(j, j, True)
            with act.Fori(1, NB // 2) as g:
                for j in range(2):
                    keep_xT(j, g * 2 + j, False)

            def keep_k(j, i, first):
                act.wait_ge(qk_ready, i + 1)
                if not first:
                    act.wait_ge(s_ready, NPAIR * i)
                act.wait_ge(consts, 1)
                for c in range(DC):
                    last = nc.scalar.activation(kT[:, j, c, :], psQ[:, (DC + c) * P:(DC + c + 1) * P], ACT.Identity,
                                                bias=bqk[:, DC + c:DC + c + 1])
                last.then_inc(k_kept, 1)

            def gate_exp(i):
                act.wait_ge(z_ready, i + 1)
                nc.scalar.activation(ez[:], z[:], ACT.Exp, scale=-1.0).then_inc(ez_ready, 1)

            def keep_mixedT(i, first):
                act.wait_ge(mixed_turned, i + 1)
                if not first:
                    act.wait_ge(out_ready, i)
                nc.scalar.copy(mixedT[:].rearrange("p c t -> p (c t)"), psM[:, 0:D]).then_inc(mixedT_ready, 1)

            def shared_exp(i, first):
                act.wait_ge(sh_ready, i + 1)
                if not first:
                    act.wait_ge(hs_ready, i)
                nc.scalar.activation(eg[:], psQ[:, 0:P], ACT.Exp, scale=-1.0).then_inc(eg_ready, 1)

            act.wait_ge(cleared, 16 * (SLOTS // (P * ZROWS)))
            act.wait_ge(routed, 1)

            def exps(i, p, first):
                n = i * NPAIR + p
                if p >= 4 or not first:
                    act.wait_ge(probs_turned, n - 3)
                for par in range(2):
                    act.wait_ge(masked, 2 * n + par + 1)
                    nc.scalar.activation(pr[:, p % 4, par, :], sm[:, p % 4, par, :], ACT.Exp,
                                         bias=nmax[:, p % 4, par:par + 1], scale=-1.0).then_inc(probs, 1)

            def keep_prT(i, p, first):
                n = i * NPAIR + p
                act.wait_ge(probs_turned, n + 1)
                if p >= 2 or not first:
                    act.wait_ge(pv_pair, n - 1)
                nc.scalar.copy(prT[:, p % 2].rearrange("p a b t -> p (a b t)"), psT[:, p % 2, :]).then_inc(prT_ready, 1)

            def body(j, i, first, tail):
                keep_k(j, i, first)
                if tail:
                    gate_exp(i - 1)
                    keep_mixedT(i - 1, isinstance(i, int) and i == 1)
                shared_exp(i, first)
                for s in range(NPAIR + 2):
                    if s < NPAIR:
                        exps(i, s, first)
                    if 2 <= s:
                        keep_prT(i, s - 2, first)
                    if s == 4:
                        act.wait_ge(lat_neg, i + 1)
                        if not first:
                            act.wait_ge(lat_turned, i)
                        nc.scalar.activation(lpr[:], lneg[:], ACT.Exp, scale=-1.0).then_inc(lat_p, 1)
                    if s == 6:
                        act.wait_ge(lat_turned, i + 1)
                        nc.scalar.copy(lprT[:].rearrange("p a t -> p (a t)"), psM[:, 0:2 * P]).then_inc(lprT_ready, 1)
                act.wait_ge(lat_oT, i + 1)
                nc.scalar.copy(latT[:], psM[0:LD, 0:P]).then_inc(latT_ready, 1)

            def attention(start):
                for j in range(2):
                    body(j, start + j, start + j == 0, j > 0)
                with act.Fori(start // 2 + 1, (start + HALF) // 2) as g:
                    for j in range(2):
                        body(j, g * 2 + j, False, True)
                gate_exp(start + HALF - 1)
                keep_mixedT(start + HALF - 1, False)

            def keep_tiles(j, u, first):
                act.wait_ge(xs_turned, u + 1)
                if not first:
                    act.wait_ge(gu_ready, u - 1)
                nc.scalar.copy(xsT[:, j % 2].rearrange("p a c t -> p (a c t)"), psT[:, j % 2, :]).then_inc(xsT_ready, 1)

            def silu(j, u, first):
                act.wait_ge(gu_ready, u + 1)
                if not first:
                    act.wait_ge(h_ready, u - 1)
                nc.scalar.activation(sg[:, j % 2, :, :], psS[:, j % 2, :].rearrange("p (a n) -> p a n", a=2)[:, :, 0:F],
                                     ACT.Silu).then_inc(silu_ready, 1)

            def step(j, g, nth, final):
                u = g * XS + j
                silu(j, u, nth < 2)
                if not final:
                    keep_tiles((j + 1) % XS, u + 1, nth == 0)

            def experts():
                keep_tiles(0, 0, True)
                for j in range(XS):
                    step(j, 0, j, False)
                with act.Fori(1, PAIRS // XS - 1) as g:
                    for j in range(XS):
                        step(j, g, MANY, False)
                for j in range(XS):
                    step(j, PAIRS // XS - 1, MANY, j == XS - 1)

            attention(0)
            act.wait_ge(masked, 2 * HALF * NPAIR)
            act.wait_ge(pv_pair, HALF * NPAIR)
            experts()
            act.wait_ge(xs_turned, PAIRS)
            act.wait_ge(h_turned, PAIRS)
            attention(HALF)

        @block.vector
        def _(dve):
            v = nc.vector
            per = NB // NX
            for n in range(NX):
                dve.wait_ge(x_in[n], 16)
                with dve.Fori(n * per, (n + 1) * per) as i:
                    v.bn_stats(stats[:, i, :], x_all[:, i, :]).then_inc(stats_done, 1)
            dve.wait_ge(stats_done, NB)
            v.tensor_tensor(mean[:], stats[:, :, 1], stats[:, :, 4], ALU.add).then_inc(mv_done, 1)
            v.tensor_tensor(mdif[:], stats[:, :, 1], stats[:, :, 4], ALU.subtract).then_inc(mv_done, 1)
            v.tensor_tensor(var[:], stats[:, :, 2], stats[:, :, 5], ALU.add).then_inc(mv_done, 1)
            dve.wait_ge(mv_done, 3)
            v.tensor_scalar(mean[:], mean[:], 0.5, None, ALU.mult).then_inc(mv_done, 1)
            v.tensor_tensor(mdif[:], mdif[:], mdif[:], ALU.mult).then_inc(mv_done, 1)
            v.tensor_scalar(var[:], var[:], 1.0 / D, None, ALU.mult).then_inc(mv_done, 1)
            dve.wait_ge(mv_done, 6)
            v.scalar_tensor_tensor(var[:], mdif[:], 0.25, var[:], ALU.mult, ALU.add).then_inc(mv_done, 1)
            dve.wait_ge(std_done, 1)
            v.reciprocal(rstd[:], std[:]).then_inc(rstd_done, 1)
            dve.wait_ge(rstd_done, 1)

            def normalise(j, n, first):
                i = n * 4 + j
                if not first:
                    dve.wait_ge(xn_turned, i - 3)
                    dve.wait_ge(xn_out[j], 16 * n)
                v.tensor_scalar(xn_st[:, j, :], x_all[:, i, :], mean[:, bass.ds(i, 1)], rstd[:, bass.ds(i, 1)],
                                ALU.subtract, ALU.mult).then_inc(xn_staged, 1)

            for j in range(4):
                normalise(j, 0, True)
            with dve.Fori(1, NB // 4) as g:
                for j in range(4):
                    normalise(j, g, False)
            dve.wait_ge(xT_kept, NB)
            dve.wait_ge(x_biased, NB)
            dve.wait_ge(consts, 1)
            dve.wait_ge(w_in, W_ALL)

            def bcast(ap, n, at):
                return ap.unsqueeze(at).broadcast_to([*ap.shape[:at], n, *ap.shape[at:]])

            n_route = 0

            def then(ins):
                nonlocal n_route
                n_route += 1
                ins.then_inc(route_steps, 1)
                dve.wait_ge(route_steps, n_route)

            dve.wait_ge(ex_ready, NB)
            tt, ts = v.tensor_tensor, v.tensor_scalar
            sml = lambda n: small[:, n, :]
            then(ts(sc_t, ex, 1.0, None, ALU.add))
            then(v.reciprocal(scores_t, sc_t))
            then(tt(sc_t, scores_t, bcast(gbias[:], NB, 1), ALU.add))
            high = sc_t.rearrange("p t (g e) -> p (t g) e", g=G)
            low = None
            n_in, bufs = EPG, [ra_t, rb_t, rc_t]
            level = 0
            while n_in > 1:
                n_in //= 2
                size = NB * G * n_in
                flat = bufs[level].rearrange("p t e -> p (t e)")
                part = lambda m: flat[:, m * size:(m + 1) * size].rearrange("p (g e) -> p g e", e=n_in)
                a, b = high[:, :, 0:n_in], high[:, :, n_in:2 * n_in]
                new_high, new_low = part(0), part(1)
                then(tt(new_high, a, b, ALU.max))
                then(tt(new_low, a, b, ALU.min))
                if low is not None:
                    then(tt(part(2), low[:, :, 0:n_in], low[:, :, n_in:2 * n_in], ALU.max))
                    then(tt(part(3), new_low, part(2), ALU.max))
                    new_low = part(3)
                high, low = new_high, new_low
                level += 1
            group = sml(0).rearrange("p (t g) -> p t g", g=G)
            then(tt(sml(0), high.rearrange("p g e -> p (g e)"), low.rearrange("p g e -> p (g e)"), ALU.add))
            other, own = bcast(group, G, 2), bcast(group, G, 3)
            gt, ge = (x.rearrange("p t (g h) -> p t g h", g=G) for x in (ra_t, rb_t))
            then(tt(gt, other, own, ALU.is_gt))
            then(tt(ge, other, own, ALU.is_ge))
            then(tt(rb_t, rb_t, bcast(lower[:].rearrange("p g h -> p (g h)"), NB, 1), ALU.mult))
            then(tt(ra_t, ra_t, rb_t, ALU.max))
            then(v.tensor_reduce(sml(1), ra_t.rearrange("p t (g h) -> p (t g) h", g=G), AX_X, ALU.add))
            then(ts(sml(2), sml(1), TG - 0.5, None, ALU.is_lt))
            then(ts(sml(3), sml(2), FILL, FILL, ALU.mult, ALU.subtract))
            by_group = lambda x: x.rearrange("p t (g e) -> p (t g) e", g=G)
            then(tt(by_group(ra_t), by_group(sc_t), bcast(sml(2), EPG, 2), ALU.mult))
            then(tt(by_group(ra_t), by_group(ra_t), bcast(sml(3), EPG, 2), ALU.add))
            for t in range(NB):
                last = v.max(top8[:, t, :], ra_t[:, t, :])
            then(last)
            for t in range(NB):
                last = v.match_replace(rb_t[:, t, :], top8[:, t, :], ra_t[:, t, :], -1.1 * FILL)
            then(last)
            tt(sel_t, ra_t, rb_t, ALU.not_equal).then_inc(sel_ready, 1)
            dve.wait_ge(sel_ready, 1)
            then(tt(sc_t, scores_t, sel_t, ALU.mult))
            then(v.tensor_reduce(wsum[:], sc_t, AX_X, ALU.add))
            then(ts(wsum[:], wsum[:], 1e-20, None, ALU.add))
            then(v.reciprocal(wsum[:], wsum[:]))
            then(ts(wsum[:], wsum[:], SCALE, None, ALU.mult))
            weight_t = scores_t
            then(tt(weight_t, sc_t, bcast(wsum[:], E, 2), ALU.mult))
            dve.wait_ge(ranks_ready, 1)
            flat = lambda x, n: x.rearrange("p t e -> p (t e)")[:, n * 512:(n + 1) * 512]
            for n, bank in enumerate((psS[:, 0, :], psS[:, 1, :], psT[:, 0, :], psT[:, 1, :])):
                v.tensor_copy(flat(sc_t, n), bank)
            for n, bank in enumerate((psQ, psV, psM, psO)):
                last = v.tensor_copy(flat(ra_t, n), bank[:])
            then(last)
            then(tt(sc_t, sc_t, ra_t, ALU.subtract))
            src, dst, d = ra_t, rb_t, 1
            while d < NB:
                v.tensor_copy(dst[:, 0:d, :], src[:, 0:d, :])
                then(tt(dst[:, d:, :], src[:, d:, :], src[:, 0:NB - d, :], ALU.add))
                src, dst, d = dst, (rc_t if dst is rb_t else rb_t), 2 * d
            upto = src
            n_e, base, e_a, e_b, e_c = (per_e[:, n, :] for n in range(5))
            then(ts(e_a, upto[:, NB - 1, :], float(P - 1), None, ALU.add))
            then(v.tensor_copy(count_i[:], e_a))
            then(ts(count_i[:], count_i[:], 7, None, ALU.arith_shift_right))
            then(v.tensor_copy(n_e, count_i[:]))
            then(v.tensor_copy(e_a, n_e))
            src, dst, d = e_a, e_b, 1
            while d < E:
                v.tensor_copy(dst[:, 0:d], src[:, 0:d])
                then(tt(dst[:, d:], src[:, d:], src[:, 0:E - d], ALU.add))
                src, dst, d = dst, (e_c if dst is e_b else e_b), 2 * d
            ends = src
            then(tt(base, ends, n_e, ALU.subtract))
            then(ts(base, base, float(P), 1.0, ALU.mult, ALU.add))
            then(ts(ends_row[:], ends[0:1, :], 3.0, None, ALU.add))
            then(ts(ends_row[:], ends_row[:], 1, None, ALU.arith_shift_right))
            then(tt(tile_cmp[:], bcast(ends, QT, 1), bcast(tile_no[:], E, 2), ALU.is_le))
            then(v.tensor_reduce(tile_e[:], tile_cmp[:], AX_X, ALU.add))
            ts(tile_ei[:], tile_e[:], float(E - 1), None, ALU.min).then_inc(tiles_ready, 1)
            then(tt(sc_t, sc_t, upto, ALU.add))
            then(tt(sc_t, sc_t, bcast(base, NB, 1), ALU.add))
            then(tt(sc_t, sc_t, sel_t, ALU.mult))
            for t in range(NB):
                last = v.max(slot8[:, t, :], sc_t[:, t, :])
            then(last)
            ts(slot_idx[:], slot8[:], 1.0, None, ALU.subtract).then_inc(slots_ready, 1)
            for t in range(NB):
                for k in range(K):
                    last = v.scalar_tensor_tensor(rb_t[:, (t % 4) * K + k, :], sc_t[:, t, :], slot8[:, t, k:k + 1], weight_t[:, t, :],
                                                  ALU.is_equal, ALU.mult, accum_out=w8[:, t, k:k + 1])
                if t % 4 == 3 and t < NB - 1:
                    then(last)
            last.then_inc(routed, 1)

            def stage(j, i, blk, first):
                if not first:
                    dve.wait_ge(lat_kv, i)
                if not isinstance(i, int) or i >= 2:
                    dve.wait_ge(sh_ready, i - 1)
                v.tensor_copy(xTs[:, j, :, :], xT_all[:, i, :, :]).then_inc(xT_staged, 1)
                dve.wait_ge(xT_staged, i + 1)
                v.tensor_scalar(mask[:, 0, :], mask_prev[:], no_past[:, bass.ds(blk, 1)], None, ALU.add).then_inc(masks_staged, 1)
                v.tensor_copy(lat_mask[:], lat_wide[:, bass.ds((BPS - 1 - blk) * LPB, NLAT)]).then_inc(masks_staged, 1)
                src = xTs[:, j, :, :].rearrange("p c (n t) -> p c n t", t=CH)
                v.tensor_reduce(pooledT[:, :, 0, bass.ds(blk * LPB, LPB)], src, AX_X, ALU.add).then_inc(masks_staged, 1)
                dve.wait_ge(masks_staged, 3 * i + 3)
                v.tensor_copy(pooledT[:, :, 1, :], pooledT[:, :, 0, :]).then_inc(pooled, 1)

            def mix(i):
                n = 0

                def step(ins):
                    nonlocal n
                    n += 1
                    ins.then_inc(mix_steps, 1)
                    return i * 9 + n

                o = psO[:, 0:H * (HD + 1)].rearrange("p (h d) -> p h d", h=H)
                dve.wait_ge(pv_pair, NPAIR * (i + 1))
                at = step(v.tensor_scalar(den[:], o[:, :, HD], TINY, None, ALU.max))
                dve.wait_ge(mix_steps, at)
                at = step(v.reciprocal(rec[:], den[:]))
                dve.wait_ge(mix_steps, at)
                v.tensor_tensor(local[:], o[:, :, 0:HD], bcast(rec[:], HD, 2), ALU.mult).then_inc(local_kept, 1)
                dve.wait_ge(local_kept, i + 1)
                dve.wait_ge(remote_kept, i + 1)
                step(v.tensor_tensor(zl[:], local[:], bcast(gl[:], H, 1), ALU.mult))
                at = step(v.tensor_tensor(zr[:], remote[:], bcast(gr[:], H, 1), ALU.mult))
                dve.wait_ge(mix_steps, at)
                at = step(v.tensor_tensor(zs[:], zl[:], zr[:], ALU.add))
                dve.wait_ge(mix_steps, at)
                v.tensor_reduce(z[:], zs[:], AX_X, ALU.add).then_inc(z_ready, 1)
                step(v.tensor_tensor(dif[:], local[:], remote[:], ALU.subtract))
                dve.wait_ge(ez_ready, i + 1)
                at = step(v.tensor_scalar(ez1[:], ez[:], 1.0, None, ALU.add))
                dve.wait_ge(mix_steps, at)
                at = step(v.reciprocal(gate[:], ez1[:]))
                dve.wait_ge(mix_steps, at)
                at = step(v.tensor_tensor(gdif[:], dif[:], bcast(gate[:], HD, 2), ALU.mult))
                dve.wait_ge(mix_steps, at)
                v.tensor_tensor(mixed[:], gdif[:], remote[:], ALU.add).then_inc(mixed_ready, 1)

            def keep_q(j, i):
                dve.wait_ge(k_kept, i + 1)
                for c in range(DC):
                    last = v.scalar_tensor_tensor(qz[:, j, c, :, :], bcast(psQ[:, c * P:(c + 1) * P], 2, 1), bqk[:, c:c + 1],
                                                  bcast(head_parity[:], P, 2), ALU.add, ALU.mult)
                last.then_inc(q_kept, 1)

            def keep_v(j, i):
                dve.wait_ge(v_ready, i + 1)
                v.tensor_tensor(vv[:, j, :, 0:HD], psV[:, 0:D].rearrange("p (h d) -> p h d", h=H),
                                bv[:].rearrange("p (h d) -> p h d", h=H), ALU.add).then_inc(v_kept, 1)
                v.scalar_tensor_tensor(rqz[:], bcast(psV[0:LD, D:D + P], LH, 1), brq[:], bcast(rq_head[:], P, 2),
                                       ALU.add, ALU.mult).then_inc(rq_kept, 1)

            def keep_shared(j, i):
                dve.wait_ge(eg_ready, i + 1)
                v.tensor_scalar(eg1[:], eg[:], 1.0, None, ALU.add).then_inc(sh_steps, 1)
                dve.wait_ge(sh_steps, 3 * i + 1)
                v.reciprocal(sig[:], eg1[:]).then_inc(sh_steps, 1)
                dve.wait_ge(sh_steps, 3 * i + 2)
                v.tensor_tensor(gs[:], psQ[:, 0:P], sig[:], ALU.mult).then_inc(sh_steps, 1)
                dve.wait_ge(sh_steps, 3 * i + 3)
                v.tensor_tensor(hsT[:, j, :], psQ[:, P:2 * P], gs[:], ALU.mult).then_inc(hs_ready, 1)

            def accumulate(i):
                dve.wait_ge(out_ready, i + 1)
                v.tensor_tensor(x_all[:, i, :], psM[:, D:2 * D], x_all[:, i, :], ALU.add).then_inc(acc_done, 1)

            def mask_pair(i, p, first):
                n = i * NPAIR + p
                dve.wait_ge(s_ready, n + 1)
                if p >= 4 or not first:
                    dve.wait_ge(probs, 2 * (n - 3))
                v.memset(met[:, p % 4:p % 4 + 1], 0.0)
                for par in range(2):
                    v.tensor_tensor_reduce(sm[:, p % 4, par, :], psS[:, p % 2, par * 2 * P:(par + 1) * 2 * P],
                                           mask[:].rearrange("p a t -> p (a t)"), -1.0, -FLOOR, ALU.add, ALU.min,
                                           nmax[:, p % 4, par:par + 1]).then_inc(masked, 1)

            def body(j, i, blk, first, tail):
                stage(j, i, blk, first)
                if tail:
                    mix(i - 1)
                keep_q(j, i)
                keep_v(j, i)
                keep_shared(j, i)
                if tail:
                    accumulate(i - 1)
                dve.wait_ge(masks_staged, 3 * i + 2)
                for p in range(NPAIR):
                    mask_pair(i, p, first)
                    if p == 1:
                        dve.wait_ge(lat_kv, i + 1)
                        v.tensor_scalar(rkT[:], psM[0:LD, 0:NLAT], 1.0 / CH, brk[:], ALU.mult, ALU.add).then_inc(rk_kept, 1)
                        for par in range(2):
                            r = slice(par * NLAT, (par + 1) * NLAT)
                            v.scalar_tensor_tensor(rv[r, par::2, 0:LHD],
                                                   psM[r, NLAT:NLAT + LD].rearrange("p (h d) -> p h d", h=LH)[:, par::2, :], 1.0 / CH,
                                                   brv[r, :].rearrange("p (h d) -> p h d", h=LH)[:, par::2, :],
                                                   ALU.mult, ALU.add).then_inc(rk_kept, 1)
                    if p == 3:
                        dve.wait_ge(lat_s, i + 1)
                        v.tensor_tensor(lsm[:], psM[:, 0:LH * NLAT].rearrange("p (h n) -> p h n", h=LH), bcast(lat_mask[:], LH, 1),
                                        ALU.add).then_inc(lat_steps, 1)
                        dve.wait_ge(lat_steps, 4 * i + 1)
                        v.tensor_reduce(lmax[:], lsm[:], AX_X, ALU.max).then_inc(lat_steps, 1)
                        dve.wait_ge(lat_steps, 4 * i + 2)
                        v.scalar_tensor_tensor(lneg[:], bcast(lmax[:], NLAT, 2), FLOOR, lsm[:], ALU.max, ALU.subtract).then_inc(lat_neg, 1)
                dve.wait_ge(lat_o, i + 1)
                lo = psM[:, 0:LH * (LHD + 1)].rearrange("p (h d) -> p h d", h=LH)
                v.tensor_scalar(lden[:], lo[:, :, LHD], TINY, None, ALU.max).then_inc(lat_steps, 1)
                dve.wait_ge(lat_steps, 4 * i + 3)
                v.reciprocal(lrec[:], lden[:]).then_inc(lat_steps, 1)
                dve.wait_ge(lat_steps, 4 * i + 4)
                v.tensor_tensor(lat[:, 0:LD].rearrange("p (h d) -> p h d", h=LH), lo[:, :, 0:LHD], bcast(lrec[:], LHD, 2),
                                ALU.mult).then_inc(lat_kept, 1)
                dve.wait_ge(remote_ready, i + 1)
                v.tensor_tensor(remote[:].rearrange("p h d -> p (h d)"), psM[:, D:2 * D], brout[:], ALU.add).then_inc(remote_kept, 1)

            def combine(j, i, n):
                dve.wait_ge(rows_ready[j], 16 * K * (n + 1))
                dve.wait_ge(acc_done, 1)
                for k in range(K):
                    ins = v.scalar_tensor_tensor(x_all[:, i, :], rows_in[:, j, k, :], w8[:, i, k:k + 1], x_all[:, i, :],
                                                 ALU.mult, ALU.add)
                    if k < K - 1:
                        ins.then_inc(combine_steps, 1)
                        dve.wait_ge(combine_steps, (K - 1) * i + k + 1)
                    else:
                        ins.then_inc(combined, 1)

            def attention(start, combining):
                def step(j, i, blk, first, tail):
                    body(j, i, blk, first, tail)
                    if combining:
                        for n in range(2):
                            combine(n, 2 * (i - start) + n, i - start)

                for j in range(2):
                    step(j, start + j, j, start + j == 0, j > 0)
                with dve.Fori(start // 2 + 1, (start + HALF) // 2) as g:
                    for j in range(2):
                        step(j, g * 2 + j, (g % (BPS // 2)) * 2 + j, False, True)
                mix(start + HALF - 1)
                accumulate(start + HALF - 1)

            def make_h(j, u, first):
                dve.wait_ge(silu_ready, u + 1)
                if not first:
                    dve.wait_ge(h_turned, u - 1)
                v.tensor_tensor(hh[:, j % 2, :, :], psS[:, j % 2, :].rearrange("p (a n) -> p a n", a=2)[:, :, F:2 * F],
                                sg[:, j % 2, :, :], ALU.mult).then_inc(h_ready, 1)

            def keep_hT(j, u, first):
                dve.wait_ge(h_turned, u + 1)
                if not first:
                    dve.wait_ge(pairs_done, u)
                v.tensor_copy(hhT[:, j % 2, :, :].rearrange("p a t -> p (a t)"), (psQ, psV)[j % 2][:, 0:2 * P]).then_inc(hT_ready, 1)

            def keep_y(j, u, turn, first):
                dve.wait_ge(pairs_done, u + 2)
                if not first:
                    dve.wait_ge(y_out[j % YS], 16 * turn)
                v.tensor_copy(ys[:, j % YS, :, :].rearrange("p a d -> p (a d)"), (psM, psO)[j % 2][:]).then_inc(y_kept, 1)

            def step(j, g, nth):
                u = g * XS + j
                make_h(j, u, nth < 2)
                if nth > 0:
                    keep_y((j - 1) % XS, u - 1, 2 * g + (j + 1) // YS - 1, nth <= 2)
                keep_hT(j, u, nth < 2)

            def experts():
                dve.wait_ge(experts_known, 16 * QT)
                by_pair = expert_row[:].rearrange("p (u a) -> p u a", a=2)
                v.scalar_tensor_tensor(pair_row[:], by_pair[:, :, 1], float(E), by_pair[:, :, 0], ALU.mult, ALU.add).then_inc(words_ready, 1)
                for j in range(XS):
                    step(j, 0, j)
                with dve.Fori(1, PAIRS // XS) as g:
                    for j in range(XS):
                        step(j, g, MANY)
                keep_y(XS - 1, PAIRS - 1, PAIRS // YS - 1, False)

            attention(0, False)
            dve.wait_ge(probs, 2 * HALF * NPAIR)
            dve.wait_ge(pv_pair, HALF * NPAIR)
            experts()
            for j in range(YS):
                dve.wait_ge(y_out[j], 16 * (PAIRS // YS))
            dve.wait_ge(gu_ready, PAIRS)
            attention(HALF, True)


_INS = ['L0_attn_x', 'L0_attn_qkv_w', 'L0_attn_qkv_b', 'L0_attn_rq_w', 'L0_attn_rq_b', 'L0_attn_rkv_w', 'L0_attn_rkv_b',
        'L0_attn_rout_w', 'L0_attn_rout_b', 'L0_attn_out_w', 'L0_attn_out_b', 'L0_attn_gl_w', 'L0_attn_gr_w',
        'L0_ffn_gate_w', 'L0_ffn_gate_bias', 'L0_ffn_We_gate', 'L0_ffn_We_up', 'L0_ffn_We_down',
        'L0_ffn_Ws_gate', 'L0_ffn_Ws_up', 'L0_ffn_Ws_down']


def kernel(**inputs):
    import numpy as np
    import concourse.bacc as bacc
    from concourse.bass_utils import run_bass_kernel_spmd

    nc = bacc.Bacc("TRN2", target_bir_lowering=False, num_devices=1)
    arrays, aps = {}, {}
    for name in _INS:
        arrays[f"in_{name}"] = np.ascontiguousarray(inputs[name])
        aps[name] = nc.dram_tensor(f"in_{name}", arrays[f"in_{name}"].shape, F32, kind="ExternalInput").ap()
    out = nc.dram_tensor("out", (B, S, D), F32, kind="ExternalOutput").ap()
    build(nc, aps, out)
    r = run_bass_kernel_spmd(nc, [arrays], core_ids=[0])
    return r.results[0]["out"]
```

```python
from contextlib import ExitStack

import concourse.bass as bass
import concourse.mybir as mybir
from concourse.alu_op_type import AluOpType as ALU

ACT = mybir.ActivationFunctionType
AX_X = mybir.AxisListType.X
F32 = mybir.dt.float32
I32 = mybir.dt.int32
U32 = mybir.dt.uint32

P = 128
B, S, D = 4, 1024, 256
T = B * S
NB = T // P
BPS = S // P
DC = D // P
H, HD = 16, 16
HPC = P // HD
NPAIR = H // 2
LD, LH = 64, 4
LHD = LD // LH
NLAT = 64
CH = S // NLAT
LPB = P // CH
PPC = NPAIR // DC
E, F, K = 64, 128, 8
G, TG = 8, 4
EPG = E // G
SCALE = 2.5
TILES = (T * K + E * (P - 1)) // P // 4 * 4 + 4
SLOTS = TILES * P
PAIRS = TILES // 2
XS, YS = 4, 2
HALF = NB // 2
QT = -(-TILES // P)
RING = 14
WE = 3 * D
MANY = 9
ZROWS = 8
FILL = 3e38
EPS = 1e-5
NEG = -1e30
FLOOR = -1e20
TINY = 1e-30


def build(nc, A, out):
    with ExitStack() as ctx:
        def sb(name, shape, dt=F32):
            return ctx.enter_context(nc.sbuf_tensor(name, shape, dt))

        def ps(name, shape):
            return ctx.enter_context(nc.psum_tensor(name, shape, F32))

        def sem(name):
            return ctx.enter_context(nc.semaphore(name))

        x_all = sb("x_all", [P, NB, D])
        xT_all = sb("xT_all", [P, NB, DC, P])
        wqkv = sb("wqkv", [P, DC, 3 * D])
        wrq = sb("wrq", [P, DC, LD])
        wrkv = sb("wrkv", [P, DC, 2 * LD])
        wout = sb("wout", [P, DC, D])
        wrout = sb("wrout", [LD, D])
        wsg = sb("wsg", [P, DC, F])
        wsu = sb("wsu", [P, DC, F])
        wsd = sb("wsd", [F, D])
        gateT = sb("gateT", [P, DC, E])
        bqk = sb("bqk", [P, 2 * DC])
        bv = sb("bv", [P, D])
        brq = sb("brq", [LD, 1])
        brk = sb("brk", [LD, 1])
        brv = sb("brv", [P, LD])
        brout = sb("brout", [P, D])
        bout = sb("bout", [P, D])
        gl = sb("gl", [P, HD])
        gr = sb("gr", [P, HD])
        ident = sb("ident", [P, P])
        head_parity = sb("head_parity", [P, 2])
        rq_head = sb("rq_head", [LD, LH])
        mask_prev = sb("mask_prev", [P, P])
        no_past = sb("no_past", [P, BPS])
        mask = sb("mask", [P, 2, P])
        lat_wide = sb("lat_wide", [P, NLAT - LPB + NLAT])
        lat_mask = sb("lat_mask", [P, NLAT])
        eps = sb("eps", [P, 1])
        stats = sb("stats", [P, NB, 6])
        mean = sb("mean", [P, NB])
        mdif = sb("mdif", [P, NB])
        var = sb("var", [P, NB])
        std = sb("std", [P, NB])
        rstd = sb("rstd", [P, NB])
        xn_st = sb("xn_st", [P, 4, D])
        xTa = sb("xTa", [P, 2, DC, P])
        shared_mem = sb("shared_mem", [P, RING * WE])
        table = lambda n: shared_mem[:, n * NB * E:(n + 1) * NB * E].rearrange("p (t e) -> p t e", t=NB)
        scores_t, sc_t, ra_t, rb_t, sel_t = (table(n) for n in range(5))
        ring_gu = shared_mem[:, 0:RING * 2 * D].rearrange("p (r c n) -> p r c n", r=RING, c=DC)
        ring_d = shared_mem[:, RING * 2 * D:RING * WE].rearrange("p (r n) -> p r n", r=RING)
        rows_in = shared_mem[:, 0:2 * K * D].rearrange("p (j k d) -> p j k d", j=2, k=K)
        gbias = sb("gbias", [P, E])
        lower = sb("lower", [P, G, G])
        before = sb("before", [P, P])
        ones = sb("ones", [P, P])
        small = sb("small", [P, 4, NB * G])
        top8 = sb("top8", [P, NB, K])
        slot8 = sb("slot8", [P, NB, K])
        slot_idx = sb("slot_idx", [P, NB, K], U32)
        w8 = sb("w8", [P, NB, K])
        wsum = sb("wsum", [P, NB])
        wj = sb("wj", [P, 2, E])
        count_i = sb("count_i", [P, E], I32)
        per_e = sb("per_e", [P, 5, E])
        tile_no_i = sb("tile_no_i", [P, QT], I32)
        tile_no = sb("tile_no", [P, QT])
        tile_cmp = sb("tile_cmp", [P, QT, E])
        tile_e = sb("tile_e", [P, QT])
        tile_ei = sb("tile_ei", [P, QT], I32)
        expert_row = sb("expert_row", [1, QT * P], I32)
        pair_row = sb("pair_row", [1, QT * P // 2], I32)
        ends_row = sb("ends_row", [1, E], I32)
        x_out_st = sb("x_out_st", [P, 2, D])
        idx_st = sb("idx_st", [P, 2, K], U32)
        ex = scores_t
        xTs = sb("xTs", [P, 2, DC, P])
        qz = sb("qz", [P, 2, DC, 2, P])
        kT = sb("kT", [P, 2, DC, P])
        vz = sb("vz", [P, 2, H, 2 * HD])
        oT = sb("oT", [P, DC, P])
        rqz = sb("rqz", [LD, LH, P])
        pooledT = sb("pooledT", [P, DC, 2, NLAT])
        rkT = sb("rkT", [LD, NLAT])
        rv = sb("rv", [P, LH, LHD + 1])
        sm = sb("sm", [P, 4, 2, 2 * P])
        nmax = sb("nmax", [P, 4, 2])
        pr = sb("pr", [P, 4, 2, 2 * P])
        prT = sb("prT", [P, 2, 2, 2, P])
        lsm = sb("lsm", [P, LH, NLAT])
        lmax = sb("lmax", [P, LH])
        lneg = sb("lneg", [P, LH, NLAT])
        lpr = sb("lpr", [P, LH, NLAT])
        lprT = sb("lprT", [P, 2, P])
        lden = sb("lden", [P, LH])
        lrec = sb("lrec", [P, LH])
        lat = sb("lat", [P, P])
        latT = sb("latT", [LD, P])
        remote = sb("remote", [P, H, HD])
        den = sb("den", [P, 2, H])
        den1 = sb("den1", [P, H])
        met = sb("met", [1, 4])
        rec = sb("rec", [P, H])
        local = sb("local", [P, H, HD])
        zl = sb("zl", [P, H, HD])
        zr = sb("zr", [P, H, HD])
        zs = sb("zs", [P, H, HD])
        z = sb("z", [P, H])
        ez = sb("ez", [P, H])
        ez1 = sb("ez1", [P, H])
        gate = sb("gate", [P, H])
        dif = sb("dif", [P, H, HD])
        gate_rows = dif[0:E].rearrange("p h d -> p (h d)")
        gdif = sb("gdif", [P, H, HD])
        mixed = sb("mixed", [P, H, HD])
        zeros = pr[:].rearrange("p a b t -> p (a b t)")
        rc_t = sm[:].rearrange("p a b (t e) -> p (a b t) e", e=E)
        pr_mem, sm_mem = (x[:].rearrange("p a b t -> p (a b t)") for x in (pr, sm))
        xs = pr_mem[:, 0:XS * 2 * D].rearrange("p (j a d) -> p j a d", j=XS, a=2)
        ys = sm_mem[:, 0:YS * 2 * D].rearrange("p (j a d) -> p j a d", j=YS, a=2)
        xsT = sm_mem[:, YS * 2 * D:(YS + 2) * 2 * D].rearrange("p (j a c t) -> p j a c t", j=2, a=2, c=DC)
        sg, hh = (prT[:].rearrange("p a b c t -> p (a b c t)")[:, n * 4 * F:(n + 1) * 4 * F].rearrange("p (j a f) -> p j a f", j=2, a=2)
                  for n in range(2))
        hhT = sb("hhT", [P, 2, 2, P])
        mixedT = sb("mixedT", [P, DC, P])
        eg = sb("eg", [F, P])
        eg1 = sb("eg1", [F, P])
        sig = sb("sig", [F, P])
        gs = sb("gs", [F, P])
        hsT = sb("hsT", [F, 2, P])

        psQ = ps("psQ", [P, 512])
        psV = ps("psV", [P, 512])
        psS = ps("psS", [P, 2, 512])
        psT = ps("psT", [P, 2, 512])
        psM = ps("psM", [P, 512])
        psO = ps("psO", [P, 512])

        NX = 4
        x_in = [sem(f"x_in{n}") for n in range(NX)]
        w_in = sem("w_in")
        consts = sem("consts")
        pool_order = sem("pool_order")
        gw_turned = sem("gw_turned")
        gw_ready = sem("gw_ready")
        stats_done = sem("stats_done")
        mv_done = sem("mv_done")
        std_done = sem("std_done")
        rstd_done = sem("rstd_done")
        xn_staged = sem("xn_staged")
        xn_turned = sem("xn_turned")
        xTa_ready = sem("xTa_ready")
        logits = sem("logits")
        ex_ready = sem("ex_ready")
        xT_kept = sem("xT_kept")
        xn_out = [sem(f"xn_out{j}") for j in range(4)]
        x_biased = sem("x_biased")
        xT_staged = sem("xT_staged")
        masks_staged = sem("masks_staged")
        pool_sums = sem("pool_sums")
        gdif_ready = sem("gdif_ready")
        pooled = sem("pooled")
        qk_ready = sem("qk_ready")
        v_ready = sem("v_ready")
        sh_ready = sem("sh_ready")
        q_kept = sem("q_kept")
        k_kept = sem("k_kept")
        v_kept = sem("v_kept")
        rq_kept = sem("rq_kept")
        eg_ready = sem("eg_ready")
        sh_steps = sem("sh_steps")
        hs_ready = sem("hs_ready")
        s_ready = sem("s_ready")
        masked = sem("masked")
        probs = sem("probs")
        probs_turned = sem("probs_turned")
        prT_ready = sem("prT_ready")
        pv_pair = sem("pv_pair")
        o_kept = sem("o_kept")
        o_turned = sem("o_turned")
        lat_kv = sem("lat_kv")
        rk_kept = sem("rk_kept")
        lat_s = sem("lat_s")
        lat_steps = sem("lat_steps")
        lat_neg = sem("lat_neg")
        lat_p = sem("lat_p")
        lat_turned = sem("lat_turned")
        lprT_ready = sem("lprT_ready")
        lat_o = sem("lat_o")
        lat_kept = sem("lat_kept")
        lat_oT = sem("lat_oT")
        latT_ready = sem("latT_ready")
        remote_ready = sem("remote_ready")
        remote_kept = sem("remote_kept")
        mix_steps = sem("mix_steps")
        z_ready = sem("z_ready")
        ez_ready = sem("ez_ready")
        local_kept = sem("local_kept")
        mixed_ready = sem("mixed_ready")
        mixed_turned = sem("mixed_turned")
        mixedT_ready = sem("mixedT_ready")
        out_ready = sem("out_ready")
        acc_done = sem("acc_done")
        stored = sem("stored")
        blocks_staged = sem("blocks_staged")
        cleared = sem("cleared")
        zeros_ready = sem("zeros_ready")
        route_steps = sem("route_steps")
        sel_ready = sem("sel_ready")
        ranks_ready = sem("ranks_ready")
        slots_ready = sem("slots_ready")
        tiles_ready = sem("tiles_ready")
        experts_known = sem("experts_known")
        words_ready = sem("words_ready")
        routed = sem("routed")
        scatter_in = [sem(f"scatter_in{j}") for j in range(2)]
        scattered = [sem(f"scattered{j}") for j in range(2)]
        weights_in = [sem(f"weights_in{j}") for j in range(2)]
        experts_ready = sem("experts_ready")
        pairs_done = sem("pairs_done")
        xs_in = [sem(f"xs_in{j}") for j in range(XS)]
        xs_turned = sem("xs_turned")
        xsT_ready = sem("xsT_ready")
        gu_ready = sem("gu_ready")
        silu_ready = sem("silu_ready")
        h_ready = sem("h_ready")
        h_turned = sem("h_turned")
        hT_ready = sem("hT_ready")
        y_ready = sem("y_ready")
        y_kept = sem("y_kept")
        y_out = [sem(f"y_out{j}") for j in range(YS)]
        idx_in = [sem(f"idx_in{j}") for j in range(2)]
        rows_ready = [sem(f"rows_ready{j}") for j in range(2)]
        combine_steps = sem("combine_steps")
        combined = sem("combined")
        slot_rows = nc.dram_tensor("slot_rows", (SLOTS, D), F32, kind="Internal").ap()
        slot_outs = nc.dram_tensor("slot_outs", (SLOTS, D), F32, kind="Internal").ap()
        xn_tiles = nc.dram_tensor("xn_tiles", (NB, P, D), F32, kind="Internal").ap()
        slot_pairs = slot_rows.rearrange("(u a p) d -> u p a d", a=2, p=P)
        out_pairs = slot_outs.rearrange("(u a p) d -> u p a d", a=2, p=P)

        xt = A["L0_attn_x"].rearrange("b (t p) d -> p (b t) d", p=P)
        yt = out.rearrange("b (t p) d -> p (b t) d", p=P)
        rows = lambda w: w.rearrange("(c p) n -> p c n", p=P)
        col = lambda b, n: b.rearrange("(c p) -> p c", p=n)
        W_ALL = 16 * 19
        block = ctx.enter_context(nc.Block())

        @block.sync
        def _(sp):
            for n in range(NX):
                t = slice(n * NB // NX, (n + 1) * NB // NX)
                sp.dma_start(x_all[:, t, :], xt[:, t, :]).then_inc(x_in[n], 16)
            spread = lambda v: v.partition_broadcast(P)
            with nc.allow_non_contiguous_dma("biases, one value a partition"):
                for dst, src in (
                    (gate_rows, A["L0_ffn_gate_w"]),
                    (wqkv[:], rows(A["L0_attn_qkv_w"])),
                    (wrq[:], rows(A["L0_attn_rq_w"])),
                    (wrkv[:], rows(A["L0_attn_rkv_w"])),
                    (wout[:], rows(A["L0_attn_out_w"])),
                    (wrout[:], A["L0_attn_rout_w"]),
                    (wsg[:], rows(A["L0_ffn_Ws_gate"])),
                    (wsu[:], rows(A["L0_ffn_Ws_up"])),
                    (wsd[:], A["L0_ffn_Ws_down"]),
                    (bqk[:], col(A["L0_attn_qkv_b"][0:2 * D], P)),
                    (bv[:], spread(A["L0_attn_qkv_b"][2 * D:3 * D])),
                    (brq[:], col(A["L0_attn_rq_b"], LD)),
                    (brk[:], col(A["L0_attn_rkv_b"][0:LD], LD)),
                    (brv[:], spread(A["L0_attn_rkv_b"][LD:2 * LD])),
                    (brout[:], spread(A["L0_attn_rout_b"])),
                    (bout[:], spread(A["L0_attn_out_b"])),
                    (gl[:], spread(A["L0_attn_gl_w"].rearrange("d a -> (d a)"))),
                    (gr[:], spread(A["L0_attn_gr_w"].rearrange("d a -> (d a)"))),
                    (gbias[:], spread(A["L0_ffn_gate_bias"])),
                ):
                    sp.dma_start(dst, src).then_inc(w_in, 16)
            def store_xn(j, i):
                sp.wait_ge(xn_staged, i + 1)
                sp.dma_start(xn_tiles[i], xn_st[:, j, :]).then_inc(xn_out[j], 16)

            with sp.Fori(0, NB // 4) as g:
                for j in range(4):
                    store_xn(j, g * 4 + j)
            sp.wait_ge(zeros_ready, 1)
            clear = slot_rows.rearrange("(n p r) d -> n p (r d)", p=P, r=ZROWS)
            with sp.Fori(0, SLOTS // (P * ZROWS)) as n:
                sp.dma_start(clear[n], zeros).then_inc(cleared, 16)
            sp.wait_ge(tiles_ready, 1)
            with nc.allow_non_contiguous_dma("a column to a row"):
                for q in range(QT):
                    sp.dma_start(expert_row[0:1, q * P:(q + 1) * P], tile_ei[:, q:q + 1]).then_inc(experts_known, 16)

            def stage_scatter(j, i, first):
                if not first:
                    sp.wait_ge(scattered[j], 16 * K * i)
                sp.dma_start(x_out_st[:, j, :], xn_tiles[2 * i + j]).then_inc(scatter_in[j], 16)
                sp.dma_start(idx_st[:, j, :], slot_idx[:, 2 * i + j, :]).then_inc(scatter_in[j], 16)

            sp.wait_ge(slots_ready, 1)
            for j in range(4):
                sp.wait_ge(xn_out[j], 16 * (NB // 4))
            for j in range(2):
                stage_scatter(j, 0, True)
            with sp.Fori(1, NB // 2) as g:
                for j in range(2):
                    stage_scatter(j, g, False)
            for j in range(2):
                sp.wait_ge(scattered[j], 16 * K * NB // 2)

            sp.wait_ge(probs_turned, HALF * NPAIR)
            sp.wait_ge(masked, 2 * HALF * NPAIR)
            sp.wait_ge(probs, 2 * HALF * NPAIR)

            def load_pair(j, g, first):
                u = g * XS + j
                if not first:
                    sp.wait_ge(xs_turned, u - XS + 1)
                sp.dma_start(xs[:, j, :, :], slot_pairs[u]).then_inc(xs_in[j], 16)

            def store_pair(j, u):
                sp.wait_ge(y_kept, u + 1)
                sp.dma_start(out_pairs[u], ys[:, j % YS, :, :]).then_inc(y_out[j % YS], 16)

            for j in range(XS):
                load_pair(j, 0, True)
            with sp.Fori(1, PAIRS // XS) as g:
                for j in range(XS):
                    load_pair(j, g, False)
                    store_pair(j, (g - 1) * XS + j)
            for j in range(XS):
                store_pair(j, PAIRS - XS + j)
            for j in range(YS):
                sp.wait_ge(y_out[j], 16 * (PAIRS // YS))

            def stage_gather(j, i, first):
                if not first:
                    sp.wait_ge(rows_ready[j], 16 * K * i)
                sp.dma_start(idx_st[:, j, :], slot_idx[:, 2 * i + j, :]).then_inc(idx_in[j], 16)

            def store_block(i):
                sp.wait_ge(combined, i + 1)
                sp.wait_ge(acc_done, i + 1)
                sp.dma_start(yt[:, i, :], x_all[:, i, :]).then_inc(stored, 16)

            for j in range(2):
                stage_gather(j, 0, True)
            with sp.Fori(1, NB // 2) as g:
                for j in range(2):
                    stage_gather(j, g, False)
                    store_block(2 * g + j - 2)
            for j in range(2):
                store_block(NB - 2 + j)
            sp.wait_ge(stored, 16 * NB)

        @block.gpsimd
        def _(pool):
            steps = 0

            def after(ins):
                nonlocal steps
                steps += 1
                ins.then_inc(pool_order, 1)
                pool.wait_ge(pool_order, steps)

            def fill(v, value, tests):
                for pattern, base, mult, op in tests:
                    after(nc.gpsimd.affine_select(out=v, in_=v, compare_op=op, fill=value, base=base,
                                                  pattern=pattern, channel_multiplier=mult))

            nc.gpsimd.memset(zeros, 0.0).then_inc(zeros_ready, 1)
            after(nc.gpsimd.memset(ident[:], 0.0))
            after(nc.gpsimd.memset(ones[:], 1.0))
            after(nc.gpsimd.memset(before[:], 1.0))
            fill(before[:], 0.0, [([[1, P]], -1, -1, ALU.is_ge)])
            after(nc.gpsimd.memset(lower[:], 1.0))
            fill(lower[:], 0.0, [([[1, G], [-1, G]], -1, 0, ALU.is_ge)])
            after(nc.gpsimd.iota(tile_no_i[:], pattern=[[P, QT]], base=0, channel_multiplier=1))
            after(nc.gpsimd.tensor_copy(tile_no[:], tile_no_i[:]))
            fill(ident[:], 1.0, [([[-1, P]], 0, 1, ALU.not_equal)])
            after(nc.gpsimd.memset(eps[:], EPS))
            after(nc.gpsimd.memset(head_parity[:], 0.0))
            for par in range(2):
                for n in range(HPC // 2):
                    lo = (2 * n + par) * HD
                    v = head_parity[:, par:par + 1]
                    t = gate[:, 0:1]
                    after(nc.gpsimd.memset(t, HD ** -0.5))
                    fill(t, 0.0, [([[0, 1]], -lo, 1, ALU.is_ge), ([[0, 1]], lo + HD - 1, -1, ALU.is_ge)])
                    after(nc.gpsimd.tensor_tensor(v, v, t, ALU.add))
            after(nc.gpsimd.memset(rq_head[:], LHD ** -0.5))
            fill(rq_head[:], 0.0, [([[-LHD, LH]], 0, 1, ALU.is_ge), ([[LHD, LH]], LHD - 1, -1, ALU.is_ge)])
            after(nc.gpsimd.memset(mask_prev[:], 0.0))
            fill(mask_prev[:], NEG, [([[1, P]], 0, -1, ALU.is_ge), ([[1, P]], -1, 0, ALU.is_ge)])
            after(nc.gpsimd.memset(no_past[:], 0.0))
            after(nc.gpsimd.memset(no_past[:, 0:1], NEG))
            after(nc.gpsimd.memset(mask[:], 0.0))
            fill(mask[:, 1, :], NEG, [([[-1, P]], -1, 1, ALU.is_ge)])
            after(nc.gpsimd.memset(lat_wide[:], 0.0))
            fill(lat_wide[:], NEG, [([[-CH, 2 * NLAT - LPB]], CH * (NLAT - LPB) - CH, 1, ALU.is_ge)])
            after(nc.gpsimd.memset(vz[:], 0.0))
            after(nc.gpsimd.memset(kT[:, 1, :, :], 0.0))
            after(nc.gpsimd.memset(rv[:], 0.0))
            for par in range(2):
                after(nc.gpsimd.memset(rv[par * NLAT:(par + 1) * NLAT, par::2, LHD:LHD + 1], 1.0))
            after(nc.gpsimd.memset(lat[:], 0.0))
            nc.gpsimd.memset(pooledT[:], 0.0).then_inc(consts, 1)
            pool.wait_ge(w_in, W_ALL)
            with pool.Fori(0, NB // 2) as g:
                for j in range(2):
                    i = g * 2 + j
                    pool.wait_ge(xn_staged, i + 1)
                    pool.wait_ge(consts, 1)
                    nc.gpsimd.tensor_tensor(x_all[:, i, :], x_all[:, i, :], bout[:], ALU.add).then_inc(x_biased, 1)
                    pool.wait_ge(xTa_ready, i + 1)
                    pool.wait_ge(consts, 1)
                    nc.gpsimd.tensor_copy(xT_all[:, i, :, :], xTa[:, j, :, :]).then_inc(xT_kept, 1)

            def scatter(j, g):
                pool.wait_ge(scatter_in[j], 32 * (g + 1))
                pool.sem_inc(blocks_staged, 1)
                for k in range(K):
                    pool.indirect_dma_start(slot_rows, bass.IndirectOffsetOnAxis(ap=idx_st[:, j, k:k + 1], axis=0),
                                            x_out_st[:, j, :], None).then_inc(scattered[j], 16)

            pool.wait_ge(cleared, 16 * (SLOTS // (P * ZROWS)))
            with pool.Fori(0, NB // 2) as g:
                for j in range(2):
                    scatter(j, g)

            def load_expert(j, e, first):
                if not first:
                    end = pool.value_load(ends_row[0:1, bass.ds(e - RING, 1)], min_val=1, max_val=PAIRS + 1)
                    pool.wait_ge(pairs_done, end)
                r = e % RING
                pool.dma_start(ring_gu[:, r, :, 0:F], rows(A["L0_ffn_We_gate"][e])).then_inc(weights_in[j], 16)
                pool.dma_start(ring_gu[:, r, :, F:2 * F], rows(A["L0_ffn_We_up"][e])).then_inc(weights_in[j], 16)
                pool.dma_start(ring_d[:, r, :], A["L0_ffn_We_down"][e]).then_inc(weights_in[j], 16)

            def announce(j, g):
                pool.wait_ge(weights_in[j], 48 * (g + 1))
                pool.sem_inc(experts_ready, 1)

            pool.wait_ge(routed, 1)
            load_expert(0, 0, True)
            load_expert(1, 1, True)
            with pool.Fori(1, RING // 2) as g:
                for j in range(2):
                    announce(j, g - 1)
                    load_expert(j, 2 * g + j, True)
            with pool.Fori(RING // 2, E // 2) as g:
                for j in range(2):
                    announce(j, g - 1)
                    load_expert(j, 2 * g + j, False)
            for j in range(2):
                announce(j, E // 2 - 1)

            def gather(j, g, first):
                pool.wait_ge(idx_in[j], 16 * (g + 1))
                if not first:
                    pool.wait_ge(combined, 2 * g + j - 1)
                pool.sem_inc(blocks_staged, 1)
                for k in range(K):
                    pool.indirect_dma_start(rows_in[:, j, k, :], None, slot_outs,
                                            bass.IndirectOffsetOnAxis(ap=idx_st[:, j, k:k + 1], axis=0)
                                            ).then_inc(rows_ready[j], 16)

            for j in range(YS):
                pool.wait_ge(y_out[j], 16 * (PAIRS // YS))
            for j in range(2):
                gather(j, 0, True)
            with pool.Fori(1, NB // 2) as g:
                for j in range(2):
                    gather(j, g, False)

        @block.tensor
        def _(pe):
            mm = nc.tensor.matmul

            pe.wait_ge(w_in, W_ALL)
            pe.wait_ge(consts, 1)
            for c in range(DC):
                last = nc.tensor.transpose(psM[:, c * E:(c + 1) * E], gate_rows[:, c * P:(c + 1) * P], ident[0:E, 0:E])
            last.then_inc(gw_turned, 1)

            def turn_x(j, i, first):
                pe.wait_ge(xn_staged, i + 1)
                if not first:
                    pe.wait_ge(xTa_ready, i - 1)
                for c in range(DC):
                    last = nc.tensor.transpose(psT[:, j % 2, c * P:(c + 1) * P], xn_st[:, j, c * P:(c + 1) * P], ident[:])
                last.then_inc(xn_turned, 1)

            def route(j, i, first):
                pe.wait_ge(xTa_ready, i + 1)
                if not first:
                    pe.wait_ge(ex_ready, i - 1)
                for c in range(DC):
                    last = mm(psS[:, j % 2, 0:E], xTa[:, j % 2, c, :], gateT[:, c, :], start=(c == 0), stop=(c == DC - 1))
                last.then_inc(logits, 1)

            pe.wait_ge(gw_ready, 1)
            for j in range(4):
                turn_x(j, j, j < 2)
                route(j, j, j < 2)
            with pe.Fori(1, NB // 4) as g:
                for j in range(4):
                    turn_x(j, g * 4 + j, False)
                    route(j, g * 4 + j, False)

            pe.wait_ge(sel_ready, 1)
            sel_flat = sel_t.rearrange("p t e -> p (t e)")
            for n in range(4):
                mm((psS[:, n, :] if n < 2 else psT[:, n - 2, :]), before[:], sel_flat[:, n * 512:(n + 1) * 512], start=True, stop=True)
            for n, bank in enumerate((psQ, psV, psM, psO)):
                last = mm(bank[:], ones[:], sel_flat[:, n * 512:(n + 1) * 512], start=True, stop=True)
            last.then_inc(ranks_ready, 1)
            pe.wait_ge(routed, 1)

            def project_qk(j, i, nth):
                pe.wait_ge(xT_staged, i + 1)
                if nth:
                    pe.wait_ge(hs_ready, i)
                for m in range(2 * DC):
                    for c in range(DC):
                        last = mm(psQ[:, m * P:(m + 1) * P], wqkv[:, c, m * P:(m + 1) * P], xTs[:, j, c, :],
                                  start=(c == 0), stop=(c == DC - 1))
                last.then_inc(qk_ready, 1)

            def project_v(j, i, nth):
                if nth > 1:
                    pe.wait_ge(acc_done, i - 1)
                if nth:
                    pe.wait_ge(v_kept, DC * i)
                    pe.wait_ge(rq_kept, i)
                for c in range(DC):
                    mm(psV[:, 0:D], xTs[:, j, c, :], wqkv[:, c, 2 * D:3 * D], start=(c == 0), stop=(c == DC - 1))
                for c in range(DC):
                    last = mm(psV[0:LD, D:D + P], wrq[:, c, :], xTs[:, j, c, :], start=(c == 0), stop=(c == DC - 1))
                last.then_inc(v_ready, 1)

            def shared(j, i):
                pe.wait_ge(q_kept, i + 1)
                pe.wait_ge(k_kept, DC * (i + 1))
                for n, w in enumerate((wsg, wsu)):
                    for c in range(DC):
                        last = mm(psQ[:, n * P:(n + 1) * P], w[:, c, :], xTs[:, j, c, :], start=(c == 0), stop=(c == DC - 1))
                last.then_inc(sh_ready, 1)

            def turn_o(i, live):
                pe.wait_ge(o_kept, i + 1)
                if live:
                    pe.wait_ge(v_kept, DC * (i + 2))
                    pe.wait_ge(rq_kept, i + 2)
                else:
                    pe.wait_ge(acc_done, i)
                for c in range(DC):
                    last = nc.tensor.transpose(psV[:, c * P:(c + 1) * P], oT[:, c, :], ident[:])
                last.then_inc(o_turned, 1)

            def turn_mixed(i):
                pe.wait_ge(mixed_ready, i + 1)
                for c in range(DC):
                    last = nc.tensor.transpose(psV[:, c * P:(c + 1) * P],
                                               mixed[:].rearrange("p h d -> p (h d)")[:, c * P:(c + 1) * P], ident[:])
                last.then_inc(mixed_turned, 1)

            def out_project(j, i):
                pe.wait_ge(mixedT_ready, i + 1)
                pe.wait_ge(hs_ready, i + 1)
                for c in range(DC):
                    mm(psV[:, D:2 * D], mixedT[:, c, :], wout[:, c, :], start=(c == 0), stop=False)
                mm(psV[:, D:2 * D], hsT[:, j, :], wsd[:], start=False, stop=True).then_inc(out_ready, 1)

            def scores(j, i, p, nth):
                n = i * NPAIR + p
                c, r = p // PPC, (p % PPC) * 2 * HD
                if p == 0:
                    pe.wait_ge(q_kept, i + 1)
                if p % PPC == 0:
                    pe.wait_ge(k_kept, DC * i + c + 1)
                if p >= 2 or nth:
                    pe.wait_ge(masked, 2 * (n - 1))
                for par in range(2):
                    for half in range(2):
                        last = mm(psS[:, p % 2, (2 * par + half) * P:(2 * par + half + 1) * P],
                                  qz[r:r + 2 * HD, j, c, par, :], kT[r:r + 2 * HD, (j + 1 + half) % 2, c, :],
                                  start=True, stop=True)
                last.then_inc(s_ready, 1)

            def turn_probs(i, p, nth):
                n = i * NPAIR + p
                pe.wait_ge(probs, 2 * n + 2)
                if p >= 2 or nth:
                    pe.wait_ge(prT_ready, n - 1)
                for par in range(2):
                    for half in range(2):
                        last = nc.tensor.transpose(psT[:, p % 2, (2 * par + half) * P:(2 * par + half + 1) * P],
                                                   pr[:, p % 4, par, half * P:(half + 1) * P], ident[:])
                last.then_inc(probs_turned, 1)

            def values(j, i, p, nth):
                n = i * NPAIR + p
                c, r = p // PPC, (p % PPC) * 2 * HD
                pe.wait_ge(prT_ready, n + 1)
                if p % PPC == 0:
                    pe.wait_ge(v_kept, DC * i + c + 1)
                if p == 0 and nth:
                    pe.wait_ge(o_kept, i)
                for par in range(2):
                    for half in range(2):
                        last = mm(psO[r:r + 2 * HD, c * P:(c + 1) * P], vz[:, (j + 1 + half) % 2, 2 * p + par, :],
                                  prT[:, p % 2, par, half, :], start=(par == 0 and half == 0), stop=(par == 1 and half == 1))
                last.then_inc(pv_pair, 1)

            def latent_kv(i, nth):
                pe.wait_ge(pooled, i + 1)
                if nth:
                    pe.wait_ge(remote_kept, i)
                for c in range(DC):
                    mm(psM[0:LD, 0:NLAT], wrkv[:, c, 0:LD], pooledT[:, c, 0, :], start=(c == 0), stop=(c == DC - 1))
                for c in range(DC):
                    last = mm(psM[:, NLAT:NLAT + LD], pooledT[:, c, :, :].rearrange("p a n -> p (a n)"), wrkv[:, c, LD:2 * LD],
                              start=(c == 0), stop=(c == DC - 1))
                last.then_inc(lat_kv, 1)

            def latent_scores(i):
                pe.wait_ge(rk_kept, 3 * i + 3)
                pe.wait_ge(rq_kept, i + 1)
                for h in range(LH):
                    last = mm(psM[:, h * NLAT:(h + 1) * NLAT], rqz[:, h, :], rkT[:], start=True, stop=True)
                last.then_inc(lat_s, 1)

            def latent_turn(i):
                pe.wait_ge(lat_p, i + 1)
                flat = lpr[:].rearrange("p h n -> p (h n)")
                for n in range(2):
                    last = nc.tensor.transpose(psM[:, n * P:(n + 1) * P], flat[:, n * P:(n + 1) * P], ident[:])
                last.then_inc(lat_turned, 1)

            def latent_values(i):
                pe.wait_ge(lprT_ready, i + 1)
                for n in range(LH // 2):
                    last = mm(psM[:, 2 * n * (LHD + 1):2 * (n + 1) * (LHD + 1)], lprT[:, n, :],
                              rv[:, 2 * n:2 * n + 2, :].rearrange("p h d -> p (h d)"), start=True, stop=True)
                last.then_inc(lat_o, 1)

            def latent_out_turn(i):
                pe.wait_ge(lat_kept, i + 1)
                nc.tensor.transpose(psM[:, 0:P], lat[:], ident[:]).then_inc(lat_oT, 1)

            def latent_project(i):
                pe.wait_ge(latT_ready, i + 1)
                mm(psM[:, D:2 * D], latT[:], wrout[:], start=True, stop=True).then_inc(remote_ready, 1)

            def body(j, i, nth, live=True, tail=True, ahead=True):
                for s in range(NPAIR):
                    if live:
                        scores(j, i, s, nth)
                    if s < 2 and tail:
                        turn_probs(i - 1, s + NPAIR - 2, nth - 1)
                    if s >= 2 and live:
                        turn_probs(i, s - 2, nth)
                    if s == 0 and tail:
                        latent_out_turn(i - 1)
                    if s == 0 and live:
                        project_v(j, i, nth)
                    if s == 1 and tail:
                        latent_project(i - 1)
                    if s == 2 and live:
                        shared(j, i)
                    if s == 3 and live:
                        latent_kv(i, nth)
                    if s < 3 and tail:
                        values(1 - j, i - 1, s + NPAIR - 3, nth - 1)
                    if s >= 3 and live:
                        values(j, i, s - 3, nth)
                    if s == 3 and tail:
                        turn_o(i - 1, live)
                    if s == 4 and live:
                        latent_scores(i)
                    if s == 5 and live and ahead:
                        project_qk(1 - j, i + 1, 2)
                    if s == 6 and live:
                        latent_turn(i)
                    if s == 6 and tail:
                        turn_mixed(i - 1)
                    if s == 7 and live:
                        latent_values(i)
                    if s == 7 and tail:
                        out_project(1 - j, i - 1)

            def attention(start):
                nth = min(start, 2)
                project_qk(0, start, nth)
                body(0, start, nth, tail=False)
                body(1, start + 1, max(nth, 1))
                with pe.Fori(start // 2 + 1, (start + HALF) // 2 - 1) as g:
                    for j in range(2):
                        body(j, g * 2 + j, 2)
                body(0, start + HALF - 2, 2)
                body(1, start + HALF - 1, 2, ahead=False)
                body(0, start + HALF, 2, live=False)

            def turn_tiles(j, u, turn, first):
                pe.wait_ge(xs_in[j], 16 * (turn + 1))
                if not first:
                    pe.wait_ge(xsT_ready, u - 1)
                for a in range(2):
                    for c in range(DC):
                        last = nc.tensor.transpose(psT[:, j % 2, (a * DC + c) * P:(a * DC + c + 1) * P],
                                                   xs[:, j, a, c * P:(c + 1) * P], ident[:])
                last.then_inc(xs_turned, 1)

            def experts_of(u):
                word = pe.value_load(pair_row[0:1, bass.ds(u, 1)], min_val=0, max_val=E * E - 1)
                return word % E, word // E

            def gate_up(j, u, experts, first):
                if not first:
                    pe.wait_ge(h_ready, u - 1)
                pe.wait_ge(xsT_ready, u + 1)
                pe.wait_ge(experts_ready, experts[1] + 1)
                for a, e in enumerate(experts):
                    for c in range(DC):
                        last = mm(psS[:, j % 2, a * 2 * F:(a + 1) * 2 * F], xsT[:, j % 2, a, c, :], ring_gu[:, e % RING, c, :],
                                  start=(c == 0), stop=(c == DC - 1))
                last.then_inc(gu_ready, 1)

            def turn_h(j, u, first):
                pe.wait_ge(h_ready, u + 1)
                if not first:
                    pe.wait_ge(hT_ready, u - 1)
                for a in range(2):
                    last = nc.tensor.transpose((psQ, psV)[j % 2][:, a * P:(a + 1) * P], hh[:, j % 2, a, :], ident[:])
                last.then_inc(h_turned, 1)

            def down(j, u, experts, first):
                pe.wait_ge(hT_ready, u + 1)
                if not first:
                    pe.wait_ge(y_kept, u - 1)
                for a, e in enumerate(experts):
                    last = mm((psM, psO)[j % 2][:, a * D:(a + 1) * D], hhT[:, j % 2, a, :], ring_d[:, e % RING, :],
                              start=True, stop=True)
                last.then_inc(pairs_done, 1)

            def round_of(g, nth, final):
                u = g * XS
                before = experts_of(u - 1) if nth > 0 else None
                now = experts_of(u)
                for j in range(XS):
                    gate_up(j, u + j, now, nth + j < 2)
                    after = experts_of(u + j + 1) if j < XS - 1 else None
                    if not (final and j == XS - 1):
                        turn_tiles((j + 1) % XS, u + j + 1, g + (j + 1) // XS, nth + j == 0)
                    if nth + j > 0:
                        down((j - 1) % XS, u + j - 1, before, nth + j <= 2)
                    turn_h(j, u + j, nth + j < 2)
                    before, now = now, after
                return before

            def experts():
                turn_tiles(0, 0, 0, True)
                round_of(0, 0, False)
                with pe.Fori(1, PAIRS // XS - 1) as g:
                    round_of(g, MANY, False)
                last = round_of(PAIRS // XS - 1, MANY, True)
                down(XS - 1, PAIRS - 1, last, False)

            pe.wait_ge(xT_kept, NB)
            attention(0)
            pe.wait_ge(words_ready, 1)
            pe.wait_ge(acc_done, HALF)
            pe.sem_inc(pairs_done, 1)
            experts()
            pe.wait_ge(y_kept, PAIRS)
            attention(HALF)

        @block.scalar
        def _(act):
            act.wait_ge(gw_turned, 1)
            nc.scalar.copy(gateT[:].rearrange("p c e -> p (c e)"), psM[:, 0:DC * E]).then_inc(gw_ready, 1)
            act.wait_ge(mv_done, 7)
            nc.scalar.activation(std[:], var[:], ACT.Sqrt, bias=eps[:]).then_inc(std_done, 1)

            def keep_xT(j, i, first):
                act.wait_ge(xn_turned, i + 1)
                if not first:
                    act.wait_ge(xT_kept, i - 1)
                    act.wait_ge(logits, i - 1)
                nc.scalar.copy(xTa[:, j, :, :].rearrange("p c t -> p (c t)"), psT[:, j, 0:D]).then_inc(xTa_ready, 1)
                act.wait_ge(logits, i + 1)
                nc.scalar.activation(ex[:, i, :], psS[:, j, 0:E], ACT.Exp, scale=-1.0).then_inc(ex_ready, 1)

            for j in range(2):
                keep_xT(j, j, True)
            with act.Fori(1, NB // 2) as g:
                for j in range(2):
                    keep_xT(j, g * 2 + j, False)

            def keep_k(j, i, c, nth):
                act.wait_ge(qk_ready, i + 1)
                if c > 0:
                    act.wait_ge(q_kept, i + 1)
                if nth:
                    act.wait_ge(s_ready, NPAIR * (i - 1) + PPC * (c + 1))
                act.wait_ge(consts, 1)
                nc.scalar.activation(kT[:, j, c, :], psQ[:, (DC + c) * P:(DC + c + 1) * P], ACT.Identity,
                                     bias=bqk[:, DC + c:DC + c + 1]).then_inc(k_kept, 1)

            def keep_oT(i, nth):
                act.wait_ge(pv_pair, NPAIR * (i + 1))
                if nth:
                    act.wait_ge(o_turned, i)
                nc.scalar.copy(oT[:].rearrange("p c t -> p (c t)"), psO[:, 0:D]).then_inc(o_kept, 1)

            def gate_exp(i):
                act.wait_ge(z_ready, i + 1)
                nc.scalar.activation(ez[:], z[:], ACT.Exp, scale=-1.0).then_inc(ez_ready, 1)

            def keep_mixedT(i, nth):
                act.wait_ge(mixed_turned, i + 1)
                if nth:
                    act.wait_ge(out_ready, i)
                nc.scalar.copy(mixedT[:].rearrange("p c t -> p (c t)"), psV[:, 0:D]).then_inc(mixedT_ready, 1)

            def shared_exp(i, nth):
                act.wait_ge(sh_ready, i + 1)
                if nth:
                    act.wait_ge(hs_ready, i)
                nc.scalar.activation(eg[:], psQ[:, 0:P], ACT.Exp, scale=-1.0).then_inc(eg_ready, 1)

            act.wait_ge(cleared, 16 * (SLOTS // (P * ZROWS)))
            act.wait_ge(routed, 1)

            def exps(j, i, p, nth):
                n = i * NPAIR + p
                if p >= 4 or nth:
                    act.wait_ge(probs_turned, n - 3)
                if p == 0 and nth > 1:
                    act.wait_ge(local_kept, i - 1)
                for par in range(2):
                    act.wait_ge(masked, 2 * n + par + 1)
                    nc.scalar.activation(pr[:, p % 4, par, :], sm[:, p % 4, par, :], ACT.Exp,
                                         bias=nmax[:, p % 4, par:par + 1], scale=-1.0,
                                         accum_out=den[:, j, 2 * p + par:2 * p + par + 1]).then_inc(probs, 1)

            def keep_prT(i, p, nth):
                n = i * NPAIR + p
                act.wait_ge(probs_turned, n + 1)
                if p >= 2 or nth:
                    act.wait_ge(pv_pair, n - 1)
                nc.scalar.copy(prT[:, p % 2].rearrange("p a b t -> p (a b t)"), psT[:, p % 2, :]).then_inc(prT_ready, 1)

            def latent_exp(i, nth):
                act.wait_ge(lat_neg, i + 1)
                if nth:
                    act.wait_ge(lat_turned, i)
                nc.scalar.activation(lpr[:], lneg[:], ACT.Exp, scale=-1.0).then_inc(lat_p, 1)

            def keep_lprT(i):
                act.wait_ge(lat_turned, i + 1)
                nc.scalar.copy(lprT[:].rearrange("p a t -> p (a t)"), psM[:, 0:2 * P]).then_inc(lprT_ready, 1)

            def keep_latT(i):
                act.wait_ge(lat_oT, i + 1)
                nc.scalar.copy(latT[:], psM[0:LD, 0:P]).then_inc(latT_ready, 1)

            def body(j, i, nth, live=True, tail=True, ahead=True):
                for s in range(NPAIR):
                    if s == 0 and live:
                        keep_k(j, i, 1, nth)
                    if s == 1 and tail:
                        keep_latT(i - 1)
                    if s == 3 and tail:
                        keep_oT(i - 1, nth - 1)
                    if s == 7 and live:
                        keep_lprT(i)
                    if live:
                        exps(j, i, s, nth)
                    if s == 5 and tail:
                        gate_exp(i - 1)
                    if s == 6 and live:
                        latent_exp(i, nth)
                    if s == 7 and tail:
                        keep_mixedT(i - 1, nth - 1)
                    if s < 2 and tail:
                        keep_prT(i - 1, s + NPAIR - 2, nth - 1)
                    if s >= 2 and live:
                        keep_prT(i, s - 2, nth)
                    if s == 2 and live:
                        shared_exp(i, nth)
                    if s == 6 and live and ahead:
                        keep_k(1 - j, i + 1, 0, 2)

            def attention(start):
                nth = min(start, 2)
                keep_k(0, start, 0, nth)
                body(0, start, nth, tail=False)
                body(1, start + 1, max(nth, 1))
                with act.Fori(start // 2 + 1, (start + HALF) // 2 - 1) as g:
                    for j in range(2):
                        body(j, g * 2 + j, 2)
                body(0, start + HALF - 2, 2)
                body(1, start + HALF - 1, 2, ahead=False)
                body(0, start + HALF, 2, live=False)

            def keep_tiles(j, u, first):
                act.wait_ge(xs_turned, u + 1)
                if not first:
                    act.wait_ge(gu_ready, u - 1)
                nc.scalar.copy(xsT[:, j % 2].rearrange("p a c t -> p (a c t)"), psT[:, j % 2, :]).then_inc(xsT_ready, 1)

            def silu(j, u, first):
                act.wait_ge(gu_ready, u + 1)
                if not first:
                    act.wait_ge(h_ready, u - 1)
                nc.scalar.activation(sg[:, j % 2, :, :], psS[:, j % 2, :].rearrange("p (a n) -> p a n", a=2)[:, :, 0:F],
                                     ACT.Silu).then_inc(silu_ready, 1)

            def step(j, g, nth, final):
                u = g * XS + j
                silu(j, u, nth < 2)
                if not final:
                    keep_tiles((j + 1) % XS, u + 1, nth == 0)

            def experts():
                keep_tiles(0, 0, True)
                for j in range(XS):
                    step(j, 0, j, False)
                with act.Fori(1, PAIRS // XS - 1) as g:
                    for j in range(XS):
                        step(j, g, MANY, False)
                for j in range(XS):
                    step(j, PAIRS // XS - 1, MANY, j == XS - 1)

            attention(0)
            act.wait_ge(masked, 2 * HALF * NPAIR)
            act.wait_ge(pv_pair, HALF * NPAIR)
            experts()
            act.wait_ge(xs_turned, PAIRS)
            act.wait_ge(h_turned, PAIRS)
            attention(HALF)

        @block.vector
        def _(dve):
            v = nc.vector
            per = NB // NX
            for n in range(NX):
                dve.wait_ge(x_in[n], 16)
                with dve.Fori(n * per, (n + 1) * per) as i:
                    v.bn_stats(stats[:, i, :], x_all[:, i, :]).then_inc(stats_done, 1)
            dve.wait_ge(stats_done, NB)
            v.tensor_tensor(mean[:], stats[:, :, 1], stats[:, :, 4], ALU.add).then_inc(mv_done, 1)
            v.tensor_tensor(mdif[:], stats[:, :, 1], stats[:, :, 4], ALU.subtract).then_inc(mv_done, 1)
            v.tensor_tensor(var[:], stats[:, :, 2], stats[:, :, 5], ALU.add).then_inc(mv_done, 1)
            dve.wait_ge(mv_done, 3)
            v.tensor_scalar(mean[:], mean[:], 0.5, None, ALU.mult).then_inc(mv_done, 1)
            v.tensor_tensor(mdif[:], mdif[:], mdif[:], ALU.mult).then_inc(mv_done, 1)
            v.tensor_scalar(var[:], var[:], 1.0 / D, None, ALU.mult).then_inc(mv_done, 1)
            dve.wait_ge(mv_done, 6)
            v.scalar_tensor_tensor(var[:], mdif[:], 0.25, var[:], ALU.mult, ALU.add).then_inc(mv_done, 1)
            dve.wait_ge(std_done, 1)
            v.reciprocal(rstd[:], std[:]).then_inc(rstd_done, 1)
            dve.wait_ge(rstd_done, 1)

            def normalise(j, n, first):
                i = n * 4 + j
                if not first:
                    dve.wait_ge(xn_turned, i - 3)
                    dve.wait_ge(xn_out[j], 16 * n)
                v.tensor_scalar(xn_st[:, j, :], x_all[:, i, :], mean[:, bass.ds(i, 1)], rstd[:, bass.ds(i, 1)],
                                ALU.subtract, ALU.mult).then_inc(xn_staged, 1)

            for j in range(4):
                normalise(j, 0, True)
            with dve.Fori(1, NB // 4) as g:
                for j in range(4):
                    normalise(j, g, False)
            dve.wait_ge(xT_kept, NB)
            dve.wait_ge(x_biased, NB)
            dve.wait_ge(consts, 1)
            dve.wait_ge(w_in, W_ALL)

            def bcast(ap, n, at):
                return ap.unsqueeze(at).broadcast_to([*ap.shape[:at], n, *ap.shape[at:]])

            n_route = 0

            def then(ins):
                nonlocal n_route
                n_route += 1
                ins.then_inc(route_steps, 1)
                dve.wait_ge(route_steps, n_route)

            dve.wait_ge(ex_ready, NB)
            tt, ts = v.tensor_tensor, v.tensor_scalar
            sml = lambda n: small[:, n, :]
            then(ts(sc_t, ex, 1.0, None, ALU.add))
            then(v.reciprocal(scores_t, sc_t))
            then(tt(sc_t, scores_t, bcast(gbias[:], NB, 1), ALU.add))
            high = sc_t.rearrange("p t (g e) -> p (t g) e", g=G)
            low = None
            n_in, bufs = EPG, [ra_t, rb_t, rc_t]
            level = 0
            while n_in > 1:
                n_in //= 2
                size = NB * G * n_in
                flat = bufs[level].rearrange("p t e -> p (t e)")
                part = lambda m: flat[:, m * size:(m + 1) * size].rearrange("p (g e) -> p g e", e=n_in)
                a, b = high[:, :, 0:n_in], high[:, :, n_in:2 * n_in]
                new_high, new_low = part(0), part(1)
                then(tt(new_high, a, b, ALU.max))
                then(tt(new_low, a, b, ALU.min))
                if low is not None:
                    then(tt(part(2), low[:, :, 0:n_in], low[:, :, n_in:2 * n_in], ALU.max))
                    then(tt(part(3), new_low, part(2), ALU.max))
                    new_low = part(3)
                high, low = new_high, new_low
                level += 1
            group = sml(0).rearrange("p (t g) -> p t g", g=G)
            then(tt(sml(0), high.rearrange("p g e -> p (g e)"), low.rearrange("p g e -> p (g e)"), ALU.add))
            other, own = bcast(group, G, 2), bcast(group, G, 3)
            gt, ge = (x.rearrange("p t (g h) -> p t g h", g=G) for x in (ra_t, rb_t))
            then(tt(gt, other, own, ALU.is_gt))
            then(tt(ge, other, own, ALU.is_ge))
            then(tt(rb_t, rb_t, bcast(lower[:].rearrange("p g h -> p (g h)"), NB, 1), ALU.mult))
            then(tt(ra_t, ra_t, rb_t, ALU.max))
            then(v.tensor_reduce(sml(1), ra_t.rearrange("p t (g h) -> p (t g) h", g=G), AX_X, ALU.add))
            then(ts(sml(2), sml(1), TG - 0.5, None, ALU.is_lt))
            then(ts(sml(3), sml(2), FILL, FILL, ALU.mult, ALU.subtract))
            by_group = lambda x: x.rearrange("p t (g e) -> p (t g) e", g=G)
            then(tt(by_group(ra_t), by_group(sc_t), bcast(sml(2), EPG, 2), ALU.mult))
            then(tt(by_group(ra_t), by_group(ra_t), bcast(sml(3), EPG, 2), ALU.add))
            for t in range(NB):
                last = v.max(top8[:, t, :], ra_t[:, t, :])
            then(last)
            for t in range(NB):
                last = v.match_replace(rb_t[:, t, :], top8[:, t, :], ra_t[:, t, :], -1.1 * FILL)
            then(last)
            tt(sel_t, ra_t, rb_t, ALU.not_equal).then_inc(sel_ready, 1)
            dve.wait_ge(sel_ready, 1)
            then(tt(sc_t, scores_t, sel_t, ALU.mult))
            then(v.tensor_reduce(wsum[:], sc_t, AX_X, ALU.add))
            then(ts(wsum[:], wsum[:], 1e-20, None, ALU.add))
            then(v.reciprocal(wsum[:], wsum[:]))
            then(ts(wsum[:], wsum[:], SCALE, None, ALU.mult))
            weight_t = scores_t
            then(tt(weight_t, sc_t, bcast(wsum[:], E, 2), ALU.mult))
            dve.wait_ge(ranks_ready, 1)
            flat = lambda x, n: x.rearrange("p t e -> p (t e)")[:, n * 512:(n + 1) * 512]
            for n, bank in enumerate((psS[:, 0, :], psS[:, 1, :], psT[:, 0, :], psT[:, 1, :])):
                v.tensor_copy(flat(sc_t, n), bank)
            for n, bank in enumerate((psQ, psV, psM, psO)):
                last = v.tensor_copy(flat(ra_t, n), bank[:])
            then(last)
            then(tt(sc_t, sc_t, ra_t, ALU.subtract))
            src, dst, d = ra_t, rb_t, 1
            while d < NB:
                v.tensor_copy(dst[:, 0:d, :], src[:, 0:d, :])
                then(tt(dst[:, d:, :], src[:, d:, :], src[:, 0:NB - d, :], ALU.add))
                src, dst, d = dst, (rc_t if dst is rb_t else rb_t), 2 * d
            upto = src
            n_e, base, e_a, e_b, e_c = (per_e[:, n, :] for n in range(5))
            then(ts(e_a, upto[:, NB - 1, :], float(P - 1), None, ALU.add))
            then(v.tensor_copy(count_i[:], e_a))
            then(ts(count_i[:], count_i[:], 7, None, ALU.arith_shift_right))
            then(v.tensor_copy(n_e, count_i[:]))
            then(v.tensor_copy(e_a, n_e))
            src, dst, d = e_a, e_b, 1
            while d < E:
                v.tensor_copy(dst[:, 0:d], src[:, 0:d])
                then(tt(dst[:, d:], src[:, d:], src[:, 0:E - d], ALU.add))
                src, dst, d = dst, (e_c if dst is e_b else e_b), 2 * d
            ends = src
            then(tt(base, ends, n_e, ALU.subtract))
            then(ts(base, base, float(P), 1.0, ALU.mult, ALU.add))
            then(ts(ends_row[:], ends[0:1, :], 3.0, None, ALU.add))
            then(ts(ends_row[:], ends_row[:], 1, None, ALU.arith_shift_right))
            then(tt(tile_cmp[:], bcast(ends, QT, 1), bcast(tile_no[:], E, 2), ALU.is_le))
            then(v.tensor_reduce(tile_e[:], tile_cmp[:], AX_X, ALU.add))
            ts(tile_ei[:], tile_e[:], float(E - 1), None, ALU.min).then_inc(tiles_ready, 1)
            then(tt(sc_t, sc_t, upto, ALU.add))
            then(tt(sc_t, sc_t, bcast(base, NB, 1), ALU.add))
            then(tt(sc_t, sc_t, sel_t, ALU.mult))
            for t in range(NB):
                last = v.max(slot8[:, t, :], sc_t[:, t, :])
            then(last)
            ts(slot_idx[:], slot8[:], 1.0, None, ALU.subtract).then_inc(slots_ready, 1)
            for t in range(NB):
                for k in range(K):
                    last = v.scalar_tensor_tensor(rb_t[:, (t % 4) * K + k, :], sc_t[:, t, :], slot8[:, t, k:k + 1], weight_t[:, t, :],
                                                  ALU.is_equal, ALU.mult, accum_out=w8[:, t, k:k + 1])
                if t % 4 == 3 and t < NB - 1:
                    then(last)
            last.then_inc(routed, 1)

            def stage(j, i, blk, nth):
                if nth:
                    dve.wait_ge(lat_kv, i)
                if nth > 1:
                    dve.wait_ge(sh_ready, i - 1)
                v.tensor_copy(xTs[:, j, :, :], xT_all[:, i, :, :]).then_inc(xT_staged, 1)
                dve.wait_ge(xT_staged, i + 1)
                src = xTs[:, j, :, :].rearrange("p c (n t) -> p c n t", t=CH)
                v.tensor_reduce(pooledT[:, :, 0, bass.ds(blk * LPB, LPB)], src, AX_X, ALU.add).then_inc(pool_sums, 1)
                dve.wait_ge(pool_sums, i + 1)
                v.tensor_copy(pooledT[:, :, 1, :], pooledT[:, :, 0, :]).then_inc(pooled, 1)

            def masks(i, blk, nth):
                if nth:
                    dve.wait_ge(masked, 2 * NPAIR * i)
                v.tensor_scalar(mask[:, 0, :], mask_prev[:], no_past[:, bass.ds(blk, 1)], None, ALU.add).then_inc(masks_staged, 1)
                v.tensor_copy(lat_mask[:], lat_wide[:, bass.ds((BPS - 1 - blk) * LPB, NLAT)]).then_inc(masks_staged, 1)
                dve.wait_ge(masks_staged, 2 * i + 2)

            MIX = 8

            def mix_gate(j, i):
                n = 0

                def step(ins, wait=True):
                    nonlocal n
                    n += 1
                    ins.then_inc(mix_steps, 1)
                    if wait:
                        dve.wait_ge(mix_steps, i * MIX + n)

                dve.wait_ge(probs, 2 * NPAIR * (i + 1))
                step(v.tensor_scalar(den1[:], den[:, j, :], TINY, None, ALU.max))
                step(v.reciprocal(rec[:], den1[:]))
                dve.wait_ge(o_turned, i + 1)
                v.tensor_tensor(local[:], psV[:, 0:D].rearrange("p (h d) -> p h d", h=H), bcast(rec[:], HD, 2),
                                ALU.mult).then_inc(local_kept, 1)
                dve.wait_ge(local_kept, i + 1)
                dve.wait_ge(remote_kept, i + 1)
                step(v.tensor_tensor(zl[:], local[:], bcast(gl[:], H, 1), ALU.mult), wait=False)
                step(v.tensor_tensor(zr[:], remote[:], bcast(gr[:], H, 1), ALU.mult))
                step(v.tensor_tensor(zs[:], zl[:], zr[:], ALU.add))
                v.tensor_reduce(z[:], zs[:], AX_X, ALU.add).then_inc(z_ready, 1)
                step(v.tensor_tensor(dif[:], local[:], remote[:], ALU.subtract), wait=False)

            def mix(i):
                dve.wait_ge(ez_ready, i + 1)
                v.tensor_scalar(ez1[:], ez[:], 1.0, None, ALU.add).then_inc(mix_steps, 1)
                dve.wait_ge(mix_steps, i * MIX + 7)
                v.reciprocal(gate[:], ez1[:]).then_inc(mix_steps, 1)
                dve.wait_ge(mix_steps, i * MIX + 8)
                v.tensor_tensor(gdif[:], dif[:], bcast(gate[:], HD, 2), ALU.mult).then_inc(gdif_ready, 1)
                dve.wait_ge(gdif_ready, i + 1)
                v.tensor_tensor(mixed[:], gdif[:], remote[:], ALU.add).then_inc(mixed_ready, 1)

            def keep_q(j, i, nth):
                dve.wait_ge(k_kept, DC * i + 1)
                if nth > 1:
                    dve.wait_ge(s_ready, NPAIR * (i - 1))
                for c in range(DC):
                    last = v.scalar_tensor_tensor(qz[:, j, c, :, :], bcast(psQ[:, c * P:(c + 1) * P], 2, 1), bqk[:, c:c + 1],
                                                  bcast(head_parity[:], P, 2), ALU.add, ALU.mult)
                last.then_inc(q_kept, 1)

            def keep_v(j, i, c, nth):
                dve.wait_ge(v_ready, i + 1)
                if nth:
                    dve.wait_ge(pv_pair, NPAIR * (i - 1) + PPC * (c + 1))
                pairs = lambda x: x.rearrange("p (n a d) -> p n a d", a=2, d=HD)[:, c * PPC:(c + 1) * PPC]
                for par in range(2):
                    last = v.tensor_tensor(vz[:, j].rearrange("p (n a) d -> p n a d", a=2)[:, c * PPC:(c + 1) * PPC, par, par * HD:(par + 1) * HD],
                                           pairs(psV[:, 0:D])[:, :, par, :], pairs(bv[:])[:, :, par, :], ALU.add)
                last.then_inc(v_kept, 1)

            def keep_rq(i, nth):
                if nth:
                    dve.wait_ge(lat_s, i)
                v.scalar_tensor_tensor(rqz[:], bcast(psV[0:LD, D:D + P], LH, 1), brq[:], bcast(rq_head[:], P, 2),
                                       ALU.add, ALU.mult).then_inc(rq_kept, 1)

            def keep_rkv(i):
                dve.wait_ge(lat_kv, i + 1)
                v.tensor_scalar(rkT[:], psM[0:LD, 0:NLAT], 1.0 / CH, brk[:], ALU.mult, ALU.add).then_inc(rk_kept, 1)
                for par in range(2):
                    r = slice(par * NLAT, (par + 1) * NLAT)
                    v.scalar_tensor_tensor(rv[r, par::2, 0:LHD],
                                           psM[r, NLAT:NLAT + LD].rearrange("p (h d) -> p h d", h=LH)[:, par::2, :], 1.0 / CH,
                                           brv[r, :].rearrange("p (h d) -> p h d", h=LH)[:, par::2, :],
                                           ALU.mult, ALU.add).then_inc(rk_kept, 1)

            def latent_max(i):
                dve.wait_ge(lat_s, i + 1)
                v.tensor_tensor(lsm[:], psM[:, 0:LH * NLAT].rearrange("p (h n) -> p h n", h=LH), bcast(lat_mask[:], LH, 1),
                                ALU.add).then_inc(lat_steps, 1)
                dve.wait_ge(lat_steps, 4 * i + 1)
                v.tensor_reduce(lmax[:], lsm[:], AX_X, ALU.max).then_inc(lat_steps, 1)
                dve.wait_ge(lat_steps, 4 * i + 2)
                v.scalar_tensor_tensor(lneg[:], bcast(lmax[:], NLAT, 2), FLOOR, lsm[:], ALU.max, ALU.subtract).then_inc(lat_neg, 1)

            def latent_out(i):
                dve.wait_ge(lat_o, i + 1)
                lo = psM[:, 0:LH * (LHD + 1)].rearrange("p (h d) -> p h d", h=LH)
                v.tensor_scalar(lden[:], lo[:, :, LHD], TINY, None, ALU.max).then_inc(lat_steps, 1)
                dve.wait_ge(lat_steps, 4 * i + 3)
                v.reciprocal(lrec[:], lden[:]).then_inc(lat_steps, 1)
                dve.wait_ge(lat_steps, 4 * i + 4)
                v.tensor_tensor(lat[:, 0:LD].rearrange("p (h d) -> p h d", h=LH), lo[:, :, 0:LHD], bcast(lrec[:], LHD, 2),
                                ALU.mult).then_inc(lat_kept, 1)

            def keep_remote(i, nth):
                dve.wait_ge(remote_ready, i + 1)
                if nth:
                    dve.wait_ge(mixed_ready, i)
                v.tensor_tensor(remote[:].rearrange("p h d -> p (h d)"), psM[:, D:2 * D], brout[:], ALU.add).then_inc(remote_kept, 1)

            def keep_shared(j, i):
                dve.wait_ge(eg_ready, i + 1)
                v.tensor_scalar(eg1[:], eg[:], 1.0, None, ALU.add).then_inc(sh_steps, 1)
                dve.wait_ge(sh_steps, 3 * i + 1)
                v.reciprocal(sig[:], eg1[:]).then_inc(sh_steps, 1)
                dve.wait_ge(sh_steps, 3 * i + 2)
                v.tensor_tensor(gs[:], psQ[:, 0:P], sig[:], ALU.mult).then_inc(sh_steps, 1)
                dve.wait_ge(sh_steps, 3 * i + 3)
                v.tensor_tensor(hsT[:, j, :], psQ[:, P:2 * P], gs[:], ALU.mult).then_inc(hs_ready, 1)

            def accumulate(i):
                dve.wait_ge(out_ready, i + 1)
                v.tensor_tensor(x_all[:, i, :], psV[:, D:2 * D], x_all[:, i, :], ALU.add).then_inc(acc_done, 1)

            def mask_pair(i, p, nth):
                n = i * NPAIR + p
                dve.wait_ge(s_ready, n + 1)
                if p >= 4 or nth:
                    dve.wait_ge(probs, 2 * (n - 3))
                v.memset(met[:, p % 4:p % 4 + 1], 0.0)
                for par in range(2):
                    v.tensor_tensor_reduce(sm[:, p % 4, par, :], psS[:, p % 2, par * 2 * P:(par + 1) * 2 * P],
                                           mask[:].rearrange("p a t -> p (a t)"), -1.0, -FLOOR, ALU.add, ALU.min,
                                           nmax[:, p % 4, par:par + 1]).then_inc(masked, 1)

            def body(j, i, blk, nth, live=True, tail=True, ahead=True, last_tail=True, next_blk=None, between=lambda s: None):
                if live:
                    masks(i, blk, nth)
                for s in range(NPAIR):
                    if live:
                        mask_pair(i, s, nth)
                    if s == 0 and tail and last_tail:
                        accumulate(i - 2)
                    if s == 0 and live:
                        keep_v(j, i, 0, nth)
                        keep_rq(i, nth)
                    if s == 2 and tail:
                        keep_remote(i - 1, nth - 1)
                    if s == 3 and live:
                        keep_v(j, i, 1, nth)
                        keep_rkv(i)
                        if ahead:
                            stage(1 - j, i + 1, next_blk, 2 if nth else 1)
                    if s == 4 and live:
                        keep_shared(j, i)
                    if s == 4 and tail:
                        mix_gate(1 - j, i - 1)
                    if s == 5 and live:
                        latent_max(i)
                    if s == 6 and tail:
                        mix(i - 1)
                    if s == 6 and live and ahead:
                        keep_q(1 - j, i + 1, 2 if nth else 1)
                    if s == 7 and live:
                        latent_out(i)
                    between(s)

            def combine(j, i, n):
                dve.wait_ge(rows_ready[j], 16 * K * (n + 1))
                dve.wait_ge(acc_done, 1)
                for k in range(K):
                    ins = v.scalar_tensor_tensor(x_all[:, i, :], rows_in[:, j, k, :], w8[:, i, k:k + 1], x_all[:, i, :],
                                                 ALU.mult, ALU.add)
                    if k < K - 1:
                        ins.then_inc(combine_steps, 1)
                        dve.wait_ge(combine_steps, (K - 1) * i + k + 1)
                    else:
                        ins.then_inc(combined, 1)

            def attention(start, combining):
                def step(j, i, blk, nth, **kw):
                    def between(s):
                        if combining and s in (1, 5):
                            n = s // 4
                            combine(n, 2 * (i - start) + n, i - start)

                    body(j, i, blk, nth, between=between, **kw)

                nth = min(start, 2)
                stage(0, start, 0, nth)
                keep_q(0, start, nth)
                step(0, start, 0, nth, tail=False, next_blk=1)
                step(1, start + 1, 1, max(nth, 1), last_tail=False, next_blk=2)
                with dve.Fori(start // 2 + 1, (start + HALF) // 2 - 1) as g:
                    first = (g % (BPS // 2)) * 2
                    step(0, g * 2, first, 2, next_blk=first + 1)
                    step(1, g * 2 + 1, first + 1, 2, next_blk=((g + 1) % (BPS // 2)) * 2)
                step(0, start + HALF - 2, BPS - 2, 2, next_blk=BPS - 1)
                step(1, start + HALF - 1, BPS - 1, 2, ahead=False)
                body(0, start + HALF, None, 2, live=False)
                accumulate(start + HALF - 1)

            def make_h(j, u, first):
                dve.wait_ge(silu_ready, u + 1)
                if not first:
                    dve.wait_ge(h_turned, u - 1)
                v.tensor_tensor(hh[:, j % 2, :, :], psS[:, j % 2, :].rearrange("p (a n) -> p a n", a=2)[:, :, F:2 * F],
                                sg[:, j % 2, :, :], ALU.mult).then_inc(h_ready, 1)

            def keep_hT(j, u, first):
                dve.wait_ge(h_turned, u + 1)
                if not first:
                    dve.wait_ge(pairs_done, u)
                v.tensor_copy(hhT[:, j % 2, :, :].rearrange("p a t -> p (a t)"), (psQ, psV)[j % 2][:, 0:2 * P]).then_inc(hT_ready, 1)

            def keep_y(j, u, turn, first):
                dve.wait_ge(pairs_done, u + 2)
                if not first:
                    dve.wait_ge(y_out[j % YS], 16 * turn)
                v.tensor_copy(ys[:, j % YS, :, :].rearrange("p a d -> p (a d)"), (psM, psO)[j % 2][:]).then_inc(y_kept, 1)

            def step(j, g, nth):
                u = g * XS + j
                make_h(j, u, nth < 2)
                if nth > 0:
                    keep_y((j - 1) % XS, u - 1, 2 * g + (j + 1) // YS - 1, nth <= 2)
                keep_hT(j, u, nth < 2)

            def experts():
                dve.wait_ge(experts_known, 16 * QT)
                by_pair = expert_row[:].rearrange("p (u a) -> p u a", a=2)
                v.scalar_tensor_tensor(pair_row[:], by_pair[:, :, 1], float(E), by_pair[:, :, 0], ALU.mult, ALU.add).then_inc(words_ready, 1)
                for j in range(XS):
                    step(j, 0, j)
                with dve.Fori(1, PAIRS // XS) as g:
                    for j in range(XS):
                        step(j, g, MANY)
                keep_y(XS - 1, PAIRS - 1, PAIRS // YS - 1, False)

            attention(0, False)
            dve.wait_ge(probs, 2 * HALF * NPAIR)
            dve.wait_ge(pv_pair, HALF * NPAIR)
            experts()
            for j in range(YS):
                dve.wait_ge(y_out[j], 16 * (PAIRS // YS))
            dve.wait_ge(gu_ready, PAIRS)
            attention(HALF, True)


_INS = ['L0_attn_x', 'L0_attn_qkv_w', 'L0_attn_qkv_b', 'L0_attn_rq_w', 'L0_attn_rq_b', 'L0_attn_rkv_w', 'L0_attn_rkv_b',
        'L0_attn_rout_w', 'L0_attn_rout_b', 'L0_attn_out_w', 'L0_attn_out_b', 'L0_attn_gl_w', 'L0_attn_gr_w',
        'L0_ffn_gate_w', 'L0_ffn_gate_bias', 'L0_ffn_We_gate', 'L0_ffn_We_up', 'L0_ffn_We_down',
        'L0_ffn_Ws_gate', 'L0_ffn_Ws_up', 'L0_ffn_Ws_down']


def kernel(**inputs):
    import numpy as np
    import concourse.bacc as bacc
    from concourse.bass_utils import run_bass_kernel_spmd

    nc = bacc.Bacc("TRN2", target_bir_lowering=False, num_devices=1)
    arrays, aps = {}, {}
    for name in _INS:
        arrays[f"in_{name}"] = np.ascontiguousarray(inputs[name])
        aps[name] = nc.dram_tensor(f"in_{name}", arrays[f"in_{name}"].shape, F32, kind="ExternalInput").ap()
    out = nc.dram_tensor("out", (B, S, D), F32, kind="ExternalOutput").ap()
    build(nc, aps, out)
    r = run_bass_kernel_spmd(nc, [arrays], core_ids=[0])
    return r.results[0]["out"]
```
